# Optimizing a Trainium2 kernel written in Bass

```python
import numpy as np
import jax
import jax.numpy as jnp

def _softmax(x, axis=-1):
    return jax.nn.softmax(x, axis=axis)

def _gelu(x):
    return jax.nn.gelu(x, approximate=True)

def _silu(x):
    return jax.nn.silu(x)

def _sigmoid(x):
    return jax.nn.sigmoid(x)

def _layernorm(x, axis=-1, eps=1e-05):
    m = jnp.mean(x, axis=axis, keepdims=True)
    v = jnp.var(x, axis=axis, keepdims=True)
    return (x - m) / jnp.sqrt(v + eps)

def _scatter_add(tgt, idx, src, axis=0):
    return tgt.at[idx].add(src)

def _segment_sum(src, seg, n):
    return jax.ops.segment_sum(src, seg, n)
kernel_name = 'mk_gnn_ffn_d1_gnn_r32_573771'

def setup_inputs(seed: int=0):
    np.random.seed(seed)
    _w = jnp.asarray

    def _rec_inputs():
        import jax
        import jax.numpy as jnp
        _gk = jax.random.key(seed)
        x = -8.776e-05 + 1 * jax.random.normal(jax.random.fold_in(_gk, 1), (10000, 512), jnp.float32)
        src = jax.random.randint(jax.random.fold_in(_gk, 2), (10000,), 0, 10000, jnp.int32)
        dst = jnp.minimum((10000 * jax.random.uniform(jax.random.fold_in(_gk, 3), (10000,)) ** 2.0).astype(jnp.int32), 9999)
        _o = jnp.argsort(dst, stable=True)
        src = src[_o]
        dst = dst[_o]
        return (x, src, dst)
    x, src, dst = _rec_inputs()

    def _L0_gnn_setup():
        import jax, jax.numpy as jnp
        import numpy as np
        N = 10000
        DIM = 512
        H = 8
        C = DIM // H
        E = 5000
        NEG_SLOPE = 0.2
        BN_EPS = 1e-05
        key = jax.random.key(seed)
        ks = jax.random.split(key, 8)
        x = jax.random.normal(ks[0], (N, DIM), dtype=jnp.float32)
        edge_index = jax.random.randint(ks[1], (2, E), 0, N, dtype=jnp.int32)
        s = 1.0 / np.sqrt(DIM)
        W_gat = jax.random.normal(ks[2], (DIM, DIM), dtype=jnp.float32) * s
        att_src = jax.random.normal(ks[3], (H, C), dtype=jnp.float32) * s
        att_dst = jax.random.normal(ks[4], (H, C), dtype=jnp.float32) * s
        gat_bias = jnp.zeros((DIM,), dtype=jnp.float32)
        bn_gamma = jnp.ones((DIM,), dtype=jnp.float32)
        bn_beta = jnp.zeros((DIM,), dtype=jnp.float32)
        W_skip = jax.random.normal(ks[5], (DIM, DIM), dtype=jnp.float32) * s
        b_skip = jnp.zeros((DIM,), dtype=jnp.float32)
        return {'x': x, 'edge_index': edge_index, 'W_gat': W_gat, 'att_src': att_src, 'att_dst': att_dst, 'gat_bias': gat_bias, 'bn_gamma': bn_gamma, 'bn_beta': bn_beta, 'W_skip': W_skip, 'b_skip': b_skip}
    _L0_gnn_all = _L0_gnn_setup()
    _L0_gnn_in = {k: v for k, v in _L0_gnn_all.items() if k in ('W_gat', 'att_src', 'att_dst', 'gat_bias', 'bn_gamma', 'bn_beta', 'W_skip', 'b_skip')}
    del _L0_gnn_all

    def _L0_ffn_setup():
        import jax, jax.numpy as jnp
        import numpy as np
        E, TOPK, H, DK, DV, D = (4, 2, 8, 64, 64, 512)
        B, L = (4, 1024)
        VDIM = H * DV

        def _silu(x):
            return x * jax.nn.sigmoid(x)

        def _l2norm(x):
            return x * jax.lax.rsqrt(jnp.sum(x * x, axis=-1, keepdims=True) + 1e-06)

        def _forward(h, Wq, Wgate, Wk, Wv, Wb, Wa, A_log, dt_bias, Wg, o_norm_weight, Wo):
            Bs, Ls, _ = h.shape
            scores = jax.nn.softmax((h @ Wgate).astype(jnp.float32), axis=-1)
            rw, sel = jax.lax.top_k(scores, TOPK)
            rw = rw / jnp.sum(rw, axis=-1, keepdims=True)
            bi = jnp.arange(Bs)[:, None, None]
            li = jnp.arange(Ls)[None, :, None]
            w_full = jnp.zeros((Bs, Ls, E), jnp.float32).at[bi, li, sel].set(rw)
            m = jnp.transpose(w_full > 0, (2, 0, 1))
            q = _l2norm(_silu(h @ Wq).reshape(Bs, Ls, H, DK))
            k = _l2norm(_silu(h @ Wk).reshape(Bs, Ls, H, DK))
            v = _silu(h @ Wv).reshape(Bs, Ls, H, DV)
            beta = jax.nn.sigmoid(h @ Wb)
            g = -jnp.exp(A_log) * jax.nn.softplus((h @ Wa).astype(jnp.float32) + dt_bias)
            beta_e = beta[None] * m[..., None]
            g_e = jnp.where(m[..., None], g[None], 0.0)
            scale = DK ** (-0.5)
            xs = (jnp.moveaxis(q, 1, 0), jnp.moveaxis(k, 1, 0), jnp.moveaxis(v, 1, 0), jnp.moveaxis(beta_e, 2, 0), jnp.moveaxis(g_e, 2, 0))

            def step(S, x):
                qt, kt, vt, bt, gt = x
                S = S * jnp.exp(gt)[..., None, None]
                kv = jnp.einsum('bhk,ebhkv->ebhv', kt, S)
                delta = (vt[None] - kv) * bt[..., None]
                S = S + kt[None, :, :, :, None] * delta[..., None, :]
                ot = jnp.einsum('bhk,ebhkv->ebhv', qt * scale, S)
                return (S, ot)
            S0 = jnp.zeros((E, Bs, H, DK, DV), jnp.float32)
            _, o = jax.lax.scan(step, S0, xs)
            o = jnp.moveaxis(o, 0, 2)
            core = jnp.einsum('ble,eblhv->blhv', w_full, o)
            gate = _silu((h @ Wg).reshape(Bs, Ls, H, DV))
            core = core * jax.lax.rsqrt(jnp.mean(core * core, axis=-1, keepdims=True) + 1e-05)
            core = core * o_norm_weight * gate
            return core.reshape(Bs, Ls, VDIM) @ Wo
        key = jax.random.key(seed)
        ks = jax.random.split(key, 12)
        std = 0.02
        h = jax.random.normal(ks[0], (B, L, D), jnp.float32)
        Wq = jax.random.normal(ks[1], (D, H * DK), jnp.float32) * std
        Wgate = jax.random.normal(ks[2], (D, E), jnp.float32) * std
        Wk = jax.random.normal(ks[3], (D, H * DK), jnp.float32) * std
        Wv = jax.random.normal(ks[4], (D, VDIM), jnp.float32) * std
        Wb = jax.random.normal(ks[5], (D, H), jnp.float32) * std
        Wa = jax.random.normal(ks[6], (D, H), jnp.float32) * std
        Wg = jax.random.normal(ks[7], (D, VDIM), jnp.float32) * std
        Wo = jax.random.normal(ks[8], (VDIM, D), jnp.float32) * std
        A = jax.random.uniform(ks[9], (H,), jnp.float32, 0.0001, 16.0)
        A_log = jnp.log(A)
        dt = jnp.exp(jax.random.uniform(ks[10], (H,), jnp.float32) * (np.float32(np.log(0.1)) - np.float32(np.log(0.001))) + np.float32(np.log(0.001)))
        dt = jnp.maximum(dt, 0.0001)
        dt_bias = dt + jnp.log(-jnp.expm1(-dt))
        o_norm_weight = jnp.ones((DV,), jnp.float32)
        return {'hidden_states': h, 'Wq': Wq, 'Wgate': Wgate, 'Wk': Wk, 'Wv': Wv, 'Wb': Wb, 'Wa': Wa, 'A_log': A_log, 'dt_bias': dt_bias, 'Wg': Wg, 'o_norm_weight': o_norm_weight, 'Wo': Wo}
    _L0_ffn_all = _L0_ffn_setup()
    _L0_ffn_in = {k: v for k, v in _L0_ffn_all.items() if k in ('Wq', 'Wgate', 'Wk', 'Wv', 'Wb', 'Wa', 'A_log', 'dt_bias', 'Wg', 'o_norm_weight', 'Wo')}
    del _L0_ffn_all
    return {'x': x, 'src': src, 'dst': dst, 'L0_gnn_W_gat': _L0_gnn_in['W_gat'], 'L0_gnn_att_src': _L0_gnn_in['att_src'], 'L0_gnn_att_dst': _L0_gnn_in['att_dst'], 'L0_gnn_gat_bias': _L0_gnn_in['gat_bias'], 'L0_gnn_bn_gamma': _L0_gnn_in['bn_gamma'], 'L0_gnn_bn_beta': _L0_gnn_in['bn_beta'], 'L0_gnn_W_skip': _L0_gnn_in['W_skip'], 'L0_gnn_b_skip': _L0_gnn_in['b_skip'], 'L0_ffn_Wq': _L0_ffn_in['Wq'], 'L0_ffn_Wgate': _L0_ffn_in['Wgate'], 'L0_ffn_Wk': _L0_ffn_in['Wk'], 'L0_ffn_Wv': _L0_ffn_in['Wv'], 'L0_ffn_Wb': _L0_ffn_in['Wb'], 'L0_ffn_Wa': _L0_ffn_in['Wa'], 'L0_ffn_A_log': _L0_ffn_in['A_log'], 'L0_ffn_dt_bias': _L0_ffn_in['dt_bias'], 'L0_ffn_Wg': _L0_ffn_in['Wg'], 'L0_ffn_o_norm_weight': _L0_ffn_in['o_norm_weight'], 'L0_ffn_Wo': _L0_ffn_in['Wo']}

def reference(x, src, dst, L0_gnn_W_gat, L0_gnn_att_src, L0_gnn_att_dst, L0_gnn_gat_bias, L0_gnn_bn_gamma, L0_gnn_bn_beta, L0_gnn_W_skip, L0_gnn_b_skip, L0_ffn_Wq, L0_ffn_Wgate, L0_ffn_Wk, L0_ffn_Wv, L0_ffn_Wb, L0_ffn_Wa, L0_ffn_A_log, L0_ffn_dt_bias, L0_ffn_Wg, L0_ffn_o_norm_weight, L0_ffn_Wo):
    import jax
    import jax.numpy as jnp

    def _L0_gnn_ref(x, edge_index, W_gat, att_src, att_dst, gat_bias, bn_gamma, bn_beta, W_skip, b_skip):
        import jax, jax.numpy as jnp
        import numpy as np
        N = 10000
        DIM = 512
        H = 8
        C = DIM // H
        E = 5000
        NEG_SLOPE = 0.2
        BN_EPS = 1e-05
        identity = x @ W_skip + b_skip
        loops = jnp.arange(N, dtype=edge_index.dtype)
        src = jnp.concatenate([edge_index[0], loops])
        dst = jnp.concatenate([edge_index[1], loops])
        h = (x @ W_gat).reshape(N, H, C)
        a_src = jnp.einsum('nhc,hc->nh', h, att_src)
        a_dst = jnp.einsum('nhc,hc->nh', h, att_dst)
        e = a_src[src] + a_dst[dst]
        e = jnp.where(e >= 0, e, NEG_SLOPE * e)
        m = jax.ops.segment_max(e, dst, num_segments=N)
        ex = jnp.exp(e - m[dst])
        denom = jax.ops.segment_sum(ex, dst, num_segments=N)
        alpha = ex / denom[dst]
        msgs = alpha[:, :, None] * h[src]
        out = jax.ops.segment_sum(msgs, dst, num_segments=N)
        out = out.reshape(N, DIM) + gat_bias
        mean = out.mean(axis=0)
        var = out.var(axis=0)
        out = (out - mean) * jax.lax.rsqrt(var + BN_EPS) * bn_gamma + bn_beta
        out = jax.nn.gelu(out, approximate=False)
        return out + identity

    def _L0_ffn_ref(hidden_states, Wq, Wgate, Wk, Wv, Wb, Wa, A_log, dt_bias, Wg, o_norm_weight, Wo):
        import jax, jax.numpy as jnp
        import numpy as np
        E, TOPK, H, DK, DV, D = (4, 2, 8, 64, 64, 512)
        B, L = (4, 1024)
        VDIM = H * DV

        def _silu(x):
            return x * jax.nn.sigmoid(x)

        def _l2norm(x):
            return x * jax.lax.rsqrt(jnp.sum(x * x, axis=-1, keepdims=True) + 1e-06)

        def _forward(h, Wq, Wgate, Wk, Wv, Wb, Wa, A_log, dt_bias, Wg, o_norm_weight, Wo):
            Bs, Ls, _ = h.shape
            scores = jax.nn.softmax((h @ Wgate).astype(jnp.float32), axis=-1)
            rw, sel = jax.lax.top_k(scores, TOPK)
            rw = rw / jnp.sum(rw, axis=-1, keepdims=True)
            bi = jnp.arange(Bs)[:, None, None]
            li = jnp.arange(Ls)[None, :, None]
            w_full = jnp.zeros((Bs, Ls, E), jnp.float32).at[bi, li, sel].set(rw)
            m = jnp.transpose(w_full > 0, (2, 0, 1))
            q = _l2norm(_silu(h @ Wq).reshape(Bs, Ls, H, DK))
            k = _l2norm(_silu(h @ Wk).reshape(Bs, Ls, H, DK))
            v = _silu(h @ Wv).reshape(Bs, Ls, H, DV)
            beta = jax.nn.sigmoid(h @ Wb)
            g = -jnp.exp(A_log) * jax.nn.softplus((h @ Wa).astype(jnp.float32) + dt_bias)
            beta_e = beta[None] * m[..., None]
            g_e = jnp.where(m[..., None], g[None], 0.0)
            scale = DK ** (-0.5)
            xs = (jnp.moveaxis(q, 1, 0), jnp.moveaxis(k, 1, 0), jnp.moveaxis(v, 1, 0), jnp.moveaxis(beta_e, 2, 0), jnp.moveaxis(g_e, 2, 0))

            def step(S, x):
                qt, kt, vt, bt, gt = x
                S = S * jnp.exp(gt)[..., None, None]
                kv = jnp.einsum('bhk,ebhkv->ebhv', kt, S)
                delta = (vt[None] - kv) * bt[..., None]
                S = S + kt[None, :, :, :, None] * delta[..., None, :]
                ot = jnp.einsum('bhk,ebhkv->ebhv', qt * scale, S)
                return (S, ot)
            S0 = jnp.zeros((E, Bs, H, DK, DV), jnp.float32)
            _, o = jax.lax.scan(step, S0, xs)
            o = jnp.moveaxis(o, 0, 2)
            core = jnp.einsum('ble,eblhv->blhv', w_full, o)
            gate = _silu((h @ Wg).reshape(Bs, Ls, H, DV))
            core = core * jax.lax.rsqrt(jnp.mean(core * core, axis=-1, keepdims=True) + 1e-05)
            core = core * o_norm_weight * gate
            return core.reshape(Bs, Ls, VDIM) @ Wo
        return _forward(hidden_states, Wq, Wgate, Wk, Wv, Wb, Wa, A_log, dt_bias, Wg, o_norm_weight, Wo)
    edge_index = jnp.stack([src, dst])
    x = x + _L0_gnn_ref(_layernorm(x, axis=-1), edge_index, L0_gnn_W_gat, L0_gnn_att_src, L0_gnn_att_dst, L0_gnn_gat_bias, L0_gnn_bn_gamma, L0_gnn_bn_beta, L0_gnn_W_skip, L0_gnn_b_skip)
    x = x + _L0_ffn_ref(_layernorm(x, axis=-1)[None], L0_ffn_Wq, L0_ffn_Wgate, L0_ffn_Wk, L0_ffn_Wv, L0_ffn_Wb, L0_ffn_Wa, L0_ffn_A_log, L0_ffn_dt_bias, L0_ffn_Wg, L0_ffn_o_norm_weight, L0_ffn_Wo)[0]
    return x

_drawn_inputs = setup_inputs


def setup_inputs(seed=0):
    import zlib

    import numpy as np

    out = dict(_drawn_inputs(seed))
    spreads = {'L0_gnn_gat_bias': (0.0, 0.8),
     'L0_gnn_bn_gamma': (1.0, 0.2),
     'L0_gnn_bn_beta': (0.0, 0.1),
     'L0_gnn_b_skip': (0.0, 0.1),
     'L0_ffn_o_norm_weight': (1.0, 0.6)}
    factors = {'L0_gnn_att_dst': 3.532,
     'L0_ffn_Wb': 5.55,
     'L0_ffn_Wa': 8.0,
     'L0_ffn_A_log': 4.071,
     'L0_ffn_dt_bias': 3.174}
    for name, (base, spread) in spreads.items():
        noise = np.random.default_rng([zlib.crc32(name.encode()), seed]).standard_normal(out[name].shape)
        drawn = base * np.exp(spread * noise) if base else spread * noise
        out[name] = jnp.asarray(drawn.astype(out[name].dtype))
    for name, factor in factors.items():
        out[name] = (out[name] * factor).astype(out[name].dtype)
    return out
```

```python
import concourse.bass as bass
from concourse import mybir
from contextlib import ExitStack

F32 = mybir.dt.float32
BF16 = mybir.dt.bfloat16
I32 = mybir.dt.int32
ALU = mybir.AluOpType
ACT = mybir.ActivationFunctionType
AX = mybir.AxisListType

N = 10000
DIM = 512
H = 8
C = DIM // H
TP = 125
NT = N // TP
KC = DIM // 128
P = 128
NE = 4
CH = 128
NCH = 2 * N // CH + NE
SLOTS = NCH * CH
NEG_SLOPE = 0.2
BN_EPS = 1e-5
LN_EPS = 1e-5
FAR = 1e30
G_FLOOR = -104.0

ST_DEN, ST_MAX, ST_DST, ST_W = DIM, DIM + H, DIM + 2 * H, DIM + 3 * H
SRC_W = H + DIM
TK_K, TK_V, TK_B, TK_NB, TK_G = DIM, 2 * DIM, 3 * DIM, 3 * DIM + H, 3 * DIM + 2 * H
TK_W = 3 * DIM + 3 * H


class Steps:

    def __init__(self, sem, names, lag=2):
        self.sem, self.names, self.lag, self.written = sem, names.split(), lag, 0
        assert len(set(self.names)) == len(self.names)

    @property
    def credit(self):
        return self.lag * len(self.names)

    def after(self, turn, name):
        k = len(self.names)
        return self.sem, (turn + self.lag) * k + self.names.index(name) + 1

    def done(self, name):
        assert name == self.names[self.written % len(self.names)], name
        self.written += 1
        return self.sem, 1


class Moves:

    def __init__(self, sems, each=1):
        self.sems, self.each = sems, each

    def after(self, pair, buf, back=0):
        return self.sems[buf], (pair + 1 - back) * 16 * self.each

    def done(self, buf):
        return self.sems[buf], 16


class Mem:

    def __init__(self, nc, ctx, tag):
        self.nc, self.ctx, self.tag = nc, ctx, tag

    def sb(self, name, shape, dt=F32):
        return self.ctx.enter_context(self.nc.sbuf_tensor(f"{self.tag}_{name}", shape, dt))

    def ps(self, name, shape=(P, 512), dt=F32):
        return self.ctx.enter_context(self.nc.psum_tensor(f"{self.tag}_{name}", list(shape), dt))

    def sem(self, name):
        return self.ctx.enter_context(self.nc.semaphore(f"{self.tag}_{name}"))

    def steps(self, name, names):
        return Steps(self.sem(name), names)

    def moves(self, name, each=1):
        return Moves([self.sem(f"{name}{b}") for b in range(2)], each)


def give_credit(eng, *counts):
    for c in counts:
        eng.sem_inc(c.sem, c.credit)


def turns(eng, n):
    yield 0
    with eng.Fori(1, n) as i:
        yield i


def held(eng, passed):
    eng.sem_inc(passed, 1)


def heads(ap, n=H):
    return ap.rearrange("p (h c) -> p h c", h=n)


def over_c(ap, c=C):
    return ap.unsqueeze(2).to_broadcast([ap.shape[0], ap.shape[1], c])


def over_h(ap, n):
    return ap.unsqueeze(1).to_broadcast([ap.shape[0], n, ap.shape[1]])


def constants(nc, m):
    k = {
        "ident": m.sb("ident", [P, P]),
        "identb": m.sb("identb", [P, P], BF16),
        "at_or_after": m.sb("at_or_after", [P, P]),
        "before": m.sb("before", [P, P]),
        "after": m.sb("after", [P, P]),
        "hide": m.sb("hide", [P, P], BF16),
        "ones": m.sb("ones", [P, P]),
        "minus_half": m.sb("minus_half", [P, 1]),
        "zeros": m.sb("zeros", [P, ST_W]),
        "merge": m.sb("merge", [P, 7, P]),
        "mergeT": m.sb("mergeT", [P, P]),
        "dump": m.sb("dump", [P, 1]),
        "dumpslot": m.sb("dumpslot", [P, 1]),
        "chunk_no": m.sb("chunk_no", [P, NCH + 2]),
    }
    made = m.sem("constants_made")
    with nc.Block() as block:

        @block.gpsimd
        def _(pool):
            step = [0]

            def then(ins):
                step[0] += 1
                ins.then_inc(made, 1)
                pool.wait_ge(made, step[0])

            for name in ("ident", "at_or_after", "before", "after", "ones"):
                nc.gpsimd.memset(k[name][:], 1.0)
            nc.gpsimd.memset(k["minus_half"][:], -0.5)
            nc.gpsimd.memset(k["hide"][:], 0.0)
            nc.gpsimd.memset(k["merge"][:], 0.0)
            nc.gpsimd.memset(k["mergeT"][:], 0.0)
            then(nc.gpsimd.memset(k["zeros"][:], 0.0))
            row = [[1, P]]
            nc.gpsimd.affine_select(out=k["ident"][:], in_=k["ident"][:], pattern=row, compare_op=ALU.is_equal, fill=0.0, base=0, channel_multiplier=-1)
            nc.gpsimd.affine_select(out=k["at_or_after"][:], in_=k["at_or_after"][:], pattern=row, compare_op=ALU.is_ge, fill=0.0, base=0, channel_multiplier=-1)
            nc.gpsimd.affine_select(out=k["after"][:], in_=k["after"][:], pattern=row, compare_op=ALU.is_gt, fill=0.0, base=0, channel_multiplier=-1)
            nc.gpsimd.affine_select(out=k["hide"][:], in_=k["hide"][:], pattern=row, compare_op=ALU.is_ge, fill=-30000.0, base=0, channel_multiplier=-1)
            nc.gpsimd.iota(k["dump"][:], [[0, 1]], base=N, channel_multiplier=1, allow_small_or_imprecise_dtypes=True)
            nc.gpsimd.iota(k["dumpslot"][:], [[0, 1]], base=SLOTS, channel_multiplier=1, allow_small_or_imprecise_dtypes=True)
            nc.gpsimd.iota(k["chunk_no"][:], [[1, NCH + 2]], base=0, channel_multiplier=0, allow_small_or_imprecise_dtypes=True)
            then(nc.gpsimd.affine_select(out=k["before"][:], in_=k["before"][:], pattern=[[-1, P]], compare_op=ALU.is_gt, fill=0.0, base=0, channel_multiplier=1))
            then(nc.gpsimd.tensor_copy(k["identb"][:], k["ident"][:]))
            for lv in range(7):
                b = 1 << lv
                cols = k["merge"][:, lv, :].rearrange("p (m r) -> p m r", r=2 * b)[:, :, 0:b]
                pairs = P // (2 * b)
                then(nc.gpsimd.memset(cols, 1.0))
                then(nc.gpsimd.affine_select(out=cols, in_=cols, pattern=[[-2 * b, pairs], [0, b]], compare_op=ALU.is_ge, fill=0.0, base=-b, channel_multiplier=1))
                then(nc.gpsimd.affine_select(out=cols, in_=cols, pattern=[[2 * b, pairs], [0, b]], compare_op=ALU.is_ge, fill=0.0, base=2 * b - 1, channel_multiplier=-1))
                then(nc.gpsimd.tensor_tensor(k["merge"][:, lv, :], k["merge"][:, lv, :], k["ident"][:], ALU.add))
            oddcols = k["mergeT"][:].rearrange("p (m r) -> p m r", r=2)[:, :, 1:2]
            then(nc.gpsimd.memset(oddcols, 1.0))
            then(nc.gpsimd.affine_select(out=oddcols, in_=oddcols, pattern=[[2, P // 2], [0, 1]], compare_op=ALU.is_equal, fill=0.0, base=0, channel_multiplier=-1))
            then(nc.gpsimd.tensor_tensor(k["mergeT"][:], k["mergeT"][:], k["ident"][:], ALU.add))
    return k


def project_nodes(nc, k, a, d):
    with ExitStack() as ctx:
        m = Mem(nc, ctx, "nodes")
        w = m.sb("w", [P, 2, KC, DIM])
        att = m.sb("att", [P, 2, DIM])
        bskip = m.sb("bskip", [P, DIM])
        x = m.sb("x", [TP, 2, DIM])
        xn = m.sb("xn", [TP, 2, DIM])
        xT = m.sb("xT", [P, 2, KC, TP])
        row = m.sb("row", [TP, 2, H + ST_W])
        skip = m.sb("skip", [TP, 2, DIM])
        prod = m.sb("prod", [TP, 2, DIM])
        stats = m.sb("stats", [TP, 2, 6])
        mv = m.sb("mv", [TP, 2, 2])
        veps = m.sb("veps", [TP, 2, 1])
        rstd = m.sb("rstd", [TP, 2, 1])
        asum = m.sb("asum", [TP, 2, H])
        p_t = [m.ps(f"p_t{b}") for b in range(2)]
        p_h = [m.ps(f"p_h{b}") for b in range(2)]
        p_s = [m.ps(f"p_s{b}") for b in range(2)]
        weights = m.sem("weights")
        x_in = m.moves("x_in")
        out = m.moves("out", 3)
        unused = m.sem("unused")
        LN = m.steps("norm", "stats aggr xn")
        V = m.steps("vector", "skip psrc pdst asrc adst den sum max")
        G = m.steps("gpsimd", "veps rstd")
        S = m.steps("scalar", "xT h")
        T = m.steps("tensor", "xT h skip")
        passed_dve = m.sem("passed_dve")
        passed_pool = m.sem("passed_pool")
        with nc.Block() as block:

            @block.sync
            def _(sp):
                sp.dma_start(w[:, 0], a["L0_gnn_W_gat"].rearrange("(c p) n -> p c n", p=P)).then_inc(weights, 16)
                sp.dma_start(w[:, 1], a["L0_gnn_W_skip"].rearrange("(c p) n -> p c n", p=P)).then_inc(weights, 16)
                sp.dma_start(att[:, 0], a["L0_gnn_att_src"].rearrange("h c -> (h c)").partition_broadcast(P)).then_inc(weights, 16)
                sp.dma_start(att[:, 1], a["L0_gnn_att_dst"].rearrange("h c -> (h c)").partition_broadcast(P)).then_inc(weights, 16)
                sp.dma_start(bskip[:], a["L0_gnn_b_skip"].partition_broadcast(P)).then_inc(weights, 16)
                with sp.Fori(0, NT // 2) as i:
                    for b in range(2):
                        t = i * 2 + b
                        sp.wait_ge(*LN.after(t - 2, "xn"))
                        sp.dma_start(x[:, b], a["x"][bass.ds(t * TP, TP), :]).then_inc(*x_in.done(b))
                sp.dma_start(d["state"][N:N + P, :], k["zeros"][:]).then_inc(unused, 16)
                sp.wait_ge(unused, 16)

            def norm(t, i, b, dve):
                dve.wait_ge(*x_in.after(i, b))
                nc.vector.bn_stats(stats[:, b], x[:, b]).then_inc(*LN.done("stats"))
                dve.wait_ge(*LN.after(t, "stats"))
                held(dve, passed_dve)
                nc.vector.bn_aggr(mv[:, b], stats[:, b]).then_inc(*LN.done("aggr"))
                dve.wait_ge(*G.after(t, "rstd"))
                dve.wait_ge(*T.after(t - 2, "xT"))
                nc.vector.tensor_scalar(xn[:, b], x[:, b], mv[:, b, 0:1], rstd[:, b], ALU.subtract, ALU.mult).then_inc(*LN.done("xn"))

            def scores(t, i, b, dve):
                dve.wait_ge(*T.after(t, "skip"))
                dve.wait_ge(*out.after(i, b, 1))
                nc.vector.tensor_tensor(skip[:, b], p_s[b][0:TP, :], bskip[0:TP, :], ALU.add).then_inc(*V.done("skip"))
                dve.wait_ge(*S.after(t, "h"))
                nc.vector.tensor_tensor(prod[:, 0], row[:, b, H:H + DIM], att[0:TP, 0], ALU.mult).then_inc(*V.done("psrc"))
                nc.vector.tensor_tensor(prod[:, 1], row[:, b, H:H + DIM], att[0:TP, 1], ALU.mult).then_inc(*V.done("pdst"))
                dve.wait_ge(*V.after(t, "psrc"))
                nc.vector.tensor_reduce(row[:, b, 0:H], heads(prod[:, 0]), AX.X, ALU.add).then_inc(*V.done("asrc"))
                dve.wait_ge(*V.after(t, "pdst"))
                nc.vector.tensor_reduce(row[:, b, H + ST_DST:H + ST_W], heads(prod[:, 1]), AX.X, ALU.add).then_inc(*V.done("adst"))
                nc.vector.memset(row[:, b, H + ST_DEN:H + ST_MAX], 1.0).then_inc(*V.done("den"))
                dve.wait_ge(*V.after(t, "adst"))
                nc.vector.tensor_tensor(asum[:, b], row[:, b, 0:H], row[:, b, H + ST_DST:H + ST_W], ALU.add).then_inc(*V.done("sum"))
                dve.wait_ge(*V.after(t, "sum"))
                nc.vector.scalar_tensor_tensor(row[:, b, H + ST_MAX:H + ST_DST], asum[:, b], NEG_SLOPE, asum[:, b], ALU.mult, ALU.max).then_inc(*V.done("max"))

            @block.vector
            def _(dve):
                give_credit(dve, V, LN)
                dve.wait_ge(weights, 80)
                norm(0, 0, 0, dve)
                for i in turns(dve, NT // 2 - 1):
                    norm(i * 2 + 1, i, 1, dve)
                    scores(i * 2, i, 0, dve)
                    norm(i * 2 + 2, i + 1, 0, dve)
                    scores(i * 2 + 1, i, 1, dve)
                norm(NT - 1, NT // 2 - 1, 1, dve)
                scores(NT - 2, NT // 2 - 1, 0, dve)
                scores(NT - 1, NT // 2 - 1, 1, dve)

            @block.tensor
            def _(pe):
                give_credit(pe, T)
                pe.wait_ge(weights, 80)
                with pe.Fori(0, NT // 2) as i:
                    for b in range(2):
                        t = i * 2 + b
                        pe.wait_ge(*LN.after(t, "xn"))
                        pe.wait_ge(*S.after(t - 2, "xT"))
                        for c in range(KC):
                            last = nc.tensor.transpose(p_t[b][:, c * TP:(c + 1) * TP], xn[:, b, c * P:(c + 1) * P], k["ident"][0:TP, 0:TP])
                        last.then_inc(*T.done("xT"))
                        pe.wait_ge(*S.after(t, "xT"))
                        pe.wait_ge(*S.after(t - 2, "h"))
                        for c in range(KC):
                            last = nc.tensor.matmul(p_h[b][0:TP, :], xT[:, b, c], w[:, 0, c], start=c == 0, stop=c == KC - 1)
                        last.then_inc(*T.done("h"))
                        pe.wait_ge(*V.after(t - 2, "skip"))
                        for c in range(KC):
                            last = nc.tensor.matmul(p_s[b][0:TP, :], xT[:, b, c], w[:, 1, c], start=c == 0, stop=c == KC - 1)
                        last.then_inc(*T.done("skip"))

            @block.scalar
            def _(act):
                give_credit(act, S)
                for i in turns(act, NT // 2):
                    for b in range(2):
                        t = i * 2 + b
                        act.wait_ge(*T.after(t, "xT"))
                        act.wait_ge(*T.after(t - 2, "skip"))
                        nc.scalar.copy(xT[:, b].rearrange("p c t -> p (c t)"), p_t[b][:, 0:KC * TP]).then_inc(*S.done("xT"))
                        act.wait_ge(*T.after(t, "h"))
                        act.wait_ge(*out.after(i, b, 1))
                        act.wait_ge(*V.after(t - 2, "pdst"))
                        nc.scalar.copy(row[:, b, H:H + DIM], p_h[b][0:TP, :]).then_inc(*S.done("h"))

            def root(t, b, pool):
                pool.wait_ge(*LN.after(t, "aggr"))
                held(pool, passed_pool)
                nc.gpsimd.tensor_scalar(veps[:, b], mv[:, b, 1:2], LN_EPS, None, ALU.add).then_inc(*G.done("veps"))
                pool.wait_ge(*G.after(t, "veps"))
                pool.wait_ge(*LN.after(t - 2, "xn"))
                nc.gpsimd.tensor_tensor(rstd[:, b], veps[:, b], k["minus_half"][0:TP, 0:1], ALU.pow).then_inc(*G.done("rstd"))

            def store(t, b, pool):
                pool.wait_ge(*V.after(t, "max"))
                rows = bass.ds(t * TP, TP)
                pool.dma_start(d["source"][rows, :], row[:, b, 0:SRC_W]).then_inc(*out.done(b))
                pool.dma_start(d["state"][rows, :], row[:, b, H:H + ST_W]).then_inc(*out.done(b))
                pool.dma_start(d["skip"][rows, :], skip[:, b]).then_inc(*out.done(b))

            @block.gpsimd
            def _(pool):
                give_credit(pool, G)
                root(0, 0, pool)
                with pool.Fori(0, NT // 2 - 1) as i:
                    root(i * 2 + 1, 1, pool)
                    store(i * 2, 0, pool)
                    root(i * 2 + 2, 0, pool)
                    store(i * 2 + 1, 1, pool)
                root(NT - 1, 1, pool)
                store(NT - 2, 0, pool)
                store(NT - 1, 1, pool)
                for b in range(2):
                    pool.wait_ge(*out.after(NT // 2 - 1, b))


def send_messages(nc, k, a, d):
    with ExitStack() as ctx:
        m = Mem(nc, ctx, "edges")
        src = m.sb("src", [TP, 2, 1], I32)
        dst = m.sb("dst", [TP, 2, 1], I32)
        dstrow = m.sb("dstrow", [TP, 2, TP], I32)
        dstf = m.sb("dstf", [TP, 2, 1])
        same = m.sb("same", [TP, 2, TP])
        far = m.sb("far", [TP, TP])
        earlier = m.sb("earlier", [TP, TP])
        dup = m.sb("dup", [TP, 1])
        first = m.sb("first", [TP, 1])
        off = m.sb("off", [TP, 1])
        target = m.sb("target", [TP, 2, 1], I32)
        hs = m.sb("hs", [TP, 2, SRC_W])
        st = m.sb("st", [TP, ST_W])
        new = m.sb("new", [TP, ST_W])
        e0 = m.sb("e0", [TP, H])
        e = m.sb("e", [TP, H])
        ebig = m.sb("ebig", [TP, H, TP])
        tmax = m.sb("tmax", [TP, H])
        diff = m.sb("diff", [TP, 2, H])
        scale = m.sb("scale", [TP, H])
        pay = m.sb("pay", [TP, DIM + H])
        p_e = m.ps("p_e", [P, 2, 512])
        p_m = m.ps("p_m", [P, 2, 512])
        idx_in = m.moves("idx_in", 3)
        hs_in = m.moves("hs_in")
        st_in = m.moves("st_in")
        st_out = m.moves("st_out")
        V = m.steps("vector", "dstf same far earlier dup first off target e0 e ebig tmax max dnew dold pay adst acc den acc2 den2")
        S = m.steps("scalar", "ex scale")
        T = m.steps("tensor", "e sum")
        passed_pool = m.sem("passed_pool")
        passed_sp = m.sem("passed_sp")
        with nc.Block() as block:

            @block.sync
            def _(sp):
                for i in turns(sp, NT // 2):
                    for b in range(2):
                        t = i * 2 + b
                        sp.wait_ge(*V.after(t - 2, "target"))
                        held(sp, passed_sp)
                        sp.wait_ge(*hs_in.after(i, b, 1))
                        sp.wait_ge(*st_in.after(i, b, 1))
                        sp.dma_start(src[:, b], a["src"][bass.ds(t * TP, TP)].unsqueeze(1)).then_inc(*idx_in.done(b))
                        sp.dma_start(dst[:, b], a["dst"][bass.ds(t * TP, TP)].unsqueeze(1)).then_inc(*idx_in.done(b))
                        sp.dma_start(dstrow[:, b], a["dst"][bass.ds(t * TP, TP)].partition_broadcast(TP)).then_inc(*idx_in.done(b))

            @block.gpsimd
            def _(pool):
                for i in turns(pool, NT // 2):
                    for b in range(2):
                        t = i * 2 + b
                        pool.wait_ge(*idx_in.after(i, b))
                        pool.wait_ge(*V.after(t - 2, "pay"))
                        held(pool, passed_pool)
                        nc.gpsimd.indirect_dma_start(out=hs[:, b], out_offset=None, in_=d["source"][:, :], in_offset=bass.IndirectOffsetOnAxis(ap=src[:, b], axis=0)).then_inc(*hs_in.done(b))
                        pool.wait_ge(*(st_out.after(i, 0) if b else st_out.after(i, 1, 1)))
                        pool.wait_ge(*V.after(t - 1, "den"))
                        held(pool, passed_pool)
                        nc.gpsimd.indirect_dma_start(out=st[:], out_offset=None, in_=d["state"][:, :], in_offset=bass.IndirectOffsetOnAxis(ap=dst[:, b], axis=0)).then_inc(*st_in.done(b))
                        pool.wait_ge(*V.after(t, "den2"))
                        held(pool, passed_pool)
                        nc.gpsimd.indirect_dma_start(out=d["state"][:, :], out_offset=bass.IndirectOffsetOnAxis(ap=target[:, b], axis=0), in_=new[:], in_offset=None).then_inc(*st_out.done(b))
                for b in range(2):
                    pool.wait_ge(*st_out.after(NT // 2 - 1, b))

            @block.vector
            def _(dve):
                give_credit(dve, V)
                for i in turns(dve, NT // 2):
                    for b in range(2):
                        t = i * 2 + b
                        dve.wait_ge(*idx_in.after(i, b))
                        nc.vector.tensor_copy(dstf[:, b], dst[:, b]).then_inc(*V.done("dstf"))
                        dve.wait_ge(*V.after(t, "dstf"))
                        dve.wait_ge(*T.after(t - 2, "sum"))
                        nc.vector.tensor_scalar(same[:, b], dstrow[:, b], dstf[:, b], None, ALU.is_equal).then_inc(*V.done("same"))
                        dve.wait_ge(*V.after(t, "same"))
                        nc.vector.tensor_scalar(far[:], same[:, b], FAR, -FAR, ALU.mult, ALU.add).then_inc(*V.done("far"))
                        nc.vector.tensor_tensor(earlier[:], same[:, b], k["before"][0:TP, 0:TP], ALU.mult).then_inc(*V.done("earlier"))
                        dve.wait_ge(*V.after(t, "earlier"))
                        nc.vector.reduce_sum(dup[:], earlier[:], AX.X).then_inc(*V.done("dup"))
                        dve.wait_ge(*V.after(t, "dup"))
                        nc.vector.tensor_scalar(first[:], dup[:], 0.0, None, ALU.is_equal).then_inc(*V.done("first"))
                        nc.vector.tensor_tensor(off[:], dstf[:, b], k["dump"][0:TP], ALU.subtract).then_inc(*V.done("off"))
                        dve.wait_ge(*V.after(t, "off"))
                        dve.wait_ge(*st_out.after(i, b, 1))
                        nc.vector.scalar_tensor_tensor(target[:, b], off[:], first[:], k["dump"][0:TP], ALU.mult, ALU.add).then_inc(*V.done("target"))
                        dve.wait_ge(*hs_in.after(i, b))
                        dve.wait_ge(*st_in.after(i, b))
                        nc.vector.tensor_tensor(e0[:], hs[:, b, 0:H], st[:, ST_DST:ST_W], ALU.add).then_inc(*V.done("e0"))
                        dve.wait_ge(*V.after(t, "e0"))
                        nc.vector.scalar_tensor_tensor(e[:], e0[:], NEG_SLOPE, e0[:], ALU.mult, ALU.max).then_inc(*V.done("e"))
                        dve.wait_ge(*T.after(t, "e"))
                        nc.vector.tensor_tensor(ebig[:].rearrange("p (g h) j -> p g h j", g=2),
                                                p_e[0:TP, :, 0:4 * TP].rearrange("p g (h j) -> p g h j", h=4),
                                                far[:].unsqueeze(1).unsqueeze(1).to_broadcast([TP, 2, 4, TP]), ALU.add).then_inc(*V.done("ebig"))
                        dve.wait_ge(*V.after(t, "ebig"))
                        nc.vector.tensor_reduce(tmax[:], ebig[:], AX.X, ALU.max).then_inc(*V.done("tmax"))
                        dve.wait_ge(*V.after(t, "tmax"))
                        dve.wait_ge(*(st_out.after(i, 0) if b else st_out.after(i, 1, 1)))
                        nc.vector.tensor_tensor(new[:, ST_MAX:ST_DST], st[:, ST_MAX:ST_DST], tmax[:], ALU.max).then_inc(*V.done("max"))
                        dve.wait_ge(*V.after(t, "max"))
                        dve.wait_ge(*S.after(t - 1, "scale"))
                        nc.vector.tensor_tensor(diff[:, 0], e[:], new[:, ST_MAX:ST_DST], ALU.subtract).then_inc(*V.done("dnew"))
                        nc.vector.tensor_tensor(diff[:, 1], st[:, ST_MAX:ST_DST], new[:, ST_MAX:ST_DST], ALU.subtract).then_inc(*V.done("dold"))
                        dve.wait_ge(*S.after(t, "ex"))
                        nc.vector.tensor_tensor(heads(pay[:, 0:DIM]), heads(hs[:, b, H:SRC_W]), over_c(pay[:, DIM:DIM + H]), ALU.mult).then_inc(*V.done("pay"))
                        nc.vector.tensor_copy(new[:, ST_DST:ST_W], st[:, ST_DST:ST_W]).then_inc(*V.done("adst"))
                        dve.wait_ge(*S.after(t, "scale"))
                        nc.vector.tensor_tensor(heads(new[:, 0:DIM]), heads(st[:, 0:DIM]), over_c(scale[:]), ALU.mult).then_inc(*V.done("acc"))
                        nc.vector.tensor_tensor(new[:, ST_DEN:ST_MAX], st[:, ST_DEN:ST_MAX], scale[:], ALU.mult).then_inc(*V.done("den"))
                        dve.wait_ge(*T.after(t, "sum"))
                        dve.wait_ge(*V.after(t, "den"))
                        nc.vector.tensor_tensor(new[:, 0:DIM], new[:, 0:DIM], p_m[0:TP, 0, :], ALU.add).then_inc(*V.done("acc2"))
                        nc.vector.tensor_tensor(new[:, ST_DEN:ST_MAX], new[:, ST_DEN:ST_MAX], p_m[0:TP, 1, 0:H], ALU.add).then_inc(*V.done("den2"))

            @block.scalar
            def _(act):
                give_credit(act, S)
                with act.Fori(0, NT // 2) as i:
                    for b in range(2):
                        t = i * 2 + b
                        act.wait_ge(*V.after(t, "dold"))
                        act.wait_ge(*T.after(t - 1, "sum"))
                        nc.scalar.activation(pay[:, DIM:DIM + H], diff[:, 0], ACT.Exp).then_inc(*S.done("ex"))
                        act.wait_ge(*V.after(t - 1, "den"))
                        nc.scalar.activation(scale[:], diff[:, 1], ACT.Exp).then_inc(*S.done("scale"))

            @block.tensor
            def _(pe):
                give_credit(pe, T)
                with pe.Fori(0, NT // 2) as i:
                    for b in range(2):
                        t = i * 2 + b
                        pe.wait_ge(*V.after(t, "e"))
                        pe.wait_ge(*V.after(t - 1, "ebig"))
                        for h in range(H):
                            last = nc.tensor.matmul(p_e[0:TP, h // 4, (h % 4) * TP:(h % 4 + 1) * TP], e[:, h:h + 1].to_broadcast([TP, TP]),
                                                    k["ident"][0:TP, 0:TP], start=True, stop=True)
                        last.then_inc(*T.done("e"))
                        pe.wait_ge(*V.after(t, "pay"))
                        pe.wait_ge(*V.after(t - 1, "den2"))
                        nc.tensor.matmul(p_m[0:TP, 0, :], same[:, b], pay[:, 0:DIM], start=True, stop=True)
                        nc.tensor.matmul(p_m[0:TP, 1, 0:H], same[:, b], pay[:, DIM:DIM + H], start=True, stop=True).then_inc(*T.done("sum"))


def batch_norm(nc, k, a, d, keep):
    with ExitStack() as ctx:
        m = Mem(nc, ctx, "bn")
        bias = m.sb("bias", [P, DIM])
        gamma = m.sb("gamma", [P, DIM])
        beta = m.sb("beta", [P, DIM])
        st = m.sb("st", [TP, 2, ST_MAX])
        rden = m.sb("rden", [TP, 2, H])
        o = m.sb("o", [TP, 2, DIM])
        sq = m.sb("sq", [TP, 2, DIM])
        ob = m.sb("ob", [TP, 2, DIM])
        mean = m.sb("mean", [P, DIM])
        meansq = m.sb("meansq", [P, DIM])
        var = m.sb("var", [P, DIM])
        p_s = m.ps("p_s")
        p_q = m.ps("p_q")
        weights = m.sem("weights")
        end = m.sem("end")
        root = m.sem("root")
        st_in = m.moves("st_in")
        out = m.moves("out")
        V = m.steps("vector", "rden o ob")
        S = m.steps("scalar", "sq")
        T = m.steps("tensor", "sum sumsq")
        with nc.Block() as block:

            @block.sync
            def _(sp):
                sp.dma_start(bias[:], a["L0_gnn_gat_bias"].partition_broadcast(P)).then_inc(weights, 16)
                sp.dma_start(gamma[:], a["L0_gnn_bn_gamma"].partition_broadcast(P)).then_inc(weights, 16)
                sp.dma_start(beta[:], a["L0_gnn_bn_beta"].partition_broadcast(P)).then_inc(weights, 16)
                with sp.Fori(0, NT // 2) as i:
                    for b in range(2):
                        t = i * 2 + b
                        sp.wait_ge(*V.after(t - 2, "o"))
                        sp.dma_start(st[:, b], d["state"][bass.ds(t * TP, TP), 0:ST_MAX]).then_inc(*st_in.done(b))

            @block.vector
            def _(dve):
                give_credit(dve, V)
                dve.wait_ge(weights, 48)
                for i in turns(dve, NT // 2):
                    for b in range(2):
                        t = i * 2 + b
                        dve.wait_ge(*st_in.after(i, b))
                        nc.vector.reciprocal(rden[:, b], st[:, b, ST_DEN:ST_MAX]).then_inc(*V.done("rden"))
                        dve.wait_ge(*V.after(t, "rden"))
                        dve.wait_ge(*T.after(t - 2, "sum"))
                        dve.wait_ge(*S.after(t - 2, "sq"))
                        nc.vector.tensor_tensor(heads(o[:, b]), heads(st[:, b, 0:DIM]), over_c(rden[:, b]), ALU.mult).then_inc(*V.done("o"))
                        dve.wait_ge(*V.after(t, "o"))
                        dve.wait_ge(*out.after(i, b, 1))
                        nc.vector.tensor_tensor(ob[:, b], o[:, b], bias[0:TP], ALU.add).then_inc(*V.done("ob"))
                dve.wait_ge(end, 1)
                step = [1]

                def then(ins):
                    step[0] += 1
                    ins.then_inc(end, 1)
                    dve.wait_ge(end, step[0])

                then(nc.vector.tensor_scalar(mean[:], p_s[:], 1.0 / N, None, ALU.mult))
                then(nc.vector.tensor_tensor(meansq[:], mean[:], mean[:], ALU.mult))
                then(nc.vector.scalar_tensor_tensor(var[:], p_q[:], 1.0 / N, meansq[:], ALU.mult, ALU.subtract))
                then(nc.vector.tensor_scalar(var[:], var[:], 0.0, BN_EPS, ALU.max, ALU.add))
                dve.wait_ge(root, 1)
                then(nc.vector.reciprocal(var[:], var[:]))
                then(nc.vector.tensor_tensor(keep["bn_scale"][:], var[:], gamma[:], ALU.mult))
                then(nc.vector.tensor_tensor(mean[:], mean[:], bias[:], ALU.add))
                then(nc.vector.tensor_tensor(mean[:], mean[:], keep["bn_scale"][:], ALU.mult))
                then(nc.vector.tensor_tensor(keep["bn_shift"][:], beta[:], mean[:], ALU.subtract))

            @block.scalar
            def _(act):
                give_credit(act, S)
                with act.Fori(0, NT // 2) as i:
                    for b in range(2):
                        t = i * 2 + b
                        act.wait_ge(*V.after(t, "o"))
                        act.wait_ge(*T.after(t - 2, "sumsq"))
                        nc.scalar.activation(sq[:, b], o[:, b], ACT.Square).then_inc(*S.done("sq"))
                act.wait_ge(end, 5)
                nc.scalar.activation(var[:], var[:], ACT.Sqrt).then_inc(root, 1)

            @block.tensor
            def _(pe):
                give_credit(pe, T)
                nc.tensor.matmul(p_s[:], k["zeros"][:, 0:P], k["zeros"][:, 0:DIM], start=True, stop=False)
                nc.tensor.matmul(p_q[:], k["zeros"][:, 0:P], k["zeros"][:, 0:DIM], start=True, stop=False)
                with pe.Fori(0, NT // 2) as i:
                    for b in range(2):
                        t = i * 2 + b
                        pe.wait_ge(*V.after(t, "o"))
                        nc.tensor.matmul(p_s[:], k["ones"][0:TP, :], o[:, b], start=False, stop=False).then_inc(*T.done("sum"))
                        pe.wait_ge(*S.after(t, "sq"))
                        nc.tensor.matmul(p_q[:], k["ones"][0:TP, :], sq[:, b], start=False, stop=False).then_inc(*T.done("sumsq"))
                nc.tensor.matmul(p_s[:], k["zeros"][:, 0:P], k["zeros"][:, 0:DIM], start=False, stop=True)
                nc.tensor.matmul(p_q[:], k["zeros"][:, 0:P], k["zeros"][:, 0:DIM], start=False, stop=True).then_inc(end, 1)

            @block.gpsimd
            def _(pool):
                with pool.Fori(0, NT // 2) as i:
                    for b in range(2):
                        t = i * 2 + b
                        pool.wait_ge(*V.after(t, "ob"))
                        pool.dma_start(d["gat"][bass.ds(t * TP, TP), :], ob[:, b]).then_inc(*out.done(b))
                for b in range(2):
                    pool.wait_ge(*out.after(NT // 2 - 1, b))


def project_tokens(nc, k, a, d, keep):
    ZW = NE + 2 * H
    with ExitStack() as ctx:
        m = Mem(nc, ctx, "tokens")
        w = m.sb("w", [P, 4, KC, DIM])
        wz = m.sb("wz", [P, KC, ZW])
        decay = m.sb("decay", [P, H])
        dtb = m.sb("dtb", [P, H])
        tie = m.sb("tie", [P, NE, NE])
        gat = m.sb("gat", [TP, 2, DIM])
        xin = m.sb("xin", [TP, 2, DIM])
        skip = m.sb("skip", [TP, 2, DIM])
        res = m.sb("res", [TP, DIM])
        y = m.sb("y", [TP, DIM])
        gl = m.sb("gl", [TP, DIM])
        x2 = m.sb("x2", [TP, 2, DIM])
        stats = m.sb("stats", [TP, 6])
        mv = m.sb("mv", [TP, 2])
        veps = m.sb("veps", [TP, 1])
        rstd = m.sb("rstd", [TP, 1])
        xn = m.sb("xn", [TP, 2, DIM])
        xT = m.sb("xT", [P, 2, KC, TP])
        row = m.sb("row", [TP, 2, TK_W])
        gate = m.sb("gate", [TP, 2, DIM])
        sq = m.sb("sq", [TP, 2 * DIM])
        ss = m.sb("ss", [TP, 2 * H])
        rn = m.sb("rn", [TP, 2 * H])
        z = m.sb("z", [TP, ZW])
        ez = m.sb("ez", [TP, ZW])
        top = m.sb("top", [TP, 1])
        za = m.sb("za", [TP, H])
        zn = m.sb("zn", [TP, H])
        s1 = m.sb("s1", [TP, H])
        s2 = m.sb("s2", [TP, H])
        s3 = m.sb("s3", [TP, H])
        poly = m.sb("poly", [TP, 9, H])
        b1 = m.sb("b1", [TP, H])
        psum_ = m.sb("psum", [TP, 1])
        pr = m.sb("pr", [TP, NE])
        gt = m.sb("gt", [TP, NE, NE])
        eq = m.sb("eq", [TP, NE, NE])
        rank = m.sb("rank", [TP, NE])
        two = m.sb("two", [TP, NE])
        wsum = m.sb("wsum", [TP, 1])
        p_t = m.ps("p_t")
        p_z = m.ps("p_z")
        p_w = [m.ps(f"p_w{j}") for j in range(4)]
        weights = m.sem("weights")
        ready = m.sem("ready")
        loads = m.moves("loads", 3)
        out = m.moves("out", 3)
        L = m.steps("ahead", "scaled y x2 stats aggr xn")
        V = m.steps("vector", "top zmax zb za zn nza b1 beta nbeta s1 s2 s3 "
                              "poly0 poly1 poly2 poly3 poly4 poly5 poly6 poly7 poly8 log pos sp g gfloor "
                              "psum prs pr gt eqr eq both rank two w1 wsum wrec w mask ss rn_q rn_k")
        GL = m.steps("gpsimd_ahead", "res veps rstd")
        G = m.steps("gpsimd", "sq sseps rn")
        SL = m.steps("scalar_ahead", "gelu xT")
        S = m.steps("scalar", "exp q k v gate")
        T = m.steps("tensor", "xT z q k v gate")
        passed_dve = m.sem("passed_dve")
        passed_pool = m.sem("passed_pool")
        with nc.Block() as block:

            @block.sync
            def _(sp):
                for j, name in enumerate(("Wq", "Wk", "Wv", "Wg")):
                    sp.dma_start(w[:, j], a["L0_ffn_" + name].rearrange("(c p) n -> p c n", p=P)).then_inc(weights, 16)
                sp.dma_start(wz[:, :, 0:NE], a["L0_ffn_Wgate"].rearrange("(c p) n -> p c n", p=P)).then_inc(weights, 16)
                sp.dma_start(wz[:, :, NE:NE + H], a["L0_ffn_Wb"].rearrange("(c p) n -> p c n", p=P)).then_inc(weights, 16)
                sp.dma_start(wz[:, :, NE + H:ZW], a["L0_ffn_Wa"].rearrange("(c p) n -> p c n", p=P)).then_inc(weights, 16)
                sp.dma_start(decay[:], a["L0_ffn_A_log"].partition_broadcast(P)).then_inc(weights, 16)
                sp.dma_start(dtb[:], a["L0_ffn_dt_bias"].partition_broadcast(P)).then_inc(weights, 16)
                with sp.Fori(0, NT // 2) as i:
                    for b in range(2):
                        t = i * 2 + b
                        rows = bass.ds(t * TP, TP)
                        sp.wait_ge(*L.after(t - 2, "scaled"))
                        sp.wait_ge(*GL.after(t - 2, "res"))
                        sp.dma_start(gat[:, b], d["gat"][rows, :]).then_inc(*loads.done(b))
                        sp.dma_start(xin[:, b], a["x"][rows, :]).then_inc(*loads.done(b))
                        sp.dma_start(skip[:, b], d["skip"][rows, :]).then_inc(*loads.done(b))

            def norm(t, i, b, dve):
                dve.wait_ge(*loads.after(i, b))
                nc.vector.tensor_tensor(y[:], gat[:, b], keep["bn_scale"][0:TP], ALU.mult).then_inc(*L.done("scaled"))
                dve.wait_ge(*L.after(t, "scaled"))
                nc.vector.tensor_tensor(y[:], y[:], keep["bn_shift"][0:TP], ALU.add).then_inc(*L.done("y"))
                dve.wait_ge(*SL.after(t, "gelu"))
                dve.wait_ge(*GL.after(t, "res"))
                dve.wait_ge(*out.after(i, b, 1))
                nc.vector.tensor_tensor(x2[:, b], gl[:], res[:], ALU.add).then_inc(*L.done("x2"))
                dve.wait_ge(*L.after(t, "x2"))
                nc.vector.bn_stats(stats[:], x2[:, b]).then_inc(*L.done("stats"))
                dve.wait_ge(*L.after(t, "stats"))
                held(dve, passed_dve)
                nc.vector.bn_aggr(mv[:], stats[:]).then_inc(*L.done("aggr"))
                dve.wait_ge(*GL.after(t, "rstd"))
                dve.wait_ge(*T.after(t - 2, "xT"))
                nc.vector.tensor_scalar(xn[:, b], x2[:, b], mv[:, 0:1], rstd[:], ALU.subtract, ALU.mult).then_inc(*L.done("xn"))

            def heads_and_router(t, i, b, dve):
                dve.wait_ge(*T.after(t, "z"))
                dve.wait_ge(*S.after(t - 1, "exp"))
                nc.vector.reduce_max(top[:], p_z[0:TP, 0:NE], AX.X).then_inc(*V.done("top"))
                dve.wait_ge(*V.after(t, "top"))
                nc.vector.tensor_scalar(z[:, 0:NE], p_z[0:TP, 0:NE], top[:], None, ALU.subtract).then_inc(*V.done("zmax"))
                nc.vector.tensor_scalar(z[:, NE:NE + H], p_z[0:TP, NE:NE + H], -1.0, None, ALU.mult).then_inc(*V.done("zb"))
                nc.vector.tensor_tensor(za[:], p_z[0:TP, NE + H:ZW], dtb[0:TP], ALU.add).then_inc(*V.done("za"))
                dve.wait_ge(*V.after(t, "za"))
                nc.vector.tensor_scalar(zn[:], za[:], -1.0, None, ALU.mult).then_inc(*V.done("zn"))
                dve.wait_ge(*V.after(t, "zn"))
                nc.vector.tensor_tensor(z[:, NE + H:ZW], za[:], zn[:], ALU.min).then_inc(*V.done("nza"))
                dve.wait_ge(*S.after(t, "exp"))
                nc.vector.tensor_scalar(b1[:], ez[:, NE:NE + H], 1.0, None, ALU.add).then_inc(*V.done("b1"))
                dve.wait_ge(*V.after(t, "b1"))
                dve.wait_ge(*out.after(i, b, 1))
                nc.vector.reciprocal(row[:, b, TK_B:TK_NB], b1[:]).then_inc(*V.done("beta"))
                dve.wait_ge(*V.after(t, "beta"))
                nc.vector.tensor_scalar(row[:, b, TK_NB:TK_G], row[:, b, TK_B:TK_NB], -1.0, None, ALU.mult).then_inc(*V.done("nbeta"))
                nc.vector.tensor_scalar(s1[:], ez[:, NE + H:ZW], 2.0, None, ALU.add).then_inc(*V.done("s1"))
                dve.wait_ge(*V.after(t, "s1"))
                nc.vector.reciprocal(s2[:], s1[:]).then_inc(*V.done("s2"))
                dve.wait_ge(*V.after(t, "s2"))
                nc.vector.tensor_tensor(s1[:], s2[:], ez[:, NE + H:ZW], ALU.mult).then_inc(*V.done("s3"))
                dve.wait_ge(*V.after(t, "s3"))
                nc.vector.tensor_tensor(s3[:], s1[:], s1[:], ALU.mult).then_inc(*V.done("poly0"))
                dve.wait_ge(*V.after(t, "poly0"))
                nc.vector.tensor_scalar(poly[:, 0], s3[:], 2.0 / 17, None, ALU.mult).then_inc(*V.done("poly1"))
                for j in range(7):
                    dve.wait_ge(*V.after(t, f"poly{j + 1}"))
                    nc.vector.scalar_tensor_tensor(poly[:, j + 1], poly[:, j], 2.0 / (15 - 2 * j), s3[:], ALU.add, ALU.mult).then_inc(*V.done(f"poly{j + 2}"))
                dve.wait_ge(*V.after(t, "poly8"))
                nc.vector.scalar_tensor_tensor(poly[:, 8], poly[:, 7], 2.0, s1[:], ALU.add, ALU.mult).then_inc(*V.done("log"))
                nc.vector.tensor_scalar(zn[:], za[:], 0.0, None, ALU.max).then_inc(*V.done("pos"))
                dve.wait_ge(*V.after(t, "pos"))
                nc.vector.tensor_tensor(zn[:], zn[:], poly[:, 8], ALU.add).then_inc(*V.done("sp"))
                dve.wait_ge(*V.after(t, "sp"))
                nc.vector.scalar_tensor_tensor(za[:], zn[:], -1.0, decay[0:TP], ALU.mult, ALU.mult).then_inc(*V.done("g"))
                dve.wait_ge(*V.after(t, "g"))
                nc.vector.tensor_scalar(row[:, b, TK_G:TK_W], za[:], G_FLOOR, None, ALU.max).then_inc(*V.done("gfloor"))
                nc.vector.reduce_sum(psum_[:], ez[:, 0:NE], AX.X).then_inc(*V.done("psum"))
                dve.wait_ge(*V.after(t, "psum"))
                nc.vector.reciprocal(wsum[:], psum_[:]).then_inc(*V.done("prs"))
                dve.wait_ge(*V.after(t, "prs"))
                nc.vector.tensor_scalar(pr[:], ez[:, 0:NE], wsum[:], None, ALU.mult).then_inc(*V.done("pr"))
                dve.wait_ge(*V.after(t, "pr"))
                mine, other = pr[:].unsqueeze(2).to_broadcast([TP, NE, NE]), pr[:].unsqueeze(1).to_broadcast([TP, NE, NE])
                nc.vector.tensor_tensor(gt[:], other, mine, ALU.is_gt).then_inc(*V.done("gt"))
                nc.vector.tensor_tensor(eq[:], other, mine, ALU.is_equal).then_inc(*V.done("eqr"))
                dve.wait_ge(*V.after(t, "eqr"))
                nc.vector.tensor_tensor(eq[:], eq[:], tie[0:TP], ALU.mult).then_inc(*V.done("eq"))
                dve.wait_ge(*V.after(t, "eq"))
                nc.vector.tensor_tensor(gt[:], gt[:], eq[:], ALU.add).then_inc(*V.done("both"))
                dve.wait_ge(*V.after(t, "both"))
                nc.vector.tensor_reduce(rank[:], gt[:], AX.X, ALU.add).then_inc(*V.done("rank"))
                dve.wait_ge(*V.after(t, "rank"))
                nc.vector.tensor_scalar(two[:], rank[:], 1.5, None, ALU.is_lt).then_inc(*V.done("two"))
                dve.wait_ge(*V.after(t, "two"))
                nc.vector.tensor_tensor(two[:], two[:], pr[:], ALU.mult).then_inc(*V.done("w1"))
                dve.wait_ge(*V.after(t, "w1"))
                nc.vector.reduce_sum(psum_[:], two[:], AX.X).then_inc(*V.done("wsum"))
                dve.wait_ge(*V.after(t, "wsum"))
                nc.vector.reciprocal(wsum[:], psum_[:]).then_inc(*V.done("wrec"))
                dve.wait_ge(*V.after(t, "wrec"))
                nc.vector.tensor_scalar(two[:], two[:], wsum[:], None, ALU.mult).then_inc(*V.done("w"))
                dve.wait_ge(*V.after(t, "w"))
                nc.vector.tensor_copy(keep["weight"][0:TP, :, bass.ds(t, 1)], two[:].unsqueeze(2)).then_inc(*V.done("mask"))
                dve.wait_ge(*G.after(t, "sq"))
                dve.wait_ge(*G.after(t - 1, "sseps"))
                nc.vector.tensor_reduce(ss[:], heads(sq[:], 2 * H), AX.X, ALU.add).then_inc(*V.done("ss"))
                dve.wait_ge(*G.after(t, "rn"))
                nc.vector.scalar_tensor_tensor(heads(row[:, b, 0:DIM]), heads(row[:, b, 0:DIM]), float(C) ** -0.5, over_c(rn[:, 0:H]), ALU.mult, ALU.mult).then_inc(*V.done("rn_q"))
                nc.vector.tensor_tensor(heads(row[:, b, TK_K:TK_V]), heads(row[:, b, TK_K:TK_V]), over_c(rn[:, H:2 * H]), ALU.mult).then_inc(*V.done("rn_k"))

            @block.vector
            def _(dve):
                give_credit(dve, V, L)
                dve.wait_ge(weights, 16 * 9)
                dve.wait_ge(ready, 2)
                norm(0, 0, 0, dve)
                for i in turns(dve, NT // 2 - 1):
                    norm(i * 2 + 1, i, 1, dve)
                    heads_and_router(i * 2, i, 0, dve)
                    norm(i * 2 + 2, i + 1, 0, dve)
                    heads_and_router(i * 2 + 1, i, 1, dve)
                norm(NT - 1, NT // 2 - 1, 1, dve)
                heads_and_router(NT - 2, NT // 2 - 1, 0, dve)
                heads_and_router(NT - 1, NT // 2 - 1, 1, dve)

            def residual(t, b, i, pool):
                pool.wait_ge(*loads.after(i, b))
                pool.wait_ge(*L.after(t - 1, "x2"))
                nc.gpsimd.tensor_tensor(res[:], xin[:, b], skip[:, b], ALU.add).then_inc(*GL.done("res"))
                pool.wait_ge(*L.after(t, "aggr"))
                held(pool, passed_pool)
                nc.gpsimd.tensor_scalar(veps[:], mv[:, 1:2], LN_EPS, None, ALU.add).then_inc(*GL.done("veps"))
                pool.wait_ge(*GL.after(t, "veps"))
                pool.wait_ge(*L.after(t - 1, "xn"))
                nc.gpsimd.tensor_tensor(rstd[:], veps[:], k["minus_half"][0:TP], ALU.pow).then_inc(*GL.done("rstd"))

            def squares(t, b, i, pool):
                pool.wait_ge(*S.after(t, "k"))
                pool.wait_ge(*V.after(t - 1, "ss"))
                nc.gpsimd.tensor_tensor(sq[:], row[:, b, 0:TK_V], row[:, b, 0:TK_V], ALU.mult).then_inc(*G.done("sq"))
                pool.wait_ge(*V.after(t, "ss"))
                held(pool, passed_pool)
                nc.gpsimd.tensor_scalar(ss[:], ss[:], 1e-6, None, ALU.add).then_inc(*G.done("sseps"))
                pool.wait_ge(*G.after(t, "sseps"))
                pool.wait_ge(*V.after(t - 1, "rn_k"))
                nc.gpsimd.tensor_tensor(rn[:], ss[:], k["minus_half"][0:TP].to_broadcast([TP, 2 * H]), ALU.pow).then_inc(*G.done("rn"))
                pool.wait_ge(*V.after(t, "rn_k"))
                pool.wait_ge(*S.after(t, "gate"))
                rows = bass.ds(t * TP, TP)
                pool.dma_start(d["token"][rows, :], row[:, b]).then_inc(*out.done(b))
                pool.dma_start(d["gate"][rows, :], gate[:, b]).then_inc(*out.done(b))
                pool.dma_start(d["x2"][rows, :], x2[:, b]).then_inc(*out.done(b))

            @block.gpsimd
            def _(pool):
                give_credit(pool, G, GL)
                nc.gpsimd.memset(tie[:], 1.0).then_inc(ready, 1)
                pool.wait_ge(ready, 2)
                nc.gpsimd.affine_select(out=tie[:], in_=tie[:], pattern=[[1, NE], [-1, NE]], compare_op=ALU.is_gt, fill=0.0, base=0, channel_multiplier=0).then_inc(ready, 1)
                residual(0, 0, 0, pool)
                with pool.Fori(0, NT // 2 - 1) as i:
                    residual(i * 2 + 1, 1, i, pool)
                    squares(i * 2, 0, i, pool)
                    residual(i * 2 + 2, 0, i + 1, pool)
                    squares(i * 2 + 1, 1, i, pool)
                residual(NT - 1, 1, NT // 2 - 1, pool)
                squares(NT - 2, 0, NT // 2 - 1, pool)
                squares(NT - 1, 1, NT // 2 - 1, pool)
                for b in range(2):
                    pool.wait_ge(*out.after(NT // 2 - 1, b))

            def ahead(t, b, act):
                act.wait_ge(*L.after(t, "y"))
                act.wait_ge(*L.after(t - 1, "x2"))
                nc.scalar.activation(gl[:], y[:], ACT.Gelu).then_inc(*SL.done("gelu"))
                act.wait_ge(*T.after(t, "xT"))
                act.wait_ge(*T.after(t - 2, "gate"))
                nc.scalar.copy(xT[:, b].rearrange("p c t -> p (c t)"), p_t[:, 0:KC * TP]).then_inc(*SL.done("xT"))

            def behind(t, i, b, act):
                act.wait_ge(*V.after(t, "nza"))
                act.wait_ge(*V.after(t - 1, "pr"))
                nc.scalar.activation(ez[:], z[:], ACT.Exp).then_inc(*S.done("exp"))
                act.wait_ge(*out.after(i, b, 1))
                for j, name in enumerate(("q", "k", "v", "gate")):
                    act.wait_ge(*T.after(t, name))
                    to = gate[:, b] if j == 3 else row[:, b, j * DIM:(j + 1) * DIM]
                    nc.scalar.activation(to, p_w[j][0:TP, :], ACT.Silu).then_inc(*S.done(name))

            @block.scalar
            def _(act):
                give_credit(act, S, SL)
                act.wait_ge(weights, 16 * 9)
                nc.scalar.activation(decay[:], decay[:], ACT.Exp).then_inc(ready, 1)
                ahead(0, 0, act)
                for i in turns(act, NT // 2 - 1):
                    ahead(i * 2 + 1, 1, act)
                    behind(i * 2, i, 0, act)
                    ahead(i * 2 + 2, 0, act)
                    behind(i * 2 + 1, i, 1, act)
                ahead(NT - 1, 1, act)
                behind(NT - 2, NT // 2 - 1, 0, act)
                behind(NT - 1, NT // 2 - 1, 1, act)

            def transposes(t, b, pe):
                pe.wait_ge(*L.after(t, "xn"))
                pe.wait_ge(*SL.after(t - 1, "xT"))
                for c in range(KC):
                    last = nc.tensor.transpose(p_t[:, c * TP:(c + 1) * TP], xn[:, b, c * P:(c + 1) * P], k["ident"][0:TP, 0:TP])
                last.then_inc(*T.done("xT"))

            @block.tensor
            def _(pe):
                give_credit(pe, T)
                pe.wait_ge(weights, 16 * 9)
                with pe.Fori(0, NT // 2) as i:
                    for b in range(2):
                        t = i * 2 + b
                        transposes(t, b, pe)
                        pe.wait_ge(*SL.after(t, "xT"))
                        pe.wait_ge(*V.after(t - 1, "za"))
                        for c in range(KC):
                            last = nc.tensor.matmul(p_z[0:TP, 0:ZW], xT[:, b, c], wz[:, c], start=c == 0, stop=c == KC - 1)
                        last.then_inc(*T.done("z"))
                        for j, name in enumerate(("q", "k", "v", "gate")):
                            pe.wait_ge(*S.after(t - 1, name))
                            for c in range(KC):
                                last = nc.tensor.matmul(p_w[j][0:TP, :], xT[:, b, c], w[:, j, c], start=c == 0, stop=c == KC - 1)
                            last.then_inc(*T.done(name))


def route(nc, k, a, d, keep):
    M = NE * NT
    with ExitStack() as ctx:
        m = Mem(nc, ctx, "route")
        mask = m.sb("mask", [P, NE, NT])
        prefix = m.sb("prefix", [P, NE, NT])
        total = m.sb("total", [P, NE, NT])
        upto = m.sb("upto", [P, NE, NT])
        pos = m.sb("pos", [P, NE, NT])
        hid = m.sb("hid", [P, NE, NT])
        tmp = m.sb("tmp", [P, NE, NT])
        sel = m.sb("sel", [P, NE, NT])
        one = m.sb("one", [P, NT])
        starts = m.sb("starts", [P, NE + 1])
        count = m.sb("count", [P, NCH])
        chunks = m.sb("chunks", [P, NE])
        slot = m.sb("slot", [P, 2, NT])
        both = m.sb("both", [P, NT])
        dumped = m.sb("dumped", [P, NT])
        isstart = m.sb("isstart", [P, NCH + 2])
        sc = m.sb("sc", [P, 2, NT], I32)
        token = m.sb("token", [P, NT], I32)
        zero = m.sb("zero", [P, NCH + 2], I32)
        col = m.sb("col", [TP, 2, 3, 1], I32)
        p_p = m.ps("p_p")
        p_t = m.ps("p_t")
        V = m.sem("vector")
        made = m.sem("made")
        counted = m.sem("counted")
        cleared = m.sem("cleared")
        G = m.steps("gpsimd", "copy0 copy1 copy2")
        moved = m.moves("moved", 2)
        ROUTED = 70
        n_steps = [0]
        passed_pool = m.sem("passed_pool")
        with nc.Block() as block:

            @block.vector
            def _(dve):
                step = [0]

                def then(ins):
                    step[0] += 1
                    ins.then_inc(V, 1)
                    dve.wait_ge(V, step[0])

                wt = keep["weight"]
                then(nc.vector.memset(one[:], 1.0))
                then(nc.vector.tensor_scalar(mask[0:TP], wt[0:TP], 0.0, None, ALU.is_gt))
                dve.wait_ge(counted, 1)
                then(nc.vector.tensor_copy(prefix[0:TP].rearrange("p e t -> p (e t)"), p_p[0:TP, 0:M]))
                then(nc.vector.tensor_copy(total[:].rearrange("p e t -> p (e t)"), p_t[:, 0:M]))
                for e in range(NE):
                    then(nc.vector.tensor_tensor_scan(upto[:, e], one[:], total[:, e], 0.0, ALU.mult, ALU.add))
                then(nc.vector.memset(starts[:], 0.0))
                for e in range(NE):
                    then(nc.vector.tensor_scalar(count[:], k["chunk_no"][:, 0:NCH], float(CH), upto[:, e, NT - 1:NT], ALU.mult, ALU.is_lt))
                    then(nc.vector.reduce_sum(chunks[:, e:e + 1], count[:], AX.X))
                    then(nc.vector.tensor_tensor(starts[:, e + 1:e + 2], starts[:, e:e + 1], chunks[:, e:e + 1], ALU.add))
                then(nc.vector.tensor_tensor(pos[:], upto[:], total[:], ALU.subtract))
                then(nc.vector.tensor_tensor(pos[0:TP], pos[0:TP], prefix[0:TP], ALU.add))
                for e in range(NE):
                    then(nc.vector.tensor_scalar(count[:, 0:1], starts[:, e:e + 1], float(CH), None, ALU.mult))
                    then(nc.vector.tensor_scalar(pos[:, e], pos[:, e], count[:, 0:1], None, ALU.add))
                for s, (far, op) in enumerate(((1.0, ALU.min), (-1.0, ALU.max))):
                    then(nc.vector.tensor_scalar(hid[0:TP], mask[0:TP], -1e6 * far, 1e6 * far, ALU.mult, ALU.add))
                    then(nc.vector.tensor_tensor(tmp[0:TP], pos[0:TP], mask[0:TP], ALU.mult))
                    then(nc.vector.tensor_tensor(tmp[0:TP], tmp[0:TP], hid[0:TP], ALU.add))
                    then(nc.vector.tensor_reduce(slot[0:TP, s], tmp[0:TP].rearrange("p e t -> p t e"), AX.X, op))
                    then(nc.vector.tensor_tensor(sel[0:TP], tmp[0:TP], slot[0:TP, s].unsqueeze(1).to_broadcast([TP, NE, NT]), ALU.is_equal))
                    then(nc.vector.tensor_tensor(sel[0:TP], sel[0:TP], wt[0:TP], ALU.mult))
                    then(nc.vector.tensor_reduce(keep["slot_weight"][0:TP, s], sel[0:TP].rearrange("p e t -> p t e"), AX.X, ALU.add))
                then(nc.vector.tensor_tensor(both[0:TP], slot[0:TP, 1], slot[0:TP, 0], ALU.is_gt))
                then(nc.vector.tensor_tensor(keep["slot_weight"][0:TP, 1], keep["slot_weight"][0:TP, 1], both[0:TP], ALU.mult))
                then(nc.vector.tensor_copy(keep["slot"][0:TP], slot[0:TP]))
                then(nc.vector.tensor_copy(sc[0:TP, 0], slot[0:TP, 0]))
                then(nc.vector.tensor_scalar(dumped[0:TP], slot[0:TP, 1], k["dumpslot"][0:TP], None, ALU.subtract))
                then(nc.vector.tensor_tensor(dumped[0:TP], dumped[0:TP], both[0:TP], ALU.mult))
                then(nc.vector.tensor_scalar(sc[0:TP, 1], dumped[0:TP], k["dumpslot"][0:TP], None, ALU.add))
                then(nc.vector.memset(keep["goes_on"][:], 1.0))
                for e in range(NE):
                    then(nc.vector.tensor_scalar(isstart[:], k["chunk_no"][:], starts[:, e:e + 1], None, ALU.not_equal))
                    then(nc.vector.tensor_tensor(keep["goes_on"][:], keep["goes_on"][:], isstart[:], ALU.mult))
                n_steps[0] = step[0]

            @block.tensor
            def _(pe):
                pe.wait_ge(V, 2)
                nc.tensor.matmul(p_p[0:TP, 0:M], k["after"][0:TP, 0:TP], mask[0:TP].rearrange("p e t -> p (e t)"), start=True, stop=True)
                nc.tensor.matmul(p_t[:, 0:M], k["ones"][0:TP, :], mask[0:TP].rearrange("p e t -> p (e t)"), start=True, stop=True).then_inc(counted, 1)

            @block.gpsimd
            def _(pool):
                give_credit(pool, G)
                nc.gpsimd.iota(token[:], [[TP, NT]], base=0, channel_multiplier=1)
                nc.gpsimd.memset(zero[:], 0).then_inc(made, 1)
                pool.wait_ge(cleared, 16)
                pool.wait_ge(V, n_steps[0])
                for i in turns(pool, NT // 2):
                    for b in range(2):
                        t = i * 2 + b
                        pool.wait_ge(*moved.after(i, b, 1))
                        nc.gpsimd.tensor_copy(col[:, b, 0], sc[0:TP, 0, bass.ds(t, 1)]).then_inc(*G.done("copy0"))
                        nc.gpsimd.tensor_copy(col[:, b, 1], sc[0:TP, 1, bass.ds(t, 1)]).then_inc(*G.done("copy1"))
                        nc.gpsimd.tensor_copy(col[:, b, 2], token[0:TP, bass.ds(t, 1)]).then_inc(*G.done("copy2"))
                        pool.wait_ge(*G.after(t, "copy2"))
                        held(pool, passed_pool)
                        for s in range(2):
                            nc.gpsimd.indirect_dma_start(out=d["table"][:, :], out_offset=bass.IndirectOffsetOnAxis(ap=col[:, b, s], axis=0), in_=col[:, b, 2], in_offset=None).then_inc(*moved.done(b))
                for b in range(2):
                    pool.wait_ge(*moved.after(NT // 2 - 1, b))

            @block.sync
            def _(sp):
                sp.wait_ge(made, 1)
                sp.dma_start(d["table"].rearrange("(p c) o -> p (c o)", p=P), zero[:]).then_inc(cleared, 16)
                sp.wait_ge(cleared, 16)


def delta_rule(nc, k, a, d, keep):
    LV = 7
    with ExitStack() as ctx:
        m = Mem(nc, ctx, "delta")
        idx = m.sb("idx", [P, 2, 1], I32)
        x = m.sb("x", [P, 2, TK_W])
        kb = m.sb("kb", [P, DIM])
        vb = m.sb("vb", [P, 2, DIM])
        gb = m.sb("gb", [P, H, P])
        kT = m.sb("kT", [P, 4, P])
        qT = m.sb("qT", [P, 2, 4, P])
        kbT = m.sb("kbT", [P, 2, 4, P])
        ex = m.sb("ex", [P, 2, 3 * H])
        exk = m.sb("exk", [P, 2, 2 * H])
        gsel = m.sb("gsel", [P, 2, 4])
        dec = m.sb("dec", [P, H, P])
        bT = m.sb("bT", [P, H, P])
        pm = m.sb("pm", [P, 2, H, P])
        inv = m.sb("inv", [P, H, 64])
        invT = m.sb("invT", [P, H, 64])
        join = m.sb("join", [P, H, 64])
        lastT = m.sb("lastT", [P, 2, H, P])
        kd = m.sb("kd", [P, 2, DIM])
        state = m.sb("state", [P, 4, C])
        s1 = m.sb("s1", [P, 4, C])
        r1 = m.sb("r1", [P, DIM])
        r = m.sb("r", [P, DIM])
        dl = m.sb("dl", [P, DIM])
        oq = m.sb("oq", [P, DIM])
        o = m.sb("o", [P, 2, DIM])
        z_ = [m.ps(f"z{n}") for n in range(2)]
        t_ = [m.ps(f"t{n}") for n in range(2)]
        u_ = [m.ps(f"u{n}") for n in range(2)]
        c_ = m.ps("c", [P, 2, 512])
        idx_in = m.moves("idx_in")
        x_in = m.moves("x_in")
        out = m.moves("out")
        levels = range(1, LV - 1)
        LAST = LV - 1
        TP_ = m.steps("pe_prep", "k q sums kb diff0 diff1 kk0 kk1 qk0 qk1 b0 b1 " + " ".join(f"z{v}0 z{v}1 " + f"t{v}0 t{v}1 " + f"u{v}0 u{v}1" for v in levels) + " zlast ulast")
        SP_ = m.steps("act_prep", "kT qT ex dec0 dec1 " + " ".join(f"t{v}0 t{v}1 u{v}0 u{v}1" for v in levels) + " ulast")
        VP_ = m.steps("dve_prep", "kbT exk gselA gselB kd a0 a1 pm0 pm1 u0 u1 t0 t1 " + " ".join(f"j{v}0 j{v}1" for v in levels) + " jlast")
        GP_ = m.steps("pool_prep", "kb gb0 gb1 vb bT0 bT1")
        TC = m.steps("pe_chain", "kq d s o")
        SC = m.steps("act_chain", "d")
        VC = m.steps("dve_chain", "r1 oq r s1 s o")
        init = m.sem("init")

        def place(h):
            return h % 2 * 4 + h // 2

        def by_parity(ap, c=C):
            return ap.rearrange("p (q r c) -> p r q c", r=2, c=c)

        def per_head(ap):
            return ap.rearrange("p (q r) -> p r q", r=2).unsqueeze(3).to_broadcast([P, 2, 4, C])

        def half(tile, n):
            return tile[:, 4 * n:4 * n + 4].rearrange("p h c -> p (h c)")

        def side(tile, s, whole=False):
            rows = slice(64 * s, 64 * s + 64)
            return tile[rows, :, rows] if whole else tile[rows]

        def side_bank(bank, s):
            return bank[64 * s:64 * s + 64].rearrange("p (h c) -> p h c", h=H)

        def side_mask(mask, s):
            rows = slice(64 * s, 64 * s + 64)
            return mask[rows, rows].unsqueeze(1).to_broadcast([64, H, 64])

        def quads(ap):
            return ap.rearrange("p (h c) -> p h c", h=4)

        passed_pool = m.sem("passed_pool")
        passed_pe = m.sem("passed_pe")
        with nc.Block() as block:

            @block.sync
            def _(sp):
                def load(p, i, b):
                    sp.wait_ge(*x_in.after(i, b, 1))
                    sp.dma_start(idx[:, b], d["table"][bass.ds(p * CH, CH), :]).then_inc(*idx_in.done(b))

                def store(c, i, b):
                    sp.wait_ge(*VC.after(c, "o"))
                    sp.dma_start(d["o"][bass.ds(c * CH, CH), :], o[:, b]).then_inc(*out.done(b))

                load(0, 0, 0)
                load(1, 0, 1)
                for i in turns(sp, NCH // 2):
                    for b in range(2):
                        load(i * 2 + 2 + b, i + 1, b)
                        store(i * 2 + b, i, b)
                for b in range(2):
                    sp.wait_ge(*idx_in.after(NCH // 2, b))
                    sp.wait_ge(*out.after(NCH // 2 - 1, b))

            @block.gpsimd
            def _(pool):
                def gather(p, i, b):
                    pool.wait_ge(*idx_in.after(i, b))
                    pool.wait_ge(*TP_.after(p - 2, "sums"))
                    pool.wait_ge(*VP_.after(p - 2, "kd"))
                    pool.wait_ge(*GP_.after(p - 2, "vb"))
                    held(pool, passed_pool)
                    nc.gpsimd.indirect_dma_start(out=x[:, b], out_offset=None, in_=d["token"][:, :], in_offset=bass.IndirectOffsetOnAxis(ap=idx[:, b], axis=0)).then_inc(*x_in.done(b))

                def prepare(p, i, b):
                    pool.wait_ge(*x_in.after(i, b))
                    pool.wait_ge(*TP_.after(p - 1, "kb"))
                    nc.gpsimd.tensor_tensor(heads(kb[:]), heads(x[:, b, TK_K:TK_V]), over_c(x[:, b, TK_NB:TK_G]), ALU.mult).then_inc(*GP_.done("kb"))
                    pool.wait_ge(*TP_.after(p - 1, "diff1"))
                    for n in range(2):
                        g = x[:, b, TK_G:TK_W].rearrange("p (q r) -> p r q", r=2)[:, n]
                        nc.gpsimd.tensor_tensor(gb[:, 4 * n:4 * n + 4], over_h(k["at_or_after"][:], 4), over_c(g, P), ALU.mult).then_inc(*GP_.done(f"gb{n}"))
                    pool.wait_ge(*VC.after(p - 2, "r"))
                    nc.gpsimd.tensor_tensor(heads(vb[:, b]), heads(x[:, b, TK_V:TK_B]), over_c(x[:, b, TK_B:TK_NB]), ALU.mult).then_inc(*GP_.done("vb"))
                    for n in range(2):
                        pool.wait_ge(*VP_.after(p, f"a{n}"))
                        part = bT[:, 4 * n:4 * n + 4]
                        held(pool, passed_pool)
                        nc.gpsimd.affine_select(out=part, in_=part, pattern=[[0, 4], [1, P]], compare_op=ALU.not_equal, fill=1.0, base=0, channel_multiplier=-1).then_inc(*GP_.done(f"bT{n}"))

                give_credit(pool, GP_)
                nc.gpsimd.memset(lastT[:], 0.0)
                nc.gpsimd.memset(state[:], 0.0).then_inc(init, 1)
                gather(0, 0, 0)
                gather(1, 0, 1)
                prepare(0, 0, 0)
                with pool.Fori(0, NCH // 2 - 1) as i:
                    gather(i * 2 + 2, i + 1, 0)
                    prepare(i * 2 + 1, i, 1)
                    gather(i * 2 + 3, i + 1, 1)
                    prepare(i * 2 + 2, i + 1, 0)
                gather(NCH, NCH // 2, 0)
                prepare(NCH - 1, NCH // 2 - 1, 1)
                prepare(NCH, NCH // 2, 0)

            @block.vector
            def _(dve):
                def begin(p, b):
                    dve.wait_ge(*TP_.after(p, "kb"))
                    dve.wait_ge(*TC.after(p - 2, "kq"))
                    nc.vector.tensor_copy(kbT[:, b].rearrange("p h c -> p (h c)"), z_[1][:]).then_inc(*VP_.done("kbT"))

                def decays(p, i, b):
                    dve.wait_ge(*SP_.after(p, "ex"))
                    dve.wait_ge(*TC.after(p - 2, "s"))
                    goes_on = keep["goes_on"][:, bass.ds(p + 1, 1)]
                    nc.vector.tensor_scalar(exk[:, b], ex[:, b, H:3 * H], goes_on, None, ALU.mult).then_inc(*VP_.done("exk"))
                    dve.wait_ge(*VP_.after(p, "exk"))
                    for r0, name in ((0, "gselA"), (1, "gselB")):
                        part = slice(C * r0, C * r0 + C)
                        nc.vector.tensor_copy(gsel[part, b], exk[part, b, H:2 * H].rearrange("p (h r) -> p h r", r=2)[:, :, r0]).then_inc(*VP_.done(name))
                    nc.vector.tensor_tensor(heads(kd[:, b]), heads(x[:, b, TK_K:TK_V]), over_c(exk[:, b, 0:H]), ALU.mult).then_inc(*VP_.done("kd"))

                def grams(p, b):
                    for n in range(2):
                        dve.wait_ge(*TP_.after(p, f"kk{n}"))
                        dve.wait_ge(*SP_.after(p, f"dec{n}"))
                        nc.vector.tensor_tensor(half(bT, n), z_[n][:], half(dec, n), ALU.mult).then_inc(*VP_.done(f"a{n}"))
                    for n in range(2):
                        dve.wait_ge(*TP_.after(p, f"qk{n}"))
                        dve.wait_ge(*TC.after(p - 2, "o"))
                        nc.vector.tensor_tensor(half(pm[:, b], n), t_[n][:], half(dec, n), ALU.mult).then_inc(*VP_.done(f"pm{n}"))
                    dve.wait_ge(*GP_.after(p, "bT1"))
                    dve.wait_ge(*TP_.after(p - 1, f"u{LAST - 1}1"))
                    for s in range(2):
                        nc.vector.tensor_tensor(side(invT, s), side(bT, s, True), side_mask(k["mergeT"], s), ALU.mult).then_inc(*VP_.done(f"u{s}"))
                    for s in range(2):
                        dve.wait_ge(*TP_.after(p, f"b{s}"))
                        nc.vector.tensor_tensor(side(inv, s), side_bank(u_[s], s), side_mask(k["merge"][:, 0], s), ALU.mult).then_inc(*VP_.done(f"t{s}"))

                def level(p, v):
                    for s in range(2):
                        dve.wait_ge(*TP_.after(p, f"z{v}{s}"))
                        nc.vector.tensor_tensor(side(join, s), side_bank(z_[s], s), side_mask(k["merge"][:, v], s), ALU.mult).then_inc(*VP_.done(f"j{v}{s}"))

                def last_level(p):
                    dve.wait_ge(*TP_.after(p, "zlast"))
                    nc.vector.tensor_copy(side(join, 1), side_bank(z_[1], 1)).then_inc(*VP_.done("jlast"))

                def rows(c, b):
                    dve.wait_ge(*TC.after(c, "kq"))
                    nc.vector.tensor_tensor(by_parity(r1[:]), c_[:, :, 0:4 * C].rearrange("p r (q c) -> p r q c", q=4), per_head(ex[:, b, 0:H]), ALU.mult).then_inc(*VC.done("r1"))
                    nc.vector.tensor_tensor(by_parity(oq[:]), c_[:, :, 4 * C:8 * C].rearrange("p r (q c) -> p r q c", q=4), per_head(ex[:, b, 0:H]), ALU.mult).then_inc(*VC.done("oq"))
                    dve.wait_ge(*VC.after(c, "r1"))
                    nc.vector.tensor_tensor(r[:], r1[:], vb[:, b], ALU.add).then_inc(*VC.done("r"))
                    nc.vector.tensor_tensor(s1[:], state[:], over_c(gsel[:, b]), ALU.mult).then_inc(*VC.done("s1"))

                def advance(c, i, b):
                    dve.wait_ge(*TC.after(c, "s"))
                    nc.vector.tensor_tensor(state[:].rearrange("p h c -> p (h c)"), s1[:].rearrange("p h c -> p (h c)"), c_[:, 0, 0:4 * C], ALU.add).then_inc(*VC.done("s"))
                    dve.wait_ge(*TC.after(c, "o"))
                    dve.wait_ge(*out.after(i, b, 1))
                    nc.vector.tensor_tensor(o[:, b], oq[:], c_[:, 1], ALU.add).then_inc(*VC.done("o"))

                def turn(p, ip, bp, c, ic, bc):
                    begin(p, bp)
                    rows(c, bc)
                    decays(p, ip, bp)
                    grams(p, bp)
                    level(p, 1)
                    advance(c, ic, bc)
                    for v in range(2, LAST):
                        level(p, v)
                    last_level(p)

                give_credit(dve, VP_, VC)
                dve.wait_ge(init, 1)
                begin(0, 0)
                decays(0, 0, 0)
                grams(0, 0)
                for v in levels:
                    level(0, v)
                last_level(0)
                for i in turns(dve, NCH // 2):
                    turn(i * 2 + 1, i, 1, i * 2, i, 0)
                    turn(i * 2 + 2, i + 1, 0, i * 2 + 1, i, 1)

            @block.scalar
            def _(act):
                def begin(p, b):
                    act.wait_ge(*TP_.after(p, "k"))
                    act.wait_ge(*TP_.after(p - 1, "qk1"))
                    nc.scalar.copy(kT[:].rearrange("p h c -> p (h c)"), z_[0][:]).then_inc(*SP_.done("kT"))
                    act.wait_ge(*TP_.after(p, "q"))
                    act.wait_ge(*TC.after(p - 2, "kq"))
                    nc.scalar.copy(qT[:, b].rearrange("p h c -> p (h c)"), t_[0][:]).then_inc(*SP_.done("qT"))
                    act.wait_ge(*TP_.after(p, "sums"))
                    act.wait_ge(*VC.after(p - 2, "oq"))
                    nc.scalar.activation(ex[:, b], t_[1][:, 0:3 * H], ACT.Exp).then_inc(*SP_.done("ex"))
                    for n in range(2):
                        act.wait_ge(*TP_.after(p, f"diff{n}"))
                        act.wait_ge(*VP_.after(p - 1, f"pm{n}"))
                        nc.scalar.activation(half(dec, n), u_[n][:], ACT.Exp).then_inc(*SP_.done(f"dec{n}"))

                def level(p, b, v):
                    for s in range(2):
                        act.wait_ge(*TP_.after(p, f"t{v}{s}"))
                        nc.scalar.copy(side(inv, s), side_bank(t_[s], s)).then_inc(*SP_.done(f"t{v}{s}"))
                    if v == LAST - 1:
                        act.wait_ge(*TC.after(p - 2, "d"))
                    for s in range(2):
                        act.wait_ge(*TP_.after(p, f"u{v}{s}"))
                        to = side(invT, s) if v < LAST - 1 else side(lastT[:, b], s, True)
                        nc.scalar.copy(to, side_bank(u_[s], s)).then_inc(*SP_.done(f"u{v}{s}"))

                def last_level(p, b):
                    act.wait_ge(*TP_.after(p, "ulast"))
                    nc.scalar.copy(lastT[0:64, b, :, 64:P], side_bank(u_[0], 0)).then_inc(*SP_.done("ulast"))

                def rows(c):
                    act.wait_ge(*TC.after(c, "d"))
                    nc.scalar.copy(dl[:], c_[:, 0]).then_inc(*SC.done("d"))

                def turn(p, bp, c):
                    begin(p, bp)
                    rows(c)
                    for v in levels:
                        level(p, bp, v)
                    last_level(p, bp)

                give_credit(act, SP_, SC)
                act.wait_ge(init, 1)
                begin(0, 0)
                for v in levels:
                    level(0, 0, v)
                last_level(0, 0)
                with act.Fori(0, NCH // 2) as i:
                    turn(i * 2 + 1, 1, i * 2)
                    turn(i * 2 + 2, 0, i * 2 + 1)

            @block.tensor
            def _(pe):
                def begin(p, i, b):
                    ident = k["ident"][:]
                    pe.wait_ge(*x_in.after(i, b))
                    pe.wait_ge(*VP_.after(p - 1, f"j{LAST - 1}0"))
                    for hp in range(4):
                        last = nc.tensor.transpose(z_[0][:, hp * P:(hp + 1) * P], x[:, b, TK_K + hp * P:TK_K + (hp + 1) * P], ident)
                    last.then_inc(*TP_.done("k"))
                    pe.wait_ge(*SP_.after(p - 1, f"t{LAST - 1}1"))
                    for hp in range(4):
                        last = nc.tensor.transpose(t_[0][:, hp * P:(hp + 1) * P], x[:, b, hp * P:(hp + 1) * P], ident)
                    last.then_inc(*TP_.done("q"))
                    g = x[:, b, TK_G:TK_W]
                    nc.tensor.matmul(t_[1][:, 0:H], k["at_or_after"][:], g, start=True, stop=True)
                    nc.tensor.matmul(t_[1][:, H:2 * H], k["before"][:], g, start=True, stop=True)
                    nc.tensor.matmul(t_[1][:, 2 * H:3 * H], k["ones"][:], g, start=True, stop=True).then_inc(*TP_.done("sums"))
                    pe.wait_ge(*GP_.after(p, "kb"))
                    pe.wait_ge(*VP_.after(p - 1, "jlast"))
                    for hp in range(4):
                        last = nc.tensor.transpose(z_[1][:, hp * P:(hp + 1) * P], kb[:, hp * P:(hp + 1) * P], ident)
                    last.then_inc(*TP_.done("kb"))

                def differences(p):
                    pe.wait_ge(*SP_.after(p - 1, "ulast"))
                    for n in range(2):
                        pe.wait_ge(*GP_.after(p, f"gb{n}"))
                        nc.tensor.matmul(u_[n][:], k["before"][:], half(gb, n), start=True, stop=False)
                        nc.tensor.matmul(quads(u_[n][:]), k["identb"][:], over_h(k["hide"][:], 4), start=False, stop=True).then_inc(*TP_.done(f"diff{n}"))

                def grams(p, b):
                    pe.wait_ge(*SP_.after(p, "kT"))
                    pe.wait_ge(*VP_.after(p, "kbT"))
                    for n in range(2):
                        half_ = slice(C * n, C * n + C)
                        for q in range(4):
                            last = nc.tensor.matmul(z_[n][:, q * P:q * P + P], kT[half_, q], kbT[half_, b, q], start=True, stop=True)
                        last.then_inc(*TP_.done(f"kk{n}"))
                    pe.wait_ge(*SP_.after(p, "ex"))
                    for n in range(2):
                        half_ = slice(C * n, C * n + C)
                        for q in range(4):
                            last = nc.tensor.matmul(t_[n][:, q * P:q * P + P], kT[half_, q], qT[half_, b, q], start=True, stop=True)
                        last.then_inc(*TP_.done(f"qk{n}"))

                def product(name, bank, left, right, s):
                    held(pe, passed_pe)
                    for h in range(H):
                        last = nc.tensor.matmul(bank[s][64 * s:64 * s + 64, h * 64:h * 64 + 64], left[:, h], right[:, h], start=True, stop=True)
                    last.then_inc(*TP_.done(name))

                def first_level(p):
                    pe.wait_ge(*GP_.after(p, "bT1"))
                    pe.wait_ge(*SP_.after(p, "dec1"))
                    for s in range(2):
                        rows = slice(64 * s, 64 * s + 64)
                        product(f"b{s}", u_, side(bT, s, True), k["ident"][rows, rows].unsqueeze(1).to_broadcast([64, H, 64]), s)

                def level(p, v):
                    for s in range(2):
                        if v == 1:
                            pe.wait_ge(*VP_.after(p, f"t{s}"))
                        else:
                            pe.wait_ge(*SP_.after(p, f"t{v - 1}{s}"))
                        product(f"z{v}{s}", z_, side(bT, s, True), side(inv, s), s)
                    for s in range(2):
                        pe.wait_ge(*VP_.after(p, f"j{v}{s}"))
                        if v > 1:
                            pe.wait_ge(*SP_.after(p, f"u{v - 1}{s}"))
                        product(f"t{v}{s}", t_, side(invT, s), side(join, s), s)
                    for s in range(2):
                        product(f"u{v}{s}", u_, side(join, s), side(invT, s), s)

                def last_level(p, b):
                    pe.wait_ge(*SP_.after(p, f"u{LAST - 1}1"))
                    held(pe, passed_pe)
                    for h in range(H):
                        last = nc.tensor.matmul(z_[1][64:P, h * 64:h * 64 + 64], bT[0:64, h, 64:P], inv[0:64, h], start=True, stop=True)
                    last.then_inc(*TP_.done("zlast"))
                    pe.wait_ge(*VP_.after(p, "jlast"))
                    held(pe, passed_pe)
                    for h in range(H):
                        last = nc.tensor.matmul(u_[0][0:64, h * 64:h * 64 + 64], join[64:P, h], lastT[64:P, b, h, 64:P], start=True, stop=True)
                    last.then_inc(*TP_.done("ulast"))

                def apply_state(c, b):
                    pe.wait_ge(*VC.after(c - 1, "o"))
                    for n, left in enumerate((kbT, qT)):
                        for h in range(H):
                            half_ = slice(C * (h % 2), C * (h % 2) + C)
                            last = nc.tensor.matmul(c_[:, h % 2, 4 * C * n + h // 2 * C:4 * C * n + (h // 2 + 1) * C], left[half_, b, h // 2], state[half_, h // 2], start=True, stop=True)
                    last.then_inc(*TC.done("kq"))

                def solve(c, b):
                    pe.wait_ge(*VC.after(c, "r"))
                    pe.wait_ge(*SP_.after(c, "ulast"))
                    for h in range(H):
                        last = nc.tensor.matmul(c_[:, 0, h * C:(h + 1) * C], lastT[:, b, place(h)], r[:, h * C:(h + 1) * C], start=True, stop=True)
                    last.then_inc(*TC.done("d"))

                def update(c, b):
                    pe.wait_ge(*SC.after(c, "d"))
                    for h in range(H):
                        half_ = slice(C * (h % 2), C * (h % 2) + C)
                        last = nc.tensor.matmul(c_[half_, 0, h // 2 * C:(h // 2 + 1) * C], kd[:, b, h * C:(h + 1) * C], dl[:, h * C:(h + 1) * C], start=True, stop=True)
                    last.then_inc(*TC.done("s"))
                    for h in range(H):
                        last = nc.tensor.matmul(c_[:, 1, h * C:(h + 1) * C], pm[:, b, place(h)], dl[:, h * C:(h + 1) * C], start=True, stop=True)
                    last.then_inc(*TC.done("o"))

                def turn(p, ip, bp, c, bc):
                    begin(p, ip, bp)
                    apply_state(c, bc)
                    differences(p)
                    grams(p, bp)
                    solve(c, bc)
                    first_level(p)
                    level(p, 1)
                    update(c, bc)
                    for v in range(2, LAST):
                        level(p, v)
                    last_level(p, bp)

                give_credit(pe, TP_, TC)
                begin(0, 0, 0)
                differences(0)
                grams(0, 0)
                first_level(0)
                for v in levels:
                    level(0, v)
                last_level(0, 0)
                with pe.Fori(0, NCH // 2) as i:
                    turn(i * 2 + 1, i, 1, i * 2, 0)
                    turn(i * 2 + 2, i + 1, 0, i * 2 + 1, 1)


def combine(nc, k, a, d, keep):
    with ExitStack() as ctx:
        m = Mem(nc, ctx, "out")
        w = m.sb("w", [P, KC, DIM])
        onw = m.sb("onw", [P, C])
        col = m.sb("col", [TP, 2, 2, 1], I32)
        og = m.sb("og", [TP, 2, 2, DIM])
        gate = m.sb("gate", [TP, 2, DIM])
        x2 = m.sb("x2", [TP, 2, DIM])
        g2 = m.sb("g2", [TP, 2, DIM])
        c1 = m.sb("c1", [TP, 2, DIM])
        sq = m.sb("sq", [TP, DIM])
        ss = m.sb("ss", [TP, H])
        rn = m.sb("rn", [TP, 2, H])
        xT = m.sb("xT", [P, 2, KC, TP])
        y = m.sb("y", [TP, 2, DIM])
        p_t = [m.ps(f"p_t{b}") for b in range(2)]
        p_y = [m.ps(f"p_y{b}") for b in range(2)]
        weights = m.sem("weights")
        loads = m.moves("loads", 2)
        gathers = m.moves("gathers", 2)
        out = m.moves("out")
        L = m.steps("ahead", "first core ss sseps")
        V = m.steps("vector", "norm gated y")
        G = m.steps("gpsimd", "col0 col1 g2 sq rn")
        S = m.steps("scalar", "xT")
        T = m.steps("tensor", "xT y")
        passed_pool = m.sem("passed_pool")
        with nc.Block() as block:

            @block.sync
            def _(sp):
                sp.dma_start(w[:], a["L0_ffn_Wo"].rearrange("(c p) n -> p c n", p=P)).then_inc(weights, 16)
                sp.dma_start(onw[:], a["L0_ffn_o_norm_weight"].partition_broadcast(P)).then_inc(weights, 16)
                with sp.Fori(0, NT // 2) as i:
                    for b in range(2):
                        t = i * 2 + b
                        rows = bass.ds(t * TP, TP)
                        sp.wait_ge(*G.after(t - 2, "g2"))
                        sp.wait_ge(*V.after(t - 2, "y"))
                        sp.dma_start(gate[:, b], d["gate"][rows, :]).then_inc(*loads.done(b))
                        sp.dma_start(x2[:, b], d["x2"][rows, :]).then_inc(*loads.done(b))

            @block.gpsimd
            def _(pool):
                def gather(t, i, b):
                    pool.wait_ge(*gathers.after(i, b, 1))
                    for s in range(2):
                        nc.gpsimd.tensor_copy(col[:, b, s], keep["slot"][0:TP, s, bass.ds(t, 1)]).then_inc(*G.done(f"col{s}"))
                    pool.wait_ge(*G.after(t, "col1"))
                    pool.wait_ge(*L.after(t - 2, "core"))
                    held(pool, passed_pool)
                    for s in range(2):
                        nc.gpsimd.indirect_dma_start(out=og[:, b, s], out_offset=None, in_=d["o"][:, :], in_offset=bass.IndirectOffsetOnAxis(ap=col[:, b, s], axis=0)).then_inc(*gathers.done(b))

                def work(t, i, b):
                    pool.wait_ge(*loads.after(i, b))
                    pool.wait_ge(*V.after(t - 2, "gated"))
                    nc.gpsimd.tensor_tensor(heads(g2[:, b]), heads(gate[:, b]), over_h(onw[0:TP], H), ALU.mult).then_inc(*G.done("g2"))
                    pool.wait_ge(*L.after(t, "core"))
                    pool.wait_ge(*L.after(t - 1, "ss"))
                    nc.gpsimd.tensor_tensor(sq[:], c1[:, b], c1[:, b], ALU.mult).then_inc(*G.done("sq"))
                    pool.wait_ge(*L.after(t, "sseps"))
                    pool.wait_ge(*V.after(t - 2, "norm"))
                    nc.gpsimd.tensor_tensor(rn[:, b], ss[:], k["minus_half"][0:TP].to_broadcast([TP, H]), ALU.pow).then_inc(*G.done("rn"))

                give_credit(pool, G)
                pool.wait_ge(weights, 32)
                for i in turns(pool, NT // 2):
                    for b in range(2):
                        gather(i * 2 + b, i, b)
                        work(i * 2 + b, i, b)

            @block.vector
            def _(dve):
                def mix(t, i, b):
                    dve.wait_ge(*gathers.after(i, b))
                    dve.wait_ge(*T.after(t - 2, "xT"))
                    nc.vector.tensor_scalar(c1[:, b], og[:, b, 0], keep["slot_weight"][0:TP, 0, bass.ds(t, 1)], None, ALU.mult).then_inc(*L.done("first"))
                    dve.wait_ge(*L.after(t, "first"))
                    nc.vector.scalar_tensor_tensor(c1[:, b], og[:, b, 1], keep["slot_weight"][0:TP, 1, bass.ds(t, 1)], c1[:, b], ALU.mult, ALU.add).then_inc(*L.done("core"))
                    dve.wait_ge(*G.after(t, "sq"))
                    dve.wait_ge(*G.after(t - 1, "rn"))
                    nc.vector.tensor_reduce(ss[:], heads(sq[:]), AX.X, ALU.add).then_inc(*L.done("ss"))
                    dve.wait_ge(*L.after(t, "ss"))
                    nc.vector.tensor_scalar(ss[:], ss[:], 1.0 / C, LN_EPS, ALU.mult, ALU.add).then_inc(*L.done("sseps"))

                def gated(t, i, b):
                    dve.wait_ge(*G.after(t, "rn"))
                    nc.vector.tensor_tensor(heads(c1[:, b]), heads(c1[:, b]), over_c(rn[:, b]), ALU.mult).then_inc(*V.done("norm"))
                    dve.wait_ge(*V.after(t, "norm"))
                    nc.vector.tensor_tensor(c1[:, b], c1[:, b], g2[:, b], ALU.mult).then_inc(*V.done("gated"))
                    dve.wait_ge(*T.after(t, "y"))
                    dve.wait_ge(*loads.after(i, b))
                    dve.wait_ge(*out.after(i, b, 1))
                    nc.vector.tensor_tensor(y[:, b], p_y[b][0:TP, :], x2[:, b], ALU.add).then_inc(*V.done("y"))

                give_credit(dve, V, L)
                for i in turns(dve, NT // 2):
                    for b in range(2):
                        mix(i * 2 + b, i, b)
                        gated(i * 2 + b, i, b)

            @block.tensor
            def _(pe):
                give_credit(pe, T)
                pe.wait_ge(weights, 32)
                with pe.Fori(0, NT // 2) as i:
                    for b in range(2):
                        t = i * 2 + b
                        pe.wait_ge(*V.after(t, "gated"))
                        pe.wait_ge(*S.after(t - 2, "xT"))
                        for c in range(KC):
                            last = nc.tensor.transpose(p_t[b][:, c * TP:(c + 1) * TP], c1[:, b, c * P:(c + 1) * P], k["ident"][0:TP, 0:TP])
                        last.then_inc(*T.done("xT"))
                        pe.wait_ge(*S.after(t, "xT"))
                        pe.wait_ge(*V.after(t - 2, "y"))
                        for c in range(KC):
                            last = nc.tensor.matmul(p_y[b][0:TP, :], xT[:, b, c], w[:, c], start=c == 0, stop=c == KC - 1)
                        last.then_inc(*T.done("y"))

            @block.scalar
            def _(act):
                give_credit(act, S)
                with act.Fori(0, NT // 2) as i:
                    for b in range(2):
                        t = i * 2 + b
                        act.wait_ge(*T.after(t, "xT"))
                        act.wait_ge(*T.after(t - 2, "y"))
                        nc.scalar.copy(xT[:, b].rearrange("p c t -> p (c t)"), p_t[b][:, 0:KC * TP]).then_inc(*S.done("xT"))
                        act.wait_ge(*V.after(t, "y"))
                        act.dma_start(a["out"][bass.ds(t * TP, TP), :], y[:, b]).then_inc(*out.done(b))
                for b in range(2):
                    act.wait_ge(*out.after(NT // 2 - 1, b))


def build(nc, a):
    def table(name, shape, dt=F32):
        return nc.dram_tensor(name, shape, dt, kind="Internal").ap()

    d = {
        "source": table("source", (N, SRC_W)), "state": table("state", (N + P, ST_W)),
        "skip": table("skip", (N, DIM)), "gat": table("gat", (N, DIM)), "x2": table("x2", (N, DIM)),
        "token": table("token", (N, TK_W)), "gate": table("gate", (N, DIM)),
        "table": table("table", (SLOTS + 2 * CH, 1), I32), "o": table("o", (SLOTS, DIM)),
    }
    with ExitStack() as ctx:
        m = Mem(nc, ctx, "all")
        k = constants(nc, m)
        keep = {
            "bn_scale": m.sb("bn_scale", [P, DIM]), "bn_shift": m.sb("bn_shift", [P, DIM]),
            "weight": m.sb("weight", [P, NE, NT]),
            "slot": m.sb("slot", [P, 2, NT], I32), "slot_weight": m.sb("slot_weight", [P, 2, NT]),
            "goes_on": m.sb("goes_on", [P, NCH + 2]),
        }
        project_nodes(nc, k, a, d)
        send_messages(nc, k, a, d)
        batch_norm(nc, k, a, d, keep)
        project_tokens(nc, k, a, d, keep)
        route(nc, k, a, d, keep)
        delta_rule(nc, k, a, d, keep)
        combine(nc, k, a, d, keep)


INS = {
    "x": (N, DIM), "src": (N,), "dst": (N,),
    "L0_gnn_W_gat": (DIM, DIM), "L0_gnn_att_src": (H, C), "L0_gnn_att_dst": (H, C), "L0_gnn_gat_bias": (DIM,),
    "L0_gnn_bn_gamma": (DIM,), "L0_gnn_bn_beta": (DIM,), "L0_gnn_W_skip": (DIM, DIM), "L0_gnn_b_skip": (DIM,),
    "L0_ffn_Wq": (DIM, DIM), "L0_ffn_Wgate": (DIM, NE), "L0_ffn_Wk": (DIM, DIM), "L0_ffn_Wv": (DIM, DIM),
    "L0_ffn_Wb": (DIM, H), "L0_ffn_Wa": (DIM, H), "L0_ffn_A_log": (H,), "L0_ffn_dt_bias": (H,),
    "L0_ffn_Wg": (DIM, DIM), "L0_ffn_o_norm_weight": (C,), "L0_ffn_Wo": (DIM, DIM),
}


def kernel(**inputs):
    import numpy as np
    import concourse.bacc as bacc
    from concourse.bass_utils import run_bass_kernel_spmd

    nc = bacc.Bacc("TRN2", target_bir_lowering=False, num_devices=1)
    a, arrays = {}, {}
    for name, shape in INS.items():
        arrays[name] = np.ascontiguousarray(inputs[name])
        a[name] = nc.dram_tensor(name, shape, I32 if name in ("src", "dst") else F32, kind="ExternalInput").ap()
    a["out"] = nc.dram_tensor("out", (N, DIM), F32, kind="ExternalOutput").ap()
    build(nc, a)
    r = run_bass_kernel_spmd(nc, [arrays], core_ids=[0])
    return r.results[0]["out"]
```

```python
import concourse.bass as bass
from concourse import mybir
from contextlib import ExitStack

F32 = mybir.dt.float32
BF16 = mybir.dt.bfloat16
I32 = mybir.dt.int32
ALU = mybir.AluOpType
ACT = mybir.ActivationFunctionType
AX = mybir.AxisListType

N = 10000
DIM = 512
H = 8
C = DIM // H
TP = 125
NT = N // TP
KC = DIM // 128
P = 128
NE = 4
CH = 128
NCH = 2 * N // CH + NE
SLOTS = NCH * CH
NEG_SLOPE = 0.2
BN_EPS = 1e-5
LN_EPS = 1e-5
FAR = 1e30
G_FLOOR = -104.0

ST_DEN, ST_MAX, ST_DST, ST_W = DIM, DIM + H, DIM + 2 * H, DIM + 3 * H
SRC_W = H + DIM
TK_K, TK_V, TK_B, TK_NB, TK_G = DIM, 2 * DIM, 3 * DIM, 3 * DIM + H, 3 * DIM + 2 * H
TK_W = 3 * DIM + 3 * H


class Steps:

    def __init__(self, sem, names, lag=2):
        self.sem, self.names, self.lag, self.written = sem, names.split(), lag, 0
        assert len(set(self.names)) == len(self.names)

    @property
    def credit(self):
        return self.lag * len(self.names)

    def after(self, turn, name):
        k = len(self.names)
        return self.sem, (turn + self.lag) * k + self.names.index(name) + 1

    def done(self, name):
        assert name == self.names[self.written % len(self.names)], name
        self.written += 1
        return self.sem, 1


class Moves:

    def __init__(self, sems, each=1):
        self.sems, self.each = sems, each

    def after(self, pair, buf, back=0):
        return self.sems[buf], (pair + 1 - back) * 16 * self.each

    def done(self, buf):
        return self.sems[buf], 16


class Mem:

    def __init__(self, nc, ctx, tag):
        self.nc, self.ctx, self.tag = nc, ctx, tag

    def sb(self, name, shape, dt=F32):
        return self.ctx.enter_context(self.nc.sbuf_tensor(f"{self.tag}_{name}", shape, dt))

    def ps(self, name, shape=(P, 512), dt=F32):
        return self.ctx.enter_context(self.nc.psum_tensor(f"{self.tag}_{name}", list(shape), dt))

    def sem(self, name):
        return self.ctx.enter_context(self.nc.semaphore(f"{self.tag}_{name}"))

    def steps(self, name, names):
        return Steps(self.sem(name), names)

    def moves(self, name, each=1):
        return Moves([self.sem(f"{name}{b}") for b in range(2)], each)


def give_credit(eng, *counts):
    for c in counts:
        eng.sem_inc(c.sem, c.credit)


def turns(eng, n):
    yield 0
    with eng.Fori(1, n) as i:
        yield i


def held(eng, passed):
    eng.sem_inc(passed, 1)


def heads(ap, n=H):
    return ap.rearrange("p (h c) -> p h c", h=n)


def over_c(ap, c=C):
    return ap.unsqueeze(2).to_broadcast([ap.shape[0], ap.shape[1], c])


def over_h(ap, n):
    return ap.unsqueeze(1).to_broadcast([ap.shape[0], n, ap.shape[1]])


def constants(nc, m):
    k = {
        "ident": m.sb("ident", [P, P]),
        "identb": m.sb("identb", [P, P], BF16),
        "at_or_after": m.sb("at_or_after", [P, P]),
        "before": m.sb("before", [P, P]),
        "after": m.sb("after", [P, P]),
        "hide": m.sb("hide", [P, P], BF16),
        "ones": m.sb("ones", [P, P]),
        "minus_half": m.sb("minus_half", [P, 1]),
        "zeros": m.sb("zeros", [P, ST_W]),
        "merge": m.sb("merge", [P, 7, P]),
        "mergeT": m.sb("mergeT", [P, P]),
        "merge_half": m.sb("merge_half", [P, 6, 64]),
        "mergeT_half": m.sb("mergeT_half", [P, 64]),
        "dump": m.sb("dump", [P, 1]),
        "dumpslot": m.sb("dumpslot", [P, 1]),
        "chunk_no": m.sb("chunk_no", [P, NCH + 4]),
    }
    made = m.sem("constants_made")
    with nc.Block() as block:

        @block.gpsimd
        def _(pool):
            step = [0]

            def then(ins):
                step[0] += 1
                ins.then_inc(made, 1)
                pool.wait_ge(made, step[0])

            for name in ("ident", "at_or_after", "before", "after", "ones"):
                nc.gpsimd.memset(k[name][:], 1.0)
            nc.gpsimd.memset(k["minus_half"][:], -0.5)
            nc.gpsimd.memset(k["hide"][:], 0.0)
            nc.gpsimd.memset(k["merge"][:], 0.0)
            nc.gpsimd.memset(k["mergeT"][:], 0.0)
            then(nc.gpsimd.memset(k["zeros"][:], 0.0))
            row = [[1, P]]
            nc.gpsimd.affine_select(out=k["ident"][:], in_=k["ident"][:], pattern=row, compare_op=ALU.is_equal, fill=0.0, base=0, channel_multiplier=-1)
            nc.gpsimd.affine_select(out=k["at_or_after"][:], in_=k["at_or_after"][:], pattern=row, compare_op=ALU.is_ge, fill=0.0, base=0, channel_multiplier=-1)
            nc.gpsimd.affine_select(out=k["after"][:], in_=k["after"][:], pattern=row, compare_op=ALU.is_gt, fill=0.0, base=0, channel_multiplier=-1)
            nc.gpsimd.affine_select(out=k["hide"][:], in_=k["hide"][:], pattern=row, compare_op=ALU.is_ge, fill=-30000.0, base=0, channel_multiplier=-1)
            nc.gpsimd.iota(k["dump"][:], [[0, 1]], base=N, channel_multiplier=1, allow_small_or_imprecise_dtypes=True)
            nc.gpsimd.iota(k["dumpslot"][:], [[0, 1]], base=SLOTS, channel_multiplier=1, allow_small_or_imprecise_dtypes=True)
            nc.gpsimd.iota(k["chunk_no"][:], [[1, NCH + 4]], base=0, channel_multiplier=0, allow_small_or_imprecise_dtypes=True)
            then(nc.gpsimd.affine_select(out=k["before"][:], in_=k["before"][:], pattern=[[-1, P]], compare_op=ALU.is_gt, fill=0.0, base=0, channel_multiplier=1))
            then(nc.gpsimd.tensor_copy(k["identb"][:], k["ident"][:]))
            for lv in range(7):
                b = 1 << lv
                cols = k["merge"][:, lv, :].rearrange("p (m r) -> p m r", r=2 * b)[:, :, 0:b]
                pairs = P // (2 * b)
                then(nc.gpsimd.memset(cols, 1.0))
                then(nc.gpsimd.affine_select(out=cols, in_=cols, pattern=[[-2 * b, pairs], [0, b]], compare_op=ALU.is_ge, fill=0.0, base=-b, channel_multiplier=1))
                then(nc.gpsimd.affine_select(out=cols, in_=cols, pattern=[[2 * b, pairs], [0, b]], compare_op=ALU.is_ge, fill=0.0, base=2 * b - 1, channel_multiplier=-1))
                then(nc.gpsimd.tensor_tensor(k["merge"][:, lv, :], k["merge"][:, lv, :], k["ident"][:], ALU.add))
            oddcols = k["mergeT"][:].rearrange("p (m r) -> p m r", r=2)[:, :, 1:2]
            then(nc.gpsimd.memset(oddcols, 1.0))
            then(nc.gpsimd.affine_select(out=oddcols, in_=oddcols, pattern=[[2, P // 2], [0, 1]], compare_op=ALU.is_equal, fill=0.0, base=0, channel_multiplier=-1))
            then(nc.gpsimd.tensor_tensor(k["mergeT"][:], k["mergeT"][:], k["ident"][:], ALU.add))
            for s in range(2):
                rows = slice(64 * s, 64 * s + 64)
                then(nc.gpsimd.tensor_copy(k["merge_half"][rows], k["merge"][rows, 0:6, rows]))
                then(nc.gpsimd.tensor_copy(k["mergeT_half"][rows], k["mergeT"][rows, rows]))
    return k


def project_nodes(nc, k, a, d):
    with ExitStack() as ctx:
        m = Mem(nc, ctx, "nodes")
        w = m.sb("w", [P, 2, KC, DIM])
        att = m.sb("att", [P, 2, DIM])
        bskip = m.sb("bskip", [P, DIM])
        x = m.sb("x", [TP, 2, DIM])
        xn = m.sb("xn", [TP, 2, DIM])
        xT = m.sb("xT", [P, 2, KC, TP])
        row = m.sb("row", [TP, 2, H + ST_W])
        skip = m.sb("skip", [TP, 2, DIM])
        prod = m.sb("prod", [TP, 2, DIM])
        stats = m.sb("stats", [TP, 2, 6])
        mv = m.sb("mv", [TP, 2, 2])
        veps = m.sb("veps", [TP, 2, 1])
        rstd = m.sb("rstd", [TP, 2, 1])
        asum = m.sb("asum", [TP, 2, H])
        p_t = [m.ps(f"p_t{b}") for b in range(2)]
        p_h = [m.ps(f"p_h{b}") for b in range(2)]
        p_s = [m.ps(f"p_s{b}") for b in range(2)]
        weights = m.sem("weights")
        x_in = m.moves("x_in")
        out = m.moves("out", 3)
        unused = m.sem("unused")
        LN = m.steps("norm", "stats aggr xn")
        V = m.steps("vector", "skip psrc pdst asrc adst den sum max")
        G = m.steps("gpsimd", "veps rstd")
        S = m.steps("scalar", "xT h")
        T = m.steps("tensor", "xT h skip")
        passed_dve = m.sem("passed_dve")
        passed_pool = m.sem("passed_pool")
        with nc.Block() as block:

            @block.sync
            def _(sp):
                sp.dma_start(w[:, 0], a["L0_gnn_W_gat"].rearrange("(c p) n -> p c n", p=P)).then_inc(weights, 16)
                sp.dma_start(w[:, 1], a["L0_gnn_W_skip"].rearrange("(c p) n -> p c n", p=P)).then_inc(weights, 16)
                sp.dma_start(att[:, 0], a["L0_gnn_att_src"].rearrange("h c -> (h c)").partition_broadcast(P)).then_inc(weights, 16)
                sp.dma_start(att[:, 1], a["L0_gnn_att_dst"].rearrange("h c -> (h c)").partition_broadcast(P)).then_inc(weights, 16)
                sp.dma_start(bskip[:], a["L0_gnn_b_skip"].partition_broadcast(P)).then_inc(weights, 16)
                with sp.Fori(0, NT // 2) as i:
                    for b in range(2):
                        t = i * 2 + b
                        sp.wait_ge(*LN.after(t - 2, "xn"))
                        sp.dma_start(x[:, b], a["x"][bass.ds(t * TP, TP), :]).then_inc(*x_in.done(b))
                sp.dma_start(d["state"][N:N + P, :], k["zeros"][:]).then_inc(unused, 16)
                sp.wait_ge(unused, 16)

            def norm(t, i, b, dve):
                dve.wait_ge(*x_in.after(i, b))
                nc.vector.bn_stats(stats[:, b], x[:, b]).then_inc(*LN.done("stats"))
                dve.wait_ge(*LN.after(t, "stats"))
                held(dve, passed_dve)
                nc.vector.bn_aggr(mv[:, b], stats[:, b]).then_inc(*LN.done("aggr"))
                dve.wait_ge(*G.after(t, "rstd"))
                dve.wait_ge(*T.after(t - 2, "xT"))
                nc.vector.tensor_scalar(xn[:, b], x[:, b], mv[:, b, 0:1], rstd[:, b], ALU.subtract, ALU.mult).then_inc(*LN.done("xn"))

            def scores(t, i, b, dve):
                dve.wait_ge(*T.after(t, "skip"))
                dve.wait_ge(*out.after(i, b, 1))
                nc.vector.tensor_tensor(skip[:, b], p_s[b][0:TP, :], bskip[0:TP, :], ALU.add).then_inc(*V.done("skip"))
                dve.wait_ge(*S.after(t, "h"))
                nc.vector.tensor_tensor(prod[:, 0], row[:, b, H:H + DIM], att[0:TP, 0], ALU.mult).then_inc(*V.done("psrc"))
                nc.vector.tensor_tensor(prod[:, 1], row[:, b, H:H + DIM], att[0:TP, 1], ALU.mult).then_inc(*V.done("pdst"))
                dve.wait_ge(*V.after(t, "psrc"))
                nc.vector.tensor_reduce(row[:, b, 0:H], heads(prod[:, 0]), AX.X, ALU.add).then_inc(*V.done("asrc"))
                dve.wait_ge(*V.after(t, "pdst"))
                nc.vector.tensor_reduce(row[:, b, H + ST_DST:H + ST_W], heads(prod[:, 1]), AX.X, ALU.add).then_inc(*V.done("adst"))
                nc.vector.memset(row[:, b, H + ST_DEN:H + ST_MAX], 1.0).then_inc(*V.done("den"))
                dve.wait_ge(*V.after(t, "adst"))
                nc.vector.tensor_tensor(asum[:, b], row[:, b, 0:H], row[:, b, H + ST_DST:H + ST_W], ALU.add).then_inc(*V.done("sum"))
                dve.wait_ge(*V.after(t, "sum"))
                nc.vector.scalar_tensor_tensor(row[:, b, H + ST_MAX:H + ST_DST], asum[:, b], NEG_SLOPE, asum[:, b], ALU.mult, ALU.max).then_inc(*V.done("max"))

            @block.vector
            def _(dve):
                give_credit(dve, V, LN)
                dve.wait_ge(weights, 80)
                norm(0, 0, 0, dve)
                for i in turns(dve, NT // 2 - 1):
                    norm(i * 2 + 1, i, 1, dve)
                    scores(i * 2, i, 0, dve)
                    norm(i * 2 + 2, i + 1, 0, dve)
                    scores(i * 2 + 1, i, 1, dve)
                norm(NT - 1, NT // 2 - 1, 1, dve)
                scores(NT - 2, NT // 2 - 1, 0, dve)
                scores(NT - 1, NT // 2 - 1, 1, dve)

            @block.tensor
            def _(pe):
                give_credit(pe, T)
                pe.wait_ge(weights, 80)
                with pe.Fori(0, NT // 2) as i:
                    for b in range(2):
                        t = i * 2 + b
                        pe.wait_ge(*LN.after(t, "xn"))
                        pe.wait_ge(*S.after(t - 2, "xT"))
                        for c in range(KC):
                            last = nc.tensor.transpose(p_t[b][:, c * TP:(c + 1) * TP], xn[:, b, c * P:(c + 1) * P], k["ident"][0:TP, 0:TP])
                        last.then_inc(*T.done("xT"))
                        pe.wait_ge(*S.after(t, "xT"))
                        pe.wait_ge(*S.after(t - 2, "h"))
                        for c in range(KC):
                            last = nc.tensor.matmul(p_h[b][0:TP, :], xT[:, b, c], w[:, 0, c], start=c == 0, stop=c == KC - 1)
                        last.then_inc(*T.done("h"))
                        pe.wait_ge(*V.after(t - 2, "skip"))
                        for c in range(KC):
                            last = nc.tensor.matmul(p_s[b][0:TP, :], xT[:, b, c], w[:, 1, c], start=c == 0, stop=c == KC - 1)
                        last.then_inc(*T.done("skip"))

            @block.scalar
            def _(act):
                give_credit(act, S)
                for i in turns(act, NT // 2):
                    for b in range(2):
                        t = i * 2 + b
                        act.wait_ge(*T.after(t, "xT"))
                        act.wait_ge(*T.after(t - 2, "skip"))
                        nc.scalar.copy(xT[:, b].rearrange("p c t -> p (c t)"), p_t[b][:, 0:KC * TP]).then_inc(*S.done("xT"))
                        act.wait_ge(*T.after(t, "h"))
                        act.wait_ge(*out.after(i, b, 1))
                        act.wait_ge(*V.after(t - 2, "pdst"))
                        nc.scalar.copy(row[:, b, H:H + DIM], p_h[b][0:TP, :]).then_inc(*S.done("h"))

            def root(t, b, pool):
                pool.wait_ge(*LN.after(t, "aggr"))
                held(pool, passed_pool)
                nc.gpsimd.tensor_scalar(veps[:, b], mv[:, b, 1:2], LN_EPS, None, ALU.add).then_inc(*G.done("veps"))
                pool.wait_ge(*G.after(t, "veps"))
                pool.wait_ge(*LN.after(t - 2, "xn"))
                nc.gpsimd.tensor_tensor(rstd[:, b], veps[:, b], k["minus_half"][0:TP, 0:1], ALU.pow).then_inc(*G.done("rstd"))

            def store(t, b, pool):
                pool.wait_ge(*V.after(t, "max"))
                rows = bass.ds(t * TP, TP)
                pool.dma_start(d["source"][rows, :], row[:, b, 0:SRC_W]).then_inc(*out.done(b))
                pool.dma_start(d["state"][rows, :], row[:, b, H:H + ST_W]).then_inc(*out.done(b))
                pool.dma_start(d["skip"][rows, :], skip[:, b]).then_inc(*out.done(b))

            @block.gpsimd
            def _(pool):
                give_credit(pool, G)
                root(0, 0, pool)
                with pool.Fori(0, NT // 2 - 1) as i:
                    root(i * 2 + 1, 1, pool)
                    store(i * 2, 0, pool)
                    root(i * 2 + 2, 0, pool)
                    store(i * 2 + 1, 1, pool)
                root(NT - 1, 1, pool)
                store(NT - 2, 0, pool)
                store(NT - 1, 1, pool)
                for b in range(2):
                    pool.wait_ge(*out.after(NT // 2 - 1, b))


def send_messages(nc, k, a, d):
    with ExitStack() as ctx:
        m = Mem(nc, ctx, "edges")
        src = m.sb("src", [TP, 2, 1], I32)
        dst = m.sb("dst", [TP, 2, 1], I32)
        dstrow = m.sb("dstrow", [TP, 2, TP], I32)
        dstf = m.sb("dstf", [TP, 2, 1])
        same = m.sb("same", [TP, 2, TP])
        far = m.sb("far", [TP, TP])
        earlier = m.sb("earlier", [TP, TP])
        dup = m.sb("dup", [TP, 1])
        first = m.sb("first", [TP, 1])
        off = m.sb("off", [TP, 1])
        target = m.sb("target", [TP, 2, 1], I32)
        hs = m.sb("hs", [TP, 2, SRC_W])
        st = m.sb("st", [TP, ST_W])
        new = m.sb("new", [TP, ST_W])
        e0 = m.sb("e0", [TP, H])
        e = m.sb("e", [TP, H])
        ebig = m.sb("ebig", [TP, H, TP])
        tmax = m.sb("tmax", [TP, H])
        diff = m.sb("diff", [TP, 2, H])
        scale = m.sb("scale", [TP, H])
        pay = m.sb("pay", [TP, DIM + H])
        p_e = m.ps("p_e", [P, 2, 512])
        p_m = m.ps("p_m", [P, 2, 512])
        idx_in = m.moves("idx_in", 3)
        hs_in = m.moves("hs_in")
        st_in = m.moves("st_in")
        st_out = m.moves("st_out")
        V = m.steps("vector", "dstf same far earlier dup first off target e0 e ebig tmax max dnew dold pay adst acc den acc2 den2")
        S = m.steps("scalar", "ex scale")
        T = m.steps("tensor", "e sum")
        passed_pool = m.sem("passed_pool")
        passed_sp = m.sem("passed_sp")
        with nc.Block() as block:

            @block.sync
            def _(sp):
                for i in turns(sp, NT // 2):
                    for b in range(2):
                        t = i * 2 + b
                        sp.wait_ge(*V.after(t - 2, "target"))
                        held(sp, passed_sp)
                        sp.wait_ge(*hs_in.after(i, b, 1))
                        sp.wait_ge(*st_in.after(i, b, 1))
                        sp.dma_start(src[:, b], a["src"][bass.ds(t * TP, TP)].unsqueeze(1)).then_inc(*idx_in.done(b))
                        sp.dma_start(dst[:, b], a["dst"][bass.ds(t * TP, TP)].unsqueeze(1)).then_inc(*idx_in.done(b))
                        sp.dma_start(dstrow[:, b], a["dst"][bass.ds(t * TP, TP)].partition_broadcast(TP)).then_inc(*idx_in.done(b))

            @block.gpsimd
            def _(pool):
                for i in turns(pool, NT // 2):
                    for b in range(2):
                        t = i * 2 + b
                        pool.wait_ge(*idx_in.after(i, b))
                        pool.wait_ge(*V.after(t - 2, "pay"))
                        held(pool, passed_pool)
                        nc.gpsimd.indirect_dma_start(out=hs[:, b], out_offset=None, in_=d["source"][:, :], in_offset=bass.IndirectOffsetOnAxis(ap=src[:, b], axis=0)).then_inc(*hs_in.done(b))
                        pool.wait_ge(*(st_out.after(i, 0) if b else st_out.after(i, 1, 1)))
                        pool.wait_ge(*V.after(t - 1, "den"))
                        held(pool, passed_pool)
                        nc.gpsimd.indirect_dma_start(out=st[:], out_offset=None, in_=d["state"][:, :], in_offset=bass.IndirectOffsetOnAxis(ap=dst[:, b], axis=0)).then_inc(*st_in.done(b))
                        pool.wait_ge(*V.after(t, "den2"))
                        held(pool, passed_pool)
                        nc.gpsimd.indirect_dma_start(out=d["state"][:, :], out_offset=bass.IndirectOffsetOnAxis(ap=target[:, b], axis=0), in_=new[:], in_offset=None).then_inc(*st_out.done(b))
                for b in range(2):
                    pool.wait_ge(*st_out.after(NT // 2 - 1, b))

            @block.vector
            def _(dve):
                give_credit(dve, V)
                for i in turns(dve, NT // 2):
                    for b in range(2):
                        t = i * 2 + b
                        dve.wait_ge(*idx_in.after(i, b))
                        nc.vector.tensor_copy(dstf[:, b], dst[:, b]).then_inc(*V.done("dstf"))
                        dve.wait_ge(*V.after(t, "dstf"))
                        dve.wait_ge(*T.after(t - 2, "sum"))
                        nc.vector.tensor_scalar(same[:, b], dstrow[:, b], dstf[:, b], None, ALU.is_equal).then_inc(*V.done("same"))
                        dve.wait_ge(*V.after(t, "same"))
                        nc.vector.tensor_scalar(far[:], same[:, b], FAR, -FAR, ALU.mult, ALU.add).then_inc(*V.done("far"))
                        nc.vector.tensor_tensor(earlier[:], same[:, b], k["before"][0:TP, 0:TP], ALU.mult).then_inc(*V.done("earlier"))
                        dve.wait_ge(*V.after(t, "earlier"))
                        nc.vector.reduce_sum(dup[:], earlier[:], AX.X).then_inc(*V.done("dup"))
                        dve.wait_ge(*V.after(t, "dup"))
                        nc.vector.tensor_scalar(first[:], dup[:], 0.0, None, ALU.is_equal).then_inc(*V.done("first"))
                        nc.vector.tensor_tensor(off[:], dstf[:, b], k["dump"][0:TP], ALU.subtract).then_inc(*V.done("off"))
                        dve.wait_ge(*V.after(t, "off"))
                        dve.wait_ge(*st_out.after(i, b, 1))
                        nc.vector.scalar_tensor_tensor(target[:, b], off[:], first[:], k["dump"][0:TP], ALU.mult, ALU.add).then_inc(*V.done("target"))
                        dve.wait_ge(*hs_in.after(i, b))
                        dve.wait_ge(*st_in.after(i, b))
                        nc.vector.tensor_tensor(e0[:], hs[:, b, 0:H], st[:, ST_DST:ST_W], ALU.add).then_inc(*V.done("e0"))
                        dve.wait_ge(*V.after(t, "e0"))
                        nc.vector.scalar_tensor_tensor(e[:], e0[:], NEG_SLOPE, e0[:], ALU.mult, ALU.max).then_inc(*V.done("e"))
                        dve.wait_ge(*T.after(t, "e"))
                        nc.vector.tensor_tensor(ebig[:].rearrange("p (g h) j -> p g h j", g=2),
                                                p_e[0:TP, :, 0:4 * TP].rearrange("p g (h j) -> p g h j", h=4),
                                                far[:].unsqueeze(1).unsqueeze(1).to_broadcast([TP, 2, 4, TP]), ALU.add).then_inc(*V.done("ebig"))
                        dve.wait_ge(*V.after(t, "ebig"))
                        nc.vector.tensor_reduce(tmax[:], ebig[:], AX.X, ALU.max).then_inc(*V.done("tmax"))
                        dve.wait_ge(*V.after(t, "tmax"))
                        dve.wait_ge(*(st_out.after(i, 0) if b else st_out.after(i, 1, 1)))
                        nc.vector.tensor_tensor(new[:, ST_MAX:ST_DST], st[:, ST_MAX:ST_DST], tmax[:], ALU.max).then_inc(*V.done("max"))
                        dve.wait_ge(*V.after(t, "max"))
                        dve.wait_ge(*S.after(t - 1, "scale"))
                        nc.vector.tensor_tensor(diff[:, 0], e[:], new[:, ST_MAX:ST_DST], ALU.subtract).then_inc(*V.done("dnew"))
                        nc.vector.tensor_tensor(diff[:, 1], st[:, ST_MAX:ST_DST], new[:, ST_MAX:ST_DST], ALU.subtract).then_inc(*V.done("dold"))
                        dve.wait_ge(*S.after(t, "ex"))
                        nc.vector.tensor_tensor(heads(pay[:, 0:DIM]), heads(hs[:, b, H:SRC_W]), over_c(pay[:, DIM:DIM + H]), ALU.mult).then_inc(*V.done("pay"))
                        nc.vector.tensor_copy(new[:, ST_DST:ST_W], st[:, ST_DST:ST_W]).then_inc(*V.done("adst"))
                        dve.wait_ge(*S.after(t, "scale"))
                        nc.vector.tensor_tensor(heads(new[:, 0:DIM]), heads(st[:, 0:DIM]), over_c(scale[:]), ALU.mult).then_inc(*V.done("acc"))
                        nc.vector.tensor_tensor(new[:, ST_DEN:ST_MAX], st[:, ST_DEN:ST_MAX], scale[:], ALU.mult).then_inc(*V.done("den"))
                        dve.wait_ge(*T.after(t, "sum"))
                        dve.wait_ge(*V.after(t, "den"))
                        nc.vector.tensor_tensor(new[:, 0:DIM], new[:, 0:DIM], p_m[0:TP, 0, :], ALU.add).then_inc(*V.done("acc2"))
                        nc.vector.tensor_tensor(new[:, ST_DEN:ST_MAX], new[:, ST_DEN:ST_MAX], p_m[0:TP, 1, 0:H], ALU.add).then_inc(*V.done("den2"))

            @block.scalar
            def _(act):
                give_credit(act, S)
                with act.Fori(0, NT // 2) as i:
                    for b in range(2):
                        t = i * 2 + b
                        act.wait_ge(*V.after(t, "dold"))
                        act.wait_ge(*T.after(t - 1, "sum"))
                        nc.scalar.activation(pay[:, DIM:DIM + H], diff[:, 0], ACT.Exp).then_inc(*S.done("ex"))
                        act.wait_ge(*V.after(t - 1, "den"))
                        nc.scalar.activation(scale[:], diff[:, 1], ACT.Exp).then_inc(*S.done("scale"))

            @block.tensor
            def _(pe):
                give_credit(pe, T)
                with pe.Fori(0, NT // 2) as i:
                    for b in range(2):
                        t = i * 2 + b
                        pe.wait_ge(*V.after(t, "e"))
                        pe.wait_ge(*V.after(t - 1, "ebig"))
                        for h in range(H):
                            last = nc.tensor.matmul(p_e[0:TP, h // 4, (h % 4) * TP:(h % 4 + 1) * TP], e[:, h:h + 1].to_broadcast([TP, TP]),
                                                    k["ident"][0:TP, 0:TP], start=True, stop=True)
                        last.then_inc(*T.done("e"))
                        pe.wait_ge(*V.after(t, "pay"))
                        pe.wait_ge(*V.after(t - 1, "den2"))
                        nc.tensor.matmul(p_m[0:TP, 0, :], same[:, b], pay[:, 0:DIM], start=True, stop=True)
                        nc.tensor.matmul(p_m[0:TP, 1, 0:H], same[:, b], pay[:, DIM:DIM + H], start=True, stop=True).then_inc(*T.done("sum"))


def batch_norm(nc, k, a, d, keep):
    with ExitStack() as ctx:
        m = Mem(nc, ctx, "bn")
        bias = m.sb("bias", [P, DIM])
        gamma = m.sb("gamma", [P, DIM])
        beta = m.sb("beta", [P, DIM])
        st = m.sb("st", [TP, 2, ST_MAX])
        rden = m.sb("rden", [TP, 2, H])
        o = m.sb("o", [TP, 2, DIM])
        sq = m.sb("sq", [TP, 2, DIM])
        ob = m.sb("ob", [TP, 2, DIM])
        mean = m.sb("mean", [P, DIM])
        meansq = m.sb("meansq", [P, DIM])
        var = m.sb("var", [P, DIM])
        p_s = m.ps("p_s")
        p_q = m.ps("p_q")
        weights = m.sem("weights")
        end = m.sem("end")
        root = m.sem("root")
        st_in = m.moves("st_in")
        out = m.moves("out")
        V = m.steps("vector", "rden o ob")
        S = m.steps("scalar", "sq")
        T = m.steps("tensor", "sum sumsq")
        with nc.Block() as block:

            @block.sync
            def _(sp):
                sp.dma_start(bias[:], a["L0_gnn_gat_bias"].partition_broadcast(P)).then_inc(weights, 16)
                sp.dma_start(gamma[:], a["L0_gnn_bn_gamma"].partition_broadcast(P)).then_inc(weights, 16)
                sp.dma_start(beta[:], a["L0_gnn_bn_beta"].partition_broadcast(P)).then_inc(weights, 16)
                with sp.Fori(0, NT // 2) as i:
                    for b in range(2):
                        t = i * 2 + b
                        sp.wait_ge(*V.after(t - 2, "o"))
                        sp.dma_start(st[:, b], d["state"][bass.ds(t * TP, TP), 0:ST_MAX]).then_inc(*st_in.done(b))

            @block.vector
            def _(dve):
                give_credit(dve, V)
                dve.wait_ge(weights, 48)
                for i in turns(dve, NT // 2):
                    for b in range(2):
                        t = i * 2 + b
                        dve.wait_ge(*st_in.after(i, b))
                        nc.vector.reciprocal(rden[:, b], st[:, b, ST_DEN:ST_MAX]).then_inc(*V.done("rden"))
                        dve.wait_ge(*V.after(t, "rden"))
                        dve.wait_ge(*T.after(t - 2, "sum"))
                        dve.wait_ge(*S.after(t - 2, "sq"))
                        nc.vector.tensor_tensor(heads(o[:, b]), heads(st[:, b, 0:DIM]), over_c(rden[:, b]), ALU.mult).then_inc(*V.done("o"))
                        dve.wait_ge(*V.after(t, "o"))
                        dve.wait_ge(*out.after(i, b, 1))
                        nc.vector.tensor_tensor(ob[:, b], o[:, b], bias[0:TP], ALU.add).then_inc(*V.done("ob"))
                dve.wait_ge(end, 1)
                step = [1]

                def then(ins):
                    step[0] += 1
                    ins.then_inc(end, 1)
                    dve.wait_ge(end, step[0])

                then(nc.vector.tensor_scalar(mean[:], p_s[:], 1.0 / N, None, ALU.mult))
                then(nc.vector.tensor_tensor(meansq[:], mean[:], mean[:], ALU.mult))
                then(nc.vector.scalar_tensor_tensor(var[:], p_q[:], 1.0 / N, meansq[:], ALU.mult, ALU.subtract))
                then(nc.vector.tensor_scalar(var[:], var[:], 0.0, BN_EPS, ALU.max, ALU.add))
                dve.wait_ge(root, 1)
                then(nc.vector.reciprocal(var[:], var[:]))
                then(nc.vector.tensor_tensor(keep["bn_scale"][:], var[:], gamma[:], ALU.mult))
                then(nc.vector.tensor_tensor(mean[:], mean[:], bias[:], ALU.add))
                then(nc.vector.tensor_tensor(mean[:], mean[:], keep["bn_scale"][:], ALU.mult))
                then(nc.vector.tensor_tensor(keep["bn_shift"][:], beta[:], mean[:], ALU.subtract))

            @block.scalar
            def _(act):
                give_credit(act, S)
                with act.Fori(0, NT // 2) as i:
                    for b in range(2):
                        t = i * 2 + b
                        act.wait_ge(*V.after(t, "o"))
                        act.wait_ge(*T.after(t - 2, "sumsq"))
                        nc.scalar.activation(sq[:, b], o[:, b], ACT.Square).then_inc(*S.done("sq"))
                act.wait_ge(end, 5)
                nc.scalar.activation(var[:], var[:], ACT.Sqrt).then_inc(root, 1)

            @block.tensor
            def _(pe):
                give_credit(pe, T)
                nc.tensor.matmul(p_s[:], k["zeros"][:, 0:P], k["zeros"][:, 0:DIM], start=True, stop=False)
                nc.tensor.matmul(p_q[:], k["zeros"][:, 0:P], k["zeros"][:, 0:DIM], start=True, stop=False)
                with pe.Fori(0, NT // 2) as i:
                    for b in range(2):
                        t = i * 2 + b
                        pe.wait_ge(*V.after(t, "o"))
                        nc.tensor.matmul(p_s[:], k["ones"][0:TP, :], o[:, b], start=False, stop=False).then_inc(*T.done("sum"))
                        pe.wait_ge(*S.after(t, "sq"))
                        nc.tensor.matmul(p_q[:], k["ones"][0:TP, :], sq[:, b], start=False, stop=False).then_inc(*T.done("sumsq"))
                nc.tensor.matmul(p_s[:], k["zeros"][:, 0:P], k["zeros"][:, 0:DIM], start=False, stop=True)
                nc.tensor.matmul(p_q[:], k["zeros"][:, 0:P], k["zeros"][:, 0:DIM], start=False, stop=True).then_inc(end, 1)

            @block.gpsimd
            def _(pool):
                with pool.Fori(0, NT // 2) as i:
                    for b in range(2):
                        t = i * 2 + b
                        pool.wait_ge(*V.after(t, "ob"))
                        pool.dma_start(d["gat"][bass.ds(t * TP, TP), :], ob[:, b]).then_inc(*out.done(b))
                for b in range(2):
                    pool.wait_ge(*out.after(NT // 2 - 1, b))


def project_tokens(nc, k, a, d, keep):
    ZW = NE + 2 * H
    with ExitStack() as ctx:
        m = Mem(nc, ctx, "tokens")
        w = m.sb("w", [P, 4, KC, DIM])
        wz = m.sb("wz", [P, KC, ZW])
        decay = m.sb("decay", [P, H])
        dtb = m.sb("dtb", [P, H])
        tie = m.sb("tie", [P, NE, NE])
        gat = m.sb("gat", [TP, 2, DIM])
        xin = m.sb("xin", [TP, 2, DIM])
        skip = m.sb("skip", [TP, 2, DIM])
        res = m.sb("res", [TP, DIM])
        y = m.sb("y", [TP, DIM])
        gl = m.sb("gl", [TP, DIM])
        x2 = m.sb("x2", [TP, 2, DIM])
        stats = m.sb("stats", [TP, 6])
        mv = m.sb("mv", [TP, 2])
        veps = m.sb("veps", [TP, 1])
        rstd = m.sb("rstd", [TP, 1])
        xn = m.sb("xn", [TP, 2, DIM])
        xT = m.sb("xT", [P, 2, KC, TP])
        row = m.sb("row", [TP, 2, TK_W])
        gate = m.sb("gate", [TP, 2, DIM])
        sq = m.sb("sq", [TP, 2 * DIM])
        ss = m.sb("ss", [TP, 2 * H])
        rn = m.sb("rn", [TP, 2 * H])
        z = m.sb("z", [TP, ZW])
        ez = m.sb("ez", [TP, ZW])
        top = m.sb("top", [TP, 1])
        za = m.sb("za", [TP, H])
        zn = m.sb("zn", [TP, H])
        s1 = m.sb("s1", [TP, H])
        s2 = m.sb("s2", [TP, H])
        s3 = m.sb("s3", [TP, H])
        poly = m.sb("poly", [TP, 9, H])
        b1 = m.sb("b1", [TP, H])
        psum_ = m.sb("psum", [TP, 1])
        pr = m.sb("pr", [TP, NE])
        gt = m.sb("gt", [TP, NE, NE])
        eq = m.sb("eq", [TP, NE, NE])
        rank = m.sb("rank", [TP, NE])
        two = m.sb("two", [TP, NE])
        wsum = m.sb("wsum", [TP, 1])
        p_t = m.ps("p_t")
        p_z = m.ps("p_z")
        p_w = [m.ps(f"p_w{j}") for j in range(4)]
        weights = m.sem("weights")
        ready = m.sem("ready")
        loads = m.moves("loads", 3)
        out = m.moves("out", 3)
        L = m.steps("ahead", "scaled y x2 stats aggr xn")
        V = m.steps("vector", "top zmax zb za zn nza b1 beta nbeta s1 s2 s3 "
                              "poly0 poly1 poly2 poly3 poly4 poly5 poly6 poly7 poly8 log pos sp g gfloor "
                              "psum prs pr gt eqr eq both rank two w1 wsum wrec w mask ss rn_q rn_k")
        GL = m.steps("gpsimd_ahead", "res veps rstd")
        G = m.steps("gpsimd", "sq sseps rn")
        SL = m.steps("scalar_ahead", "gelu xT")
        S = m.steps("scalar", "exp q k v gate")
        T = m.steps("tensor", "xT z q k v gate")
        passed_dve = m.sem("passed_dve")
        passed_pool = m.sem("passed_pool")
        with nc.Block() as block:

            @block.sync
            def _(sp):
                for j, name in enumerate(("Wq", "Wk", "Wv", "Wg")):
                    sp.dma_start(w[:, j], a["L0_ffn_" + name].rearrange("(c p) n -> p c n", p=P)).then_inc(weights, 16)
                sp.dma_start(wz[:, :, 0:NE], a["L0_ffn_Wgate"].rearrange("(c p) n -> p c n", p=P)).then_inc(weights, 16)
                sp.dma_start(wz[:, :, NE:NE + H], a["L0_ffn_Wb"].rearrange("(c p) n -> p c n", p=P)).then_inc(weights, 16)
                sp.dma_start(wz[:, :, NE + H:ZW], a["L0_ffn_Wa"].rearrange("(c p) n -> p c n", p=P)).then_inc(weights, 16)
                sp.dma_start(decay[:], a["L0_ffn_A_log"].partition_broadcast(P)).then_inc(weights, 16)
                sp.dma_start(dtb[:], a["L0_ffn_dt_bias"].partition_broadcast(P)).then_inc(weights, 16)
                with sp.Fori(0, NT // 2) as i:
                    for b in range(2):
                        t = i * 2 + b
                        rows = bass.ds(t * TP, TP)
                        sp.wait_ge(*L.after(t - 2, "scaled"))
                        sp.wait_ge(*GL.after(t - 2, "res"))
                        sp.dma_start(gat[:, b], d["gat"][rows, :]).then_inc(*loads.done(b))
                        sp.dma_start(xin[:, b], a["x"][rows, :]).then_inc(*loads.done(b))
                        sp.dma_start(skip[:, b], d["skip"][rows, :]).then_inc(*loads.done(b))

            def norm(t, i, b, dve):
                dve.wait_ge(*loads.after(i, b))
                nc.vector.tensor_tensor(y[:], gat[:, b], keep["bn_scale"][0:TP], ALU.mult).then_inc(*L.done("scaled"))
                dve.wait_ge(*L.after(t, "scaled"))
                nc.vector.tensor_tensor(y[:], y[:], keep["bn_shift"][0:TP], ALU.add).then_inc(*L.done("y"))
                dve.wait_ge(*SL.after(t, "gelu"))
                dve.wait_ge(*GL.after(t, "res"))
                dve.wait_ge(*out.after(i, b, 1))
                nc.vector.tensor_tensor(x2[:, b], gl[:], res[:], ALU.add).then_inc(*L.done("x2"))
                dve.wait_ge(*L.after(t, "x2"))
                nc.vector.bn_stats(stats[:], x2[:, b]).then_inc(*L.done("stats"))
                dve.wait_ge(*L.after(t, "stats"))
                held(dve, passed_dve)
                nc.vector.bn_aggr(mv[:], stats[:]).then_inc(*L.done("aggr"))
                dve.wait_ge(*GL.after(t, "rstd"))
                dve.wait_ge(*T.after(t - 2, "xT"))
                nc.vector.tensor_scalar(xn[:, b], x2[:, b], mv[:, 0:1], rstd[:], ALU.subtract, ALU.mult).then_inc(*L.done("xn"))

            def heads_and_router(t, i, b, dve):
                dve.wait_ge(*T.after(t, "z"))
                dve.wait_ge(*S.after(t - 1, "exp"))
                nc.vector.reduce_max(top[:], p_z[0:TP, 0:NE], AX.X).then_inc(*V.done("top"))
                dve.wait_ge(*V.after(t, "top"))
                nc.vector.tensor_scalar(z[:, 0:NE], p_z[0:TP, 0:NE], top[:], None, ALU.subtract).then_inc(*V.done("zmax"))
                nc.vector.tensor_scalar(z[:, NE:NE + H], p_z[0:TP, NE:NE + H], -1.0, None, ALU.mult).then_inc(*V.done("zb"))
                nc.vector.tensor_tensor(za[:], p_z[0:TP, NE + H:ZW], dtb[0:TP], ALU.add).then_inc(*V.done("za"))
                dve.wait_ge(*V.after(t, "za"))
                nc.vector.tensor_scalar(zn[:], za[:], -1.0, None, ALU.mult).then_inc(*V.done("zn"))
                dve.wait_ge(*V.after(t, "zn"))
                nc.vector.tensor_tensor(z[:, NE + H:ZW], za[:], zn[:], ALU.min).then_inc(*V.done("nza"))
                dve.wait_ge(*S.after(t, "exp"))
                nc.vector.tensor_scalar(b1[:], ez[:, NE:NE + H], 1.0, None, ALU.add).then_inc(*V.done("b1"))
                dve.wait_ge(*V.after(t, "b1"))
                dve.wait_ge(*out.after(i, b, 1))
                nc.vector.reciprocal(row[:, b, TK_B:TK_NB], b1[:]).then_inc(*V.done("beta"))
                dve.wait_ge(*V.after(t, "beta"))
                nc.vector.tensor_scalar(row[:, b, TK_NB:TK_G], row[:, b, TK_B:TK_NB], -1.0, None, ALU.mult).then_inc(*V.done("nbeta"))
                nc.vector.tensor_scalar(s1[:], ez[:, NE + H:ZW], 2.0, None, ALU.add).then_inc(*V.done("s1"))
                dve.wait_ge(*V.after(t, "s1"))
                nc.vector.reciprocal(s2[:], s1[:]).then_inc(*V.done("s2"))
                dve.wait_ge(*V.after(t, "s2"))
                nc.vector.tensor_tensor(s1[:], s2[:], ez[:, NE + H:ZW], ALU.mult).then_inc(*V.done("s3"))
                dve.wait_ge(*V.after(t, "s3"))
                nc.vector.tensor_tensor(s3[:], s1[:], s1[:], ALU.mult).then_inc(*V.done("poly0"))
                dve.wait_ge(*V.after(t, "poly0"))
                nc.vector.tensor_scalar(poly[:, 0], s3[:], 2.0 / 17, None, ALU.mult).then_inc(*V.done("poly1"))
                for j in range(7):
                    dve.wait_ge(*V.after(t, f"poly{j + 1}"))
                    nc.vector.scalar_tensor_tensor(poly[:, j + 1], poly[:, j], 2.0 / (15 - 2 * j), s3[:], ALU.add, ALU.mult).then_inc(*V.done(f"poly{j + 2}"))
                dve.wait_ge(*V.after(t, "poly8"))
                nc.vector.scalar_tensor_tensor(poly[:, 8], poly[:, 7], 2.0, s1[:], ALU.add, ALU.mult).then_inc(*V.done("log"))
                nc.vector.tensor_scalar(zn[:], za[:], 0.0, None, ALU.max).then_inc(*V.done("pos"))
                dve.wait_ge(*V.after(t, "pos"))
                nc.vector.tensor_tensor(zn[:], zn[:], poly[:, 8], ALU.add).then_inc(*V.done("sp"))
                dve.wait_ge(*V.after(t, "sp"))
                nc.vector.scalar_tensor_tensor(za[:], zn[:], -1.0, decay[0:TP], ALU.mult, ALU.mult).then_inc(*V.done("g"))
                dve.wait_ge(*V.after(t, "g"))
                nc.vector.tensor_scalar(row[:, b, TK_G:TK_W], za[:], G_FLOOR, None, ALU.max).then_inc(*V.done("gfloor"))
                nc.vector.reduce_sum(psum_[:], ez[:, 0:NE], AX.X).then_inc(*V.done("psum"))
                dve.wait_ge(*V.after(t, "psum"))
                nc.vector.reciprocal(wsum[:], psum_[:]).then_inc(*V.done("prs"))
                dve.wait_ge(*V.after(t, "prs"))
                nc.vector.tensor_scalar(pr[:], ez[:, 0:NE], wsum[:], None, ALU.mult).then_inc(*V.done("pr"))
                dve.wait_ge(*V.after(t, "pr"))
                mine, other = pr[:].unsqueeze(2).to_broadcast([TP, NE, NE]), pr[:].unsqueeze(1).to_broadcast([TP, NE, NE])
                nc.vector.tensor_tensor(gt[:], other, mine, ALU.is_gt).then_inc(*V.done("gt"))
                nc.vector.tensor_tensor(eq[:], other, mine, ALU.is_equal).then_inc(*V.done("eqr"))
                dve.wait_ge(*V.after(t, "eqr"))
                nc.vector.tensor_tensor(eq[:], eq[:], tie[0:TP], ALU.mult).then_inc(*V.done("eq"))
                dve.wait_ge(*V.after(t, "eq"))
                nc.vector.tensor_tensor(gt[:], gt[:], eq[:], ALU.add).then_inc(*V.done("both"))
                dve.wait_ge(*V.after(t, "both"))
                nc.vector.tensor_reduce(rank[:], gt[:], AX.X, ALU.add).then_inc(*V.done("rank"))
                dve.wait_ge(*V.after(t, "rank"))
                nc.vector.tensor_scalar(two[:], rank[:], 1.5, None, ALU.is_lt).then_inc(*V.done("two"))
                dve.wait_ge(*V.after(t, "two"))
                nc.vector.tensor_tensor(two[:], two[:], pr[:], ALU.mult).then_inc(*V.done("w1"))
                dve.wait_ge(*V.after(t, "w1"))
                nc.vector.reduce_sum(psum_[:], two[:], AX.X).then_inc(*V.done("wsum"))
                dve.wait_ge(*V.after(t, "wsum"))
                nc.vector.reciprocal(wsum[:], psum_[:]).then_inc(*V.done("wrec"))
                dve.wait_ge(*V.after(t, "wrec"))
                nc.vector.tensor_scalar(two[:], two[:], wsum[:], None, ALU.mult).then_inc(*V.done("w"))
                dve.wait_ge(*V.after(t, "w"))
                nc.vector.tensor_copy(keep["weight"][0:TP, :, bass.ds(t, 1)], two[:].unsqueeze(2)).then_inc(*V.done("mask"))
                dve.wait_ge(*G.after(t, "sq"))
                dve.wait_ge(*G.after(t - 1, "sseps"))
                nc.vector.tensor_reduce(ss[:], heads(sq[:], 2 * H), AX.X, ALU.add).then_inc(*V.done("ss"))
                dve.wait_ge(*G.after(t, "rn"))
                nc.vector.scalar_tensor_tensor(heads(row[:, b, 0:DIM]), heads(row[:, b, 0:DIM]), float(C) ** -0.5, over_c(rn[:, 0:H]), ALU.mult, ALU.mult).then_inc(*V.done("rn_q"))
                nc.vector.tensor_tensor(heads(row[:, b, TK_K:TK_V]), heads(row[:, b, TK_K:TK_V]), over_c(rn[:, H:2 * H]), ALU.mult).then_inc(*V.done("rn_k"))

            @block.vector
            def _(dve):
                give_credit(dve, V, L)
                dve.wait_ge(weights, 16 * 9)
                dve.wait_ge(ready, 2)
                norm(0, 0, 0, dve)
                for i in turns(dve, NT // 2 - 1):
                    norm(i * 2 + 1, i, 1, dve)
                    heads_and_router(i * 2, i, 0, dve)
                    norm(i * 2 + 2, i + 1, 0, dve)
                    heads_and_router(i * 2 + 1, i, 1, dve)
                norm(NT - 1, NT // 2 - 1, 1, dve)
                heads_and_router(NT - 2, NT // 2 - 1, 0, dve)
                heads_and_router(NT - 1, NT // 2 - 1, 1, dve)

            def residual(t, b, i, pool):
                pool.wait_ge(*loads.after(i, b))
                pool.wait_ge(*L.after(t - 1, "x2"))
                nc.gpsimd.tensor_tensor(res[:], xin[:, b], skip[:, b], ALU.add).then_inc(*GL.done("res"))
                pool.wait_ge(*L.after(t, "aggr"))
                held(pool, passed_pool)
                nc.gpsimd.tensor_scalar(veps[:], mv[:, 1:2], LN_EPS, None, ALU.add).then_inc(*GL.done("veps"))
                pool.wait_ge(*GL.after(t, "veps"))
                pool.wait_ge(*L.after(t - 1, "xn"))
                nc.gpsimd.tensor_tensor(rstd[:], veps[:], k["minus_half"][0:TP], ALU.pow).then_inc(*GL.done("rstd"))

            def squares(t, b, i, pool):
                pool.wait_ge(*S.after(t, "k"))
                pool.wait_ge(*V.after(t - 1, "ss"))
                nc.gpsimd.tensor_tensor(sq[:], row[:, b, 0:TK_V], row[:, b, 0:TK_V], ALU.mult).then_inc(*G.done("sq"))
                pool.wait_ge(*V.after(t, "ss"))
                held(pool, passed_pool)
                nc.gpsimd.tensor_scalar(ss[:], ss[:], 1e-6, None, ALU.add).then_inc(*G.done("sseps"))
                pool.wait_ge(*G.after(t, "sseps"))
                pool.wait_ge(*V.after(t - 1, "rn_k"))
                nc.gpsimd.tensor_tensor(rn[:], ss[:], k["minus_half"][0:TP].to_broadcast([TP, 2 * H]), ALU.pow).then_inc(*G.done("rn"))
                pool.wait_ge(*V.after(t, "rn_k"))
                pool.wait_ge(*S.after(t, "gate"))
                rows = bass.ds(t * TP, TP)
                pool.dma_start(d["token"][rows, :], row[:, b]).then_inc(*out.done(b))
                pool.dma_start(d["gate"][rows, :], gate[:, b]).then_inc(*out.done(b))
                pool.dma_start(d["x2"][rows, :], x2[:, b]).then_inc(*out.done(b))

            @block.gpsimd
            def _(pool):
                give_credit(pool, G, GL)
                nc.gpsimd.memset(tie[:], 1.0).then_inc(ready, 1)
                pool.wait_ge(ready, 2)
                nc.gpsimd.affine_select(out=tie[:], in_=tie[:], pattern=[[1, NE], [-1, NE]], compare_op=ALU.is_gt, fill=0.0, base=0, channel_multiplier=0).then_inc(ready, 1)
                residual(0, 0, 0, pool)
                with pool.Fori(0, NT // 2 - 1) as i:
                    residual(i * 2 + 1, 1, i, pool)
                    squares(i * 2, 0, i, pool)
                    residual(i * 2 + 2, 0, i + 1, pool)
                    squares(i * 2 + 1, 1, i, pool)
                residual(NT - 1, 1, NT // 2 - 1, pool)
                squares(NT - 2, 0, NT // 2 - 1, pool)
                squares(NT - 1, 1, NT // 2 - 1, pool)
                for b in range(2):
                    pool.wait_ge(*out.after(NT // 2 - 1, b))

            def ahead(t, b, act):
                act.wait_ge(*L.after(t, "y"))
                act.wait_ge(*L.after(t - 1, "x2"))
                nc.scalar.activation(gl[:], y[:], ACT.Gelu).then_inc(*SL.done("gelu"))
                act.wait_ge(*T.after(t, "xT"))
                act.wait_ge(*T.after(t - 2, "gate"))
                nc.scalar.copy(xT[:, b].rearrange("p c t -> p (c t)"), p_t[:, 0:KC * TP]).then_inc(*SL.done("xT"))

            def behind(t, i, b, act):
                act.wait_ge(*V.after(t, "nza"))
                act.wait_ge(*V.after(t - 1, "pr"))
                nc.scalar.activation(ez[:], z[:], ACT.Exp).then_inc(*S.done("exp"))
                act.wait_ge(*out.after(i, b, 1))
                for j, name in enumerate(("q", "k", "v", "gate")):
                    act.wait_ge(*T.after(t, name))
                    to = gate[:, b] if j == 3 else row[:, b, j * DIM:(j + 1) * DIM]
                    nc.scalar.activation(to, p_w[j][0:TP, :], ACT.Silu).then_inc(*S.done(name))

            @block.scalar
            def _(act):
                give_credit(act, S, SL)
                act.wait_ge(weights, 16 * 9)
                nc.scalar.activation(decay[:], decay[:], ACT.Exp).then_inc(ready, 1)
                ahead(0, 0, act)
                for i in turns(act, NT // 2 - 1):
                    ahead(i * 2 + 1, 1, act)
                    behind(i * 2, i, 0, act)
                    ahead(i * 2 + 2, 0, act)
                    behind(i * 2 + 1, i, 1, act)
                ahead(NT - 1, 1, act)
                behind(NT - 2, NT // 2 - 1, 0, act)
                behind(NT - 1, NT // 2 - 1, 1, act)

            def transposes(t, b, pe):
                pe.wait_ge(*L.after(t, "xn"))
                pe.wait_ge(*SL.after(t - 1, "xT"))
                for c in range(KC):
                    last = nc.tensor.transpose(p_t[:, c * TP:(c + 1) * TP], xn[:, b, c * P:(c + 1) * P], k["ident"][0:TP, 0:TP])
                last.then_inc(*T.done("xT"))

            @block.tensor
            def _(pe):
                give_credit(pe, T)
                pe.wait_ge(weights, 16 * 9)
                with pe.Fori(0, NT // 2) as i:
                    for b in range(2):
                        t = i * 2 + b
                        transposes(t, b, pe)
                        pe.wait_ge(*SL.after(t, "xT"))
                        pe.wait_ge(*V.after(t - 1, "za"))
                        for c in range(KC):
                            last = nc.tensor.matmul(p_z[0:TP, 0:ZW], xT[:, b, c], wz[:, c], start=c == 0, stop=c == KC - 1)
                        last.then_inc(*T.done("z"))
                        for j, name in enumerate(("q", "k", "v", "gate")):
                            pe.wait_ge(*S.after(t - 1, name))
                            for c in range(KC):
                                last = nc.tensor.matmul(p_w[j][0:TP, :], xT[:, b, c], w[:, j, c], start=c == 0, stop=c == KC - 1)
                            last.then_inc(*T.done(name))


def route(nc, k, a, d, keep):
    M = NE * NT
    with ExitStack() as ctx:
        m = Mem(nc, ctx, "route")
        mask = m.sb("mask", [P, NE, NT])
        prefix = m.sb("prefix", [P, NE, NT])
        total = m.sb("total", [P, NE, NT])
        upto = m.sb("upto", [P, NE, NT])
        pos = m.sb("pos", [P, NE, NT])
        hid = m.sb("hid", [P, NE, NT])
        tmp = m.sb("tmp", [P, NE, NT])
        sel = m.sb("sel", [P, NE, NT])
        one = m.sb("one", [P, NT])
        starts = m.sb("starts", [P, NE + 1])
        count = m.sb("count", [P, NCH])
        chunks = m.sb("chunks", [P, NE])
        slot = m.sb("slot", [P, 2, NT])
        both = m.sb("both", [P, NT])
        dumped = m.sb("dumped", [P, NT])
        isstart = m.sb("isstart", [P, NCH + 4])
        sc = m.sb("sc", [P, 2, NT], I32)
        token = m.sb("token", [P, NT], I32)
        zero = m.sb("zero", [P, NCH + 4], I32)
        col = m.sb("col", [TP, 2, 3, 1], I32)
        p_p = m.ps("p_p")
        p_t = m.ps("p_t")
        V = m.sem("vector")
        made = m.sem("made")
        counted = m.sem("counted")
        cleared = m.sem("cleared")
        G = m.steps("gpsimd", "copy0 copy1 copy2")
        moved = m.moves("moved", 2)
        ROUTED = 70
        n_steps = [0]
        passed_pool = m.sem("passed_pool")
        with nc.Block() as block:

            @block.vector
            def _(dve):
                step = [0]

                def then(ins):
                    step[0] += 1
                    ins.then_inc(V, 1)
                    dve.wait_ge(V, step[0])

                wt = keep["weight"]
                then(nc.vector.memset(one[:], 1.0))
                then(nc.vector.tensor_scalar(mask[0:TP], wt[0:TP], 0.0, None, ALU.is_gt))
                dve.wait_ge(counted, 1)
                then(nc.vector.tensor_copy(prefix[0:TP].rearrange("p e t -> p (e t)"), p_p[0:TP, 0:M]))
                then(nc.vector.tensor_copy(total[:].rearrange("p e t -> p (e t)"), p_t[:, 0:M]))
                for e in range(NE):
                    then(nc.vector.tensor_tensor_scan(upto[:, e], one[:], total[:, e], 0.0, ALU.mult, ALU.add))
                then(nc.vector.memset(starts[:], 0.0))
                for e in range(NE):
                    then(nc.vector.tensor_scalar(count[:], k["chunk_no"][:, 0:NCH], float(CH), upto[:, e, NT - 1:NT], ALU.mult, ALU.is_lt))
                    then(nc.vector.reduce_sum(chunks[:, e:e + 1], count[:], AX.X))
                    then(nc.vector.tensor_tensor(starts[:, e + 1:e + 2], starts[:, e:e + 1], chunks[:, e:e + 1], ALU.add))
                then(nc.vector.tensor_tensor(pos[:], upto[:], total[:], ALU.subtract))
                then(nc.vector.tensor_tensor(pos[0:TP], pos[0:TP], prefix[0:TP], ALU.add))
                for e in range(NE):
                    then(nc.vector.tensor_scalar(count[:, 0:1], starts[:, e:e + 1], float(CH), None, ALU.mult))
                    then(nc.vector.tensor_scalar(pos[:, e], pos[:, e], count[:, 0:1], None, ALU.add))
                for s, (far, op) in enumerate(((1.0, ALU.min), (-1.0, ALU.max))):
                    then(nc.vector.tensor_scalar(hid[0:TP], mask[0:TP], -1e6 * far, 1e6 * far, ALU.mult, ALU.add))
                    then(nc.vector.tensor_tensor(tmp[0:TP], pos[0:TP], mask[0:TP], ALU.mult))
                    then(nc.vector.tensor_tensor(tmp[0:TP], tmp[0:TP], hid[0:TP], ALU.add))
                    then(nc.vector.tensor_reduce(slot[0:TP, s], tmp[0:TP].rearrange("p e t -> p t e"), AX.X, op))
                    then(nc.vector.tensor_tensor(sel[0:TP], tmp[0:TP], slot[0:TP, s].unsqueeze(1).to_broadcast([TP, NE, NT]), ALU.is_equal))
                    then(nc.vector.tensor_tensor(sel[0:TP], sel[0:TP], wt[0:TP], ALU.mult))
                    then(nc.vector.tensor_reduce(keep["slot_weight"][0:TP, s], sel[0:TP].rearrange("p e t -> p t e"), AX.X, ALU.add))
                then(nc.vector.tensor_tensor(both[0:TP], slot[0:TP, 1], slot[0:TP, 0], ALU.is_gt))
                then(nc.vector.tensor_tensor(keep["slot_weight"][0:TP, 1], keep["slot_weight"][0:TP, 1], both[0:TP], ALU.mult))
                then(nc.vector.tensor_copy(keep["slot"][0:TP], slot[0:TP]))
                then(nc.vector.tensor_copy(sc[0:TP, 0], slot[0:TP, 0]))
                then(nc.vector.tensor_scalar(dumped[0:TP], slot[0:TP, 1], k["dumpslot"][0:TP], None, ALU.subtract))
                then(nc.vector.tensor_tensor(dumped[0:TP], dumped[0:TP], both[0:TP], ALU.mult))
                then(nc.vector.tensor_scalar(sc[0:TP, 1], dumped[0:TP], k["dumpslot"][0:TP], None, ALU.add))
                then(nc.vector.memset(keep["goes_on"][:], 1.0))
                for e in range(NE):
                    then(nc.vector.tensor_scalar(isstart[:], k["chunk_no"][:], starts[:, e:e + 1], None, ALU.not_equal))
                    then(nc.vector.tensor_tensor(keep["goes_on"][:], keep["goes_on"][:], isstart[:], ALU.mult))
                n_steps[0] = step[0]

            @block.tensor
            def _(pe):
                pe.wait_ge(V, 2)
                nc.tensor.matmul(p_p[0:TP, 0:M], k["after"][0:TP, 0:TP], mask[0:TP].rearrange("p e t -> p (e t)"), start=True, stop=True)
                nc.tensor.matmul(p_t[:, 0:M], k["ones"][0:TP, :], mask[0:TP].rearrange("p e t -> p (e t)"), start=True, stop=True).then_inc(counted, 1)

            @block.gpsimd
            def _(pool):
                give_credit(pool, G)
                nc.gpsimd.iota(token[:], [[TP, NT]], base=0, channel_multiplier=1)
                nc.gpsimd.memset(zero[:], 0).then_inc(made, 1)
                pool.wait_ge(cleared, 16)
                pool.wait_ge(V, n_steps[0])
                for i in turns(pool, NT // 2):
                    for b in range(2):
                        t = i * 2 + b
                        pool.wait_ge(*moved.after(i, b, 1))
                        nc.gpsimd.tensor_copy(col[:, b, 0], sc[0:TP, 0, bass.ds(t, 1)]).then_inc(*G.done("copy0"))
                        nc.gpsimd.tensor_copy(col[:, b, 1], sc[0:TP, 1, bass.ds(t, 1)]).then_inc(*G.done("copy1"))
                        nc.gpsimd.tensor_copy(col[:, b, 2], token[0:TP, bass.ds(t, 1)]).then_inc(*G.done("copy2"))
                        pool.wait_ge(*G.after(t, "copy2"))
                        held(pool, passed_pool)
                        for s in range(2):
                            nc.gpsimd.indirect_dma_start(out=d["table"][:, :], out_offset=bass.IndirectOffsetOnAxis(ap=col[:, b, s], axis=0), in_=col[:, b, 2], in_offset=None).then_inc(*moved.done(b))
                for b in range(2):
                    pool.wait_ge(*moved.after(NT // 2 - 1, b))

            @block.sync
            def _(sp):
                sp.wait_ge(made, 1)
                sp.dma_start(d["table"].rearrange("(p c) o -> p (c o)", p=P), zero[:]).then_inc(cleared, 16)
                sp.wait_ge(cleared, 16)


def delta_rule(nc, k, a, d, keep):
    LV = 7
    with ExitStack() as ctx:
        m = Mem(nc, ctx, "delta")
        idx = m.sb("idx", [P, 2, 1], I32)
        x = m.sb("x", [P, 2, TK_W])
        kb = m.sb("kb", [P, DIM])
        vb = m.sb("vb", [P, 2, DIM])
        gb = m.sb("gb", [P, H, P])
        kT = m.sb("kT", [P, 4, P])
        qT = m.sb("qT", [P, 2, 4, P])
        kbT = m.sb("kbT", [P, 2, 4, P])
        ex = m.sb("ex", [P, 2, 3 * H])
        exk = m.sb("exk", [P, 2, 2 * H])
        gsel = m.sb("gsel", [P, 2, 4])
        dec = m.sb("dec", [P, H, P])
        bT = m.sb("bT", [P, 2, H, P])
        pm = m.sb("pm", [P, 2, H, P])
        invs = m.sb("invs", [P, 2, H, 64])
        join = m.sb("join", [P, H, 64])
        lastT = m.sb("lastT", [P, 2, H, P])
        kd = m.sb("kd", [P, 2, DIM])
        state = m.sb("state", [P, 4, C])
        s1 = m.sb("s1", [P, 4, C])
        r1 = m.sb("r1", [P, DIM])
        r = m.sb("r", [P, DIM])
        dl = m.sb("dl", [P, DIM])
        oq = m.sb("oq", [P, DIM])
        o = m.sb("o", [P, 2, DIM])
        z_ = [m.ps(f"z{n}") for n in range(2)]
        tu_ = [m.ps(f"tu{n}") for n in range(2)]
        e_ = [m.ps(f"e{n}") for n in range(2)]
        c_ = m.ps("c", [P, 2, 512])
        idx_in = m.moves("idx_in")
        x_in = m.moves("x_in")
        out = m.moves("out")
        levels = range(1, LV - 1)
        LAST = LV - 1
        TE = m.steps("pe_early", "k kb q sums diff0 diff1 kk0 kk1 qk0 qk1")
        SE = m.steps("act_early", "kT qT ex dec0 dec1")
        VE = m.steps("dve_early", "kbT exk gselA gselB kd a0 a1 pm0 pm1")
        GE = m.steps("pool_early", "kb gb0 gb1 vb bT0 bT1")
        TL = m.steps("pe_late", "b0 b1 " + " ".join(f"z{v}0 z{v}1 tu{v}0 tu{v}1" for v in levels) + " zlast ulast")
        SL = m.steps("act_late", " ".join(f"tu{v}0 tu{v}1" for v in levels) + " ulast")
        VL = m.steps("dve_late", "u0 u1 t0 t1 " + " ".join(f"j{v}0 j{v}1" for v in levels) + " jlast")
        TC = m.steps("pe_chain", "kq d s o")
        SC = m.steps("act_chain", "d")
        VC = m.steps("dve_chain", "r1 oq r s1 s o")
        init = m.sem("init")

        def place(h):
            return h % 2 * 4 + h // 2

        def by_parity(ap, c=C):
            return ap.rearrange("p (q r c) -> p r q c", r=2, c=c)

        def per_head(ap):
            return ap.rearrange("p (q r) -> p r q", r=2).unsqueeze(3).to_broadcast([P, 2, 4, C])

        def half(tile, n):
            return tile[:, 4 * n:4 * n + 4].rearrange("p h c -> p (h c)")

        def side(tile, s):
            rows = slice(64 * s, 64 * s + 64)
            return tile[rows, :, rows]

        def quads(ap):
            return ap.rearrange("p (h c) -> p h c", h=4)

        passed_pool = m.sem("passed_pool")
        passed_pe = m.sem("passed_pe")
        with nc.Block() as block:

            @block.sync
            def _(sp):
                def load(i, b):
                    sp.wait_ge(*x_in.after(i, b, 1))
                    sp.dma_start(idx[:, b], d["table"][bass.ds((i * 2 + b) * CH, CH), :]).then_inc(*idx_in.done(b))

                def store(c, b):
                    sp.wait_ge(*VC.after(c, "o"))
                    sp.dma_start(d["o"][bass.ds(c * CH, CH), :], o[:, b]).then_inc(*out.done(b))

                load(0, 0)
                load(0, 1)
                load(1, 0)
                with sp.Fori(0, NCH // 2) as i:
                    load(i + 1, 1)
                    store(i * 2, 0)
                    load(i + 2, 0)
                    store(i * 2 + 1, 1)
                sp.wait_ge(*idx_in.after(NCH // 2 + 1, 0))
                sp.wait_ge(*idx_in.after(NCH // 2, 1))
                for b in range(2):
                    sp.wait_ge(*out.after(NCH // 2 - 1, b))

            @block.gpsimd
            def _(pool):
                def gather(i, b):
                    p = i * 2 + b
                    pool.wait_ge(*idx_in.after(i, b))
                    pool.wait_ge(*TE.after(p - 2, "sums"))
                    pool.wait_ge(*VE.after(p - 2, "kd"))
                    pool.wait_ge(*GE.after(p - 2, "vb"))
                    held(pool, passed_pool)
                    nc.gpsimd.indirect_dma_start(out=x[:, b], out_offset=None, in_=d["token"][:, :], in_offset=bass.IndirectOffsetOnAxis(ap=idx[:, b], axis=0)).then_inc(*x_in.done(b))

                def early(i, b):
                    p = i * 2 + b
                    pool.wait_ge(*x_in.after(i, b))
                    pool.wait_ge(*TE.after(p - 1, "kb"))
                    nc.gpsimd.tensor_tensor(heads(kb[:]), heads(x[:, b, TK_K:TK_V]), over_c(x[:, b, TK_NB:TK_G]), ALU.mult).then_inc(*GE.done("kb"))
                    pool.wait_ge(*TE.after(p - 1, "diff1"))
                    for n in range(2):
                        g = x[:, b, TK_G:TK_W].rearrange("p (q r) -> p r q", r=2)[:, n]
                        nc.gpsimd.tensor_tensor(gb[:, 4 * n:4 * n + 4], over_h(k["at_or_after"][:], 4), over_c(g, P), ALU.mult).then_inc(*GE.done(f"gb{n}"))
                    pool.wait_ge(*VC.after(p - 2, "r"))
                    nc.gpsimd.tensor_tensor(heads(vb[:, b]), heads(x[:, b, TK_V:TK_B]), over_c(x[:, b, TK_B:TK_NB]), ALU.mult).then_inc(*GE.done("vb"))
                    for n in range(2):
                        pool.wait_ge(*VE.after(p, f"a{n}"))
                        held(pool, passed_pool)
                        part = bT[:, b, 4 * n:4 * n + 4]
                        nc.gpsimd.affine_select(out=part, in_=part, pattern=[[0, 4], [1, P]], compare_op=ALU.not_equal, fill=1.0, base=0, channel_multiplier=-1).then_inc(*GE.done(f"bT{n}"))

                give_credit(pool, GE)
                nc.gpsimd.memset(lastT[:], 0.0)
                nc.gpsimd.memset(state[:], 0.0).then_inc(init, 1)
                gather(0, 0)
                gather(0, 1)
                early(0, 0)
                gather(1, 0)
                early(0, 1)
                with pool.Fori(0, NCH // 2) as i:
                    gather(i + 1, 1)
                    early(i + 1, 0)
                    gather(i + 2, 0)
                    early(i + 1, 1)
                pool.wait_ge(*x_in.after(NCH // 2 + 1, 0))

            @block.vector
            def _(dve):
                def key_rows(p, b):
                    dve.wait_ge(*TE.after(p, "kb"))
                    dve.wait_ge(*TC.after(p - 2, "kq"))
                    nc.vector.tensor_copy(kbT[:, b].rearrange("p h c -> p (h c)"), e_[1][:]).then_inc(*VE.done("kbT"))

                def decays(p, b):
                    dve.wait_ge(*SE.after(p, "ex"))
                    dve.wait_ge(*TC.after(p - 2, "s"))
                    nc.vector.tensor_scalar(exk[:, b], ex[:, b, H:3 * H], keep["goes_on"][:, bass.ds(p + 1, 1)], None, ALU.mult).then_inc(*VE.done("exk"))
                    dve.wait_ge(*VE.after(p, "exk"))
                    for r0, name in ((0, "gselA"), (1, "gselB")):
                        part = slice(C * r0, C * r0 + C)
                        nc.vector.tensor_copy(gsel[part, b], exk[part, b, H:2 * H].rearrange("p (h r) -> p h r", r=2)[:, :, r0]).then_inc(*VE.done(name))
                    nc.vector.tensor_tensor(heads(kd[:, b]), heads(x[:, b, TK_K:TK_V]), over_c(exk[:, b, 0:H]), ALU.mult).then_inc(*VE.done("kd"))

                def key_grams(p, b):
                    dve.wait_ge(*TL.after(p - 2, "zlast"))
                    for n in range(2):
                        dve.wait_ge(*TE.after(p, f"kk{n}"))
                        dve.wait_ge(*SE.after(p, f"dec{n}"))
                        nc.vector.tensor_tensor(half(bT[:, b], n), e_[n][:], half(dec, n), ALU.mult).then_inc(*VE.done(f"a{n}"))

                def query_grams(p, b):
                    dve.wait_ge(*TC.after(p - 2, "o"))
                    for n in range(2):
                        dve.wait_ge(*TE.after(p, f"qk{n}"))
                        nc.vector.tensor_tensor(half(pm[:, b], n), e_[n][:], half(dec, n), ALU.mult).then_inc(*VE.done(f"pm{n}"))

                def first_level(p, b):
                    dve.wait_ge(*GE.after(p, "bT1"))
                    dve.wait_ge(*TL.after(p - 1, f"tu{LAST - 1}1"))
                    for s in range(2):
                        rows = slice(64 * s, 64 * s + 64)
                        nc.vector.tensor_tensor(invs[rows, 1], side(bT[:, b], s), over_h(k["mergeT_half"][rows], H), ALU.mult).then_inc(*VL.done(f"u{s}"))
                    for n in range(2):
                        dve.wait_ge(*TL.after(p, f"b{n}"))
                        nc.vector.tensor_tensor(invs[:, 0, 4 * n:4 * n + 4], quads(z_[n][:, 0:256]), over_h(k["merge_half"][:, 0], 4), ALU.mult).then_inc(*VL.done(f"t{n}"))

                def level(p, v):
                    for n in range(2):
                        dve.wait_ge(*TL.after(p, f"z{v}{n}"))
                        nc.vector.tensor_tensor(join[:, 4 * n:4 * n + 4], quads(z_[n][:, 0:256]), over_h(k["merge_half"][:, v], 4), ALU.mult).then_inc(*VL.done(f"j{v}{n}"))

                def last_level(p):
                    dve.wait_ge(*TL.after(p, "zlast"))
                    nc.vector.tensor_copy(join[64:P].rearrange("p h c -> p (h c)"), z_[0][64:P, :]).then_inc(*VL.done("jlast"))

                def rows(c, b):
                    dve.wait_ge(*TC.after(c, "kq"))
                    nc.vector.tensor_tensor(by_parity(r1[:]), c_[:, :, 0:4 * C].rearrange("p r (q c) -> p r q c", q=4), per_head(ex[:, b, 0:H]), ALU.mult).then_inc(*VC.done("r1"))
                    nc.vector.tensor_tensor(by_parity(oq[:]), c_[:, :, 4 * C:8 * C].rearrange("p r (q c) -> p r q c", q=4), per_head(ex[:, b, 0:H]), ALU.mult).then_inc(*VC.done("oq"))
                    dve.wait_ge(*VC.after(c, "r1"))
                    nc.vector.tensor_tensor(r[:], r1[:], vb[:, b], ALU.add).then_inc(*VC.done("r"))
                    nc.vector.tensor_tensor(s1[:], state[:], over_c(gsel[:, b]), ALU.mult).then_inc(*VC.done("s1"))

                def advance(c, i, b):
                    dve.wait_ge(*TC.after(c, "s"))
                    nc.vector.tensor_tensor(state[:].rearrange("p h c -> p (h c)"), s1[:].rearrange("p h c -> p (h c)"), c_[:, 0, 0:4 * C], ALU.add).then_inc(*VC.done("s"))
                    dve.wait_ge(*TC.after(c, "o"))
                    dve.wait_ge(*out.after(i, b, 1))
                    nc.vector.tensor_tensor(o[:, b], oq[:], c_[:, 1], ALU.add).then_inc(*VC.done("o"))

                def turn(i, b, c):
                    first_level(c + 1, 1 - b)
                    rows(c, b)
                    level(c + 1, 1)
                    key_rows(c + 2, b)
                    level(c + 1, 2)
                    advance(c, i, b)
                    decays(c + 2, b)
                    level(c + 1, 3)
                    key_grams(c + 2, b)
                    level(c + 1, 4)
                    query_grams(c + 2, b)
                    level(c + 1, 5)
                    last_level(c + 1)

                give_credit(dve, VE, VL, VC)
                dve.wait_ge(init, 1)
                for p in range(2):
                    key_rows(p, p)
                    decays(p, p)
                    key_grams(p, p)
                    query_grams(p, p)
                    if p == 0:
                        first_level(0, 0)
                        for v in levels:
                            level(0, v)
                        last_level(0)
                for i in turns(dve, NCH // 2):
                    turn(i, 0, i * 2)
                    turn(i, 1, i * 2 + 1)

            @block.scalar
            def _(act):
                def key_rows(p, b):
                    act.wait_ge(*TE.after(p, "k"))
                    act.wait_ge(*TE.after(p - 1, "qk1"))
                    nc.scalar.copy(kT[:].rearrange("p h c -> p (h c)"), e_[0][:]).then_inc(*SE.done("kT"))

                def decays(p, b):
                    act.wait_ge(*TE.after(p, "q"))
                    act.wait_ge(*TC.after(p - 2, "kq"))
                    nc.scalar.copy(qT[:, b].rearrange("p h c -> p (h c)"), e_[0][:]).then_inc(*SE.done("qT"))
                    act.wait_ge(*TE.after(p, "sums"))
                    act.wait_ge(*VC.after(p - 2, "oq"))
                    nc.scalar.activation(ex[:, b], e_[1][:, 0:3 * H], ACT.Exp).then_inc(*SE.done("ex"))
                    for n in range(2):
                        act.wait_ge(*TE.after(p, f"diff{n}"))
                        act.wait_ge(*VE.after(p - 1, f"pm{n}"))
                        nc.scalar.activation(half(dec, n), e_[n][:], ACT.Exp).then_inc(*SE.done(f"dec{n}"))

                def level(p, b, v):
                    if v == LAST - 1:
                        act.wait_ge(*TC.after(p - 2, "d"))
                    for n in range(2):
                        hs = slice(4 * n, 4 * n + 4)
                        act.wait_ge(*TL.after(p, f"tu{v}{n}"))
                        if v < LAST - 1:
                            nc.scalar.copy(invs[:, :, hs].rearrange("p w h c -> p w (h c)"), tu_[n][:].rearrange("p (w c) -> p w c", w=2)).then_inc(*SL.done(f"tu{v}{n}"))
                        else:
                            nc.scalar.copy(invs[:, 0, hs], quads(tu_[n][:, 0:256]))
                            nc.scalar.copy(lastT[0:64, b, hs, 0:64], quads(tu_[n][0:64, 256:512]))
                            nc.scalar.copy(lastT[64:P, b, hs, 64:P], quads(tu_[n][64:P, 256:512])).then_inc(*SL.done(f"tu{v}{n}"))

                def last_level(p, b):
                    act.wait_ge(*TL.after(p, "ulast"))
                    nc.scalar.copy(lastT[0:64, b, :, 64:P], tu_[0][0:64, :].rearrange("p (h c) -> p h c", h=H)).then_inc(*SL.done("ulast"))

                def rows(c):
                    act.wait_ge(*TC.after(c, "d"))
                    nc.scalar.copy(dl[:], c_[:, 0]).then_inc(*SC.done("d"))

                def turn(b, c):
                    level(c + 1, 1 - b, 1)
                    rows(c)
                    key_rows(c + 2, b)
                    level(c + 1, 1 - b, 2)
                    decays(c + 2, b)
                    for v in range(3, LAST):
                        level(c + 1, 1 - b, v)
                    last_level(c + 1, 1 - b)

                give_credit(act, SE, SL, SC)
                act.wait_ge(init, 1)
                for p in range(2):
                    key_rows(p, p)
                    decays(p, p)
                    if p == 0:
                        for v in levels:
                            level(0, 0, v)
                        last_level(0, 0)
                with act.Fori(0, NCH // 2) as i:
                    turn(0, i * 2)
                    turn(1, i * 2 + 1)

            @block.tensor
            def _(pe):
                ident = k["ident"][:]

                def keys(p, i, b):
                    pe.wait_ge(*x_in.after(i, b))
                    pe.wait_ge(*VE.after(p - 1, "pm1"))
                    for q in range(4):
                        last = nc.tensor.transpose(e_[0][:, q * P:(q + 1) * P], x[:, b, TK_K + q * P:TK_K + (q + 1) * P], ident)
                    last.then_inc(*TE.done("k"))
                    pe.wait_ge(*GE.after(p, "kb"))
                    for q in range(4):
                        last = nc.tensor.transpose(e_[1][:, q * P:(q + 1) * P], kb[:, q * P:(q + 1) * P], ident)
                    last.then_inc(*TE.done("kb"))

                def queries(p, b):
                    pe.wait_ge(*SE.after(p, "kT"))
                    for q in range(4):
                        last = nc.tensor.transpose(e_[0][:, q * P:(q + 1) * P], x[:, b, q * P:(q + 1) * P], ident)
                    last.then_inc(*TE.done("q"))
                    pe.wait_ge(*VE.after(p, "kbT"))
                    g = x[:, b, TK_G:TK_W]
                    nc.tensor.matmul(e_[1][:, 0:H], k["at_or_after"][:], g, start=True, stop=True)
                    nc.tensor.matmul(e_[1][:, H:2 * H], k["before"][:], g, start=True, stop=True)
                    nc.tensor.matmul(e_[1][:, 2 * H:3 * H], k["ones"][:], g, start=True, stop=True).then_inc(*TE.done("sums"))

                def differences(p):
                    for n, name in enumerate(("qT", "ex")):
                        pe.wait_ge(*GE.after(p, f"gb{n}"))
                        pe.wait_ge(*SE.after(p, name))
                        nc.tensor.matmul(e_[n][:], k["before"][:], half(gb, n), start=True, stop=False)
                        nc.tensor.matmul(quads(e_[n][:]), k["identb"][:], over_h(k["hide"][:], 4), start=False, stop=True).then_inc(*TE.done(f"diff{n}"))

                def grams(p, b, right, name, free):
                    for n in range(2):
                        pe.wait_ge(*free(n))
                        part = slice(C * n, C * n + C)
                        for q in range(4):
                            last = nc.tensor.matmul(e_[n][:, q * P:q * P + P], kT[part, q], right[part, b, q], start=True, stop=True)
                        last.then_inc(*TE.done(f"{name}{n}"))

                def key_grams(p, b):
                    grams(p, b, kbT, "kk", lambda n: SE.after(p, f"dec{n}"))

                def query_grams(p, b):
                    grams(p, b, qT, "qk", lambda n: VE.after(p, f"a{n}"))

                def product(to, left, right, n):
                    for h in range(4):
                        for s in range(2):
                            rows = slice(64 * s, 64 * s + 64)
                            last = nc.tensor.matmul(to[rows, h * 64:h * 64 + 64], left(rows, 4 * n + h), right(rows, 4 * n + h), start=True, stop=True)
                    return last

                def first_level(p, b):
                    pe.wait_ge(*GE.after(p, "bT1"))
                    pe.wait_ge(*VL.after(p - 1, "jlast"))
                    held(pe, passed_pe)
                    for n in range(2):
                        product(z_[n], lambda rows, h: bT[rows, b, h, rows], lambda rows, h: k["ident"][rows, rows], n).then_inc(*TL.done(f"b{n}"))

                def level_z(p, b, v):
                    for n in range(2):
                        pe.wait_ge(*(VL.after(p, f"t{n}") if v == 1 else SL.after(p, f"tu{v - 1}{n}")))
                        held(pe, passed_pe)
                        product(z_[n], lambda rows, h: bT[rows, b, h, rows], lambda rows, h: invs[rows, 0, h], n).then_inc(*TL.done(f"z{v}{n}"))

                def level_tu(p, v):
                    for n in range(2):
                        pe.wait_ge(*VL.after(p, f"j{v}{n}"))
                        if v == 1:
                            pe.wait_ge(*SL.after(p - 1, "ulast"))
                        held(pe, passed_pe)
                        product(tu_[n][:, 0:256], lambda rows, h: invs[rows, 1, h], lambda rows, h: join[rows, h], n)
                        product(tu_[n][:, 256:512], lambda rows, h: join[rows, h], lambda rows, h: invs[rows, 1, h], n).then_inc(*TL.done(f"tu{v}{n}"))

                def last_level(p, b):
                    pe.wait_ge(*SL.after(p, f"tu{LAST - 1}1"))
                    held(pe, passed_pe)
                    for h in range(H):
                        last = nc.tensor.matmul(z_[0][64:P, h * 64:h * 64 + 64], bT[0:64, b, h, 64:P], invs[0:64, 0, h], start=True, stop=True)
                    last.then_inc(*TL.done("zlast"))
                    pe.wait_ge(*VL.after(p, "jlast"))
                    held(pe, passed_pe)
                    for h in range(H):
                        last = nc.tensor.matmul(tu_[0][0:64, h * 64:h * 64 + 64], join[64:P, h], lastT[64:P, b, h, 64:P], start=True, stop=True)
                    last.then_inc(*TL.done("ulast"))

                def apply_state(c, b):
                    pe.wait_ge(*VC.after(c - 1, "o"))
                    for n, left in enumerate((kbT, qT)):
                        for h in range(H):
                            part = slice(C * (h % 2), C * (h % 2) + C)
                            last = nc.tensor.matmul(c_[:, h % 2, 4 * C * n + h // 2 * C:4 * C * n + (h // 2 + 1) * C], left[part, b, h // 2], state[part, h // 2], start=True, stop=True)
                    last.then_inc(*TC.done("kq"))

                def solve(c, b):
                    pe.wait_ge(*VC.after(c, "r"))
                    pe.wait_ge(*SL.after(c, "ulast"))
                    for h in range(H):
                        last = nc.tensor.matmul(c_[:, 0, h * C:(h + 1) * C], lastT[:, b, place(h)], r[:, h * C:(h + 1) * C], start=True, stop=True)
                    last.then_inc(*TC.done("d"))

                def update(c, b):
                    pe.wait_ge(*SC.after(c, "d"))
                    for h in range(H):
                        part = slice(C * (h % 2), C * (h % 2) + C)
                        last = nc.tensor.matmul(c_[part, 0, h // 2 * C:(h // 2 + 1) * C], kd[:, b, h * C:(h + 1) * C], dl[:, h * C:(h + 1) * C], start=True, stop=True)
                    last.then_inc(*TC.done("s"))
                    for h in range(H):
                        last = nc.tensor.matmul(c_[:, 1, h * C:(h + 1) * C], pm[:, b, place(h)], dl[:, h * C:(h + 1) * C], start=True, stop=True)
                    last.then_inc(*TC.done("o"))

                def turn(i, b, c):
                    first_level(c + 1, 1 - b)
                    apply_state(c, b)
                    level_z(c + 1, 1 - b, 1)
                    level_tu(c + 1, 1)
                    solve(c, b)
                    keys(c + 2, i + 1, b)
                    level_z(c + 1, 1 - b, 2)
                    level_tu(c + 1, 2)
                    update(c, b)
                    queries(c + 2, b)
                    level_z(c + 1, 1 - b, 3)
                    differences(c + 2)
                    level_tu(c + 1, 3)
                    key_grams(c + 2, b)
                    level_z(c + 1, 1 - b, 4)
                    level_tu(c + 1, 4)
                    query_grams(c + 2, b)
                    level_z(c + 1, 1 - b, 5)
                    level_tu(c + 1, 5)
                    last_level(c + 1, 1 - b)

                give_credit(pe, TE, TL, TC)
                for p in range(2):
                    keys(p, 0, p)
                    queries(p, p)
                    differences(p)
                    key_grams(p, p)
                    query_grams(p, p)
                    if p == 0:
                        first_level(0, 0)
                        for v in levels:
                            level_z(0, 0, v)
                            level_tu(0, v)
                        last_level(0, 0)
                with pe.Fori(0, NCH // 2) as i:
                    turn(i, 0, i * 2)
                    turn(i, 1, i * 2 + 1)


def combine(nc, k, a, d, keep):
    with ExitStack() as ctx:
        m = Mem(nc, ctx, "out")
        w = m.sb("w", [P, KC, DIM])
        onw = m.sb("onw", [P, C])
        col = m.sb("col", [TP, 2, 2, 1], I32)
        og = m.sb("og", [TP, 2, 2, DIM])
        gate = m.sb("gate", [TP, 2, DIM])
        x2 = m.sb("x2", [TP, 2, DIM])
        g2 = m.sb("g2", [TP, 2, DIM])
        c1 = m.sb("c1", [TP, 2, DIM])
        sq = m.sb("sq", [TP, DIM])
        ss = m.sb("ss", [TP, H])
        rn = m.sb("rn", [TP, 2, H])
        xT = m.sb("xT", [P, 2, KC, TP])
        y = m.sb("y", [TP, 2, DIM])
        p_t = [m.ps(f"p_t{b}") for b in range(2)]
        p_y = [m.ps(f"p_y{b}") for b in range(2)]
        weights = m.sem("weights")
        loads = m.moves("loads", 2)
        gathers = m.moves("gathers", 2)
        out = m.moves("out")
        L = m.steps("mixed", "first core")
        LS = m.steps("summed", "ss sseps")
        V = m.steps("vector", "norm gated y")
        GC = m.steps("columns", "col0 col1")
        G = m.steps("gpsimd", "g2 sq rn")
        S = m.steps("scalar", "xT")
        T = m.steps("tensor", "xT y")
        passed_pool = m.sem("passed_pool")
        passed_sp = m.sem("passed_sp")
        with nc.Block() as block:

            @block.sync
            def _(sp):
                sp.dma_start(w[:], a["L0_ffn_Wo"].rearrange("(c p) n -> p c n", p=P)).then_inc(weights, 16)
                sp.dma_start(onw[:], a["L0_ffn_o_norm_weight"].partition_broadcast(P)).then_inc(weights, 16)
                with sp.Fori(0, NT // 2) as i:
                    for b in range(2):
                        t = i * 2 + b
                        rows = bass.ds(t * TP, TP)
                        sp.wait_ge(*G.after(t - 2, "g2"))
                        held(sp, passed_sp)
                        sp.wait_ge(*V.after(t - 2, "y"))
                        sp.dma_start(gate[:, b], d["gate"][rows, :]).then_inc(*loads.done(b))
                        sp.dma_start(x2[:, b], d["x2"][rows, :]).then_inc(*loads.done(b))

            @block.gpsimd
            def _(pool):
                def gather(t, i, b):
                    pool.wait_ge(*gathers.after(i, b, 1))
                    for s in range(2):
                        nc.gpsimd.tensor_copy(col[:, b, s], keep["slot"][0:TP, s, bass.ds(t, 1)]).then_inc(*GC.done(f"col{s}"))
                    pool.wait_ge(*GC.after(t, "col1"))
                    pool.wait_ge(*L.after(t - 2, "core"))
                    held(pool, passed_pool)
                    for s in range(2):
                        nc.gpsimd.indirect_dma_start(out=og[:, b, s], out_offset=None, in_=d["o"][:, :], in_offset=bass.IndirectOffsetOnAxis(ap=col[:, b, s], axis=0)).then_inc(*gathers.done(b))

                def work(t, i, b):
                    pool.wait_ge(*loads.after(i, b))
                    pool.wait_ge(*V.after(t - 2, "gated"))
                    nc.gpsimd.tensor_tensor(heads(g2[:, b]), heads(gate[:, b]), over_h(onw[0:TP], H), ALU.mult).then_inc(*G.done("g2"))
                    pool.wait_ge(*L.after(t, "core"))
                    pool.wait_ge(*LS.after(t - 1, "ss"))
                    nc.gpsimd.tensor_tensor(sq[:], c1[:, b], c1[:, b], ALU.mult).then_inc(*G.done("sq"))
                    pool.wait_ge(*LS.after(t, "sseps"))
                    pool.wait_ge(*V.after(t - 2, "norm"))
                    nc.gpsimd.tensor_tensor(rn[:, b], ss[:], k["minus_half"][0:TP].to_broadcast([TP, H]), ALU.pow).then_inc(*G.done("rn"))

                give_credit(pool, G, GC)
                pool.wait_ge(weights, 32)
                gather(0, 0, 0)
                gather(1, 0, 1)
                work(0, 0, 0)
                with pool.Fori(0, NT // 2 - 1) as i:
                    gather(i * 2 + 2, i + 1, 0)
                    work(i * 2 + 1, i, 1)
                    gather(i * 2 + 3, i + 1, 1)
                    work(i * 2 + 2, i + 1, 0)
                work(NT - 1, NT // 2 - 1, 1)

            @block.vector
            def _(dve):
                def mix(t, i, b):
                    dve.wait_ge(*gathers.after(i, b))
                    dve.wait_ge(*T.after(t - 2, "xT"))
                    nc.vector.tensor_scalar(c1[:, b], og[:, b, 0], keep["slot_weight"][0:TP, 0, bass.ds(t, 1)], None, ALU.mult).then_inc(*L.done("first"))
                    dve.wait_ge(*L.after(t, "first"))
                    nc.vector.scalar_tensor_tensor(c1[:, b], og[:, b, 1], keep["slot_weight"][0:TP, 1, bass.ds(t, 1)], c1[:, b], ALU.mult, ALU.add).then_inc(*L.done("core"))

                def sums(t):
                    dve.wait_ge(*G.after(t, "sq"))
                    dve.wait_ge(*G.after(t - 1, "rn"))
                    nc.vector.tensor_reduce(ss[:], heads(sq[:]), AX.X, ALU.add).then_inc(*LS.done("ss"))
                    dve.wait_ge(*LS.after(t, "ss"))
                    nc.vector.tensor_scalar(ss[:], ss[:], 1.0 / C, LN_EPS, ALU.mult, ALU.add).then_inc(*LS.done("sseps"))

                def gated(t, b):
                    dve.wait_ge(*G.after(t, "rn"))
                    nc.vector.tensor_tensor(heads(c1[:, b]), heads(c1[:, b]), over_c(rn[:, b]), ALU.mult).then_inc(*V.done("norm"))
                    dve.wait_ge(*V.after(t, "norm"))
                    nc.vector.tensor_tensor(c1[:, b], c1[:, b], g2[:, b], ALU.mult).then_inc(*V.done("gated"))

                def residual(t, i, b):
                    dve.wait_ge(*T.after(t, "y"))
                    dve.wait_ge(*loads.after(i, b))
                    dve.wait_ge(*out.after(i, b, 1))
                    nc.vector.tensor_tensor(y[:, b], p_y[b][0:TP, :], x2[:, b], ALU.add).then_inc(*V.done("y"))

                def turn(t, i, b, i_next):
                    mix(t + 1, i_next, 1 - b)
                    gated(t, b)
                    sums(t + 1)
                    residual(t, i, b)

                give_credit(dve, V, L, LS)
                mix(0, 0, 0)
                sums(0)
                for i in turns(dve, NT // 2 - 1):
                    turn(i * 2, i, 0, i)
                    turn(i * 2 + 1, i, 1, i + 1)
                turn(NT - 2, NT // 2 - 1, 0, NT // 2 - 1)
                gated(NT - 1, 1)
                residual(NT - 1, NT // 2 - 1, 1)

            @block.tensor
            def _(pe):
                give_credit(pe, T)
                pe.wait_ge(weights, 32)
                with pe.Fori(0, NT // 2) as i:
                    for b in range(2):
                        t = i * 2 + b
                        pe.wait_ge(*V.after(t, "gated"))
                        pe.wait_ge(*S.after(t - 2, "xT"))
                        for c in range(KC):
                            last = nc.tensor.transpose(p_t[b][:, c * TP:(c + 1) * TP], c1[:, b, c * P:(c + 1) * P], k["ident"][0:TP, 0:TP])
                        last.then_inc(*T.done("xT"))
                        pe.wait_ge(*S.after(t, "xT"))
                        pe.wait_ge(*V.after(t - 2, "y"))
                        for c in range(KC):
                            last = nc.tensor.matmul(p_y[b][0:TP, :], xT[:, b, c], w[:, c], start=c == 0, stop=c == KC - 1)
                        last.then_inc(*T.done("y"))

            @block.scalar
            def _(act):
                give_credit(act, S)
                with act.Fori(0, NT // 2) as i:
                    for b in range(2):
                        t = i * 2 + b
                        act.wait_ge(*T.after(t, "xT"))
                        act.wait_ge(*T.after(t - 2, "y"))
                        nc.scalar.copy(xT[:, b].rearrange("p c t -> p (c t)"), p_t[b][:, 0:KC * TP]).then_inc(*S.done("xT"))
                        act.wait_ge(*V.after(t, "y"))
                        act.dma_start(a["out"][bass.ds(t * TP, TP), :], y[:, b]).then_inc(*out.done(b))
                for b in range(2):
                    act.wait_ge(*out.after(NT // 2 - 1, b))


def build(nc, a):
    def table(name, shape, dt=F32):
        return nc.dram_tensor(name, shape, dt, kind="Internal").ap()

    d = {
        "source": table("source", (N, SRC_W)), "state": table("state", (N + P, ST_W)),
        "skip": table("skip", (N, DIM)), "gat": table("gat", (N, DIM)), "x2": table("x2", (N, DIM)),
        "token": table("token", (N, TK_W)), "gate": table("gate", (N, DIM)),
        "table": table("table", (SLOTS + 4 * CH, 1), I32), "o": table("o", (SLOTS, DIM)),
    }
    with ExitStack() as ctx:
        m = Mem(nc, ctx, "all")
        k = constants(nc, m)
        keep = {
            "bn_scale": m.sb("bn_scale", [P, DIM]), "bn_shift": m.sb("bn_shift", [P, DIM]),
            "weight": m.sb("weight", [P, NE, NT]),
            "slot": m.sb("slot", [P, 2, NT], I32), "slot_weight": m.sb("slot_weight", [P, 2, NT]),
            "goes_on": m.sb("goes_on", [P, NCH + 4]),
        }
        project_nodes(nc, k, a, d)
        send_messages(nc, k, a, d)
        batch_norm(nc, k, a, d, keep)
        project_tokens(nc, k, a, d, keep)
        route(nc, k, a, d, keep)
        delta_rule(nc, k, a, d, keep)
        combine(nc, k, a, d, keep)


INS = {
    "x": (N, DIM), "src": (N,), "dst": (N,),
    "L0_gnn_W_gat": (DIM, DIM), "L0_gnn_att_src": (H, C), "L0_gnn_att_dst": (H, C), "L0_gnn_gat_bias": (DIM,),
    "L0_gnn_bn_gamma": (DIM,), "L0_gnn_bn_beta": (DIM,), "L0_gnn_W_skip": (DIM, DIM), "L0_gnn_b_skip": (DIM,),
    "L0_ffn_Wq": (DIM, DIM), "L0_ffn_Wgate": (DIM, NE), "L0_ffn_Wk": (DIM, DIM), "L0_ffn_Wv": (DIM, DIM),
    "L0_ffn_Wb": (DIM, H), "L0_ffn_Wa": (DIM, H), "L0_ffn_A_log": (H,), "L0_ffn_dt_bias": (H,),
    "L0_ffn_Wg": (DIM, DIM), "L0_ffn_o_norm_weight": (C,), "L0_ffn_Wo": (DIM, DIM),
}


def kernel(**inputs):
    import numpy as np
    import concourse.bacc as bacc
    from concourse.bass_utils import run_bass_kernel_spmd

    nc = bacc.Bacc("TRN2", target_bir_lowering=False, num_devices=1)
    a, arrays = {}, {}
    for name, shape in INS.items():
        arrays[name] = np.ascontiguousarray(inputs[name])
        a[name] = nc.dram_tensor(name, shape, I32 if name in ("src", "dst") else F32, kind="ExternalInput").ap()
    a["out"] = nc.dram_tensor("out", (N, DIM), F32, kind="ExternalOutput").ap()
    build(nc, a)
    r = run_bass_kernel_spmd(nc, [arrays], core_ids=[0])
    return r.results[0]["out"]
```

```python
import concourse.bass as bass
from concourse import mybir
from contextlib import ExitStack

F32 = mybir.dt.float32
BF16 = mybir.dt.bfloat16
I32 = mybir.dt.int32
ALU = mybir.AluOpType
ACT = mybir.ActivationFunctionType
AX = mybir.AxisListType

N = 10000
DIM = 512
H = 8
C = DIM // H
TP = 125
NT = N // TP
TR = 32
KC = DIM // 128
P = 128
NE = 4
CH = 128
NCH = 2 * N // CH + NE
SLOTS = NCH * CH
NEG_SLOPE = 0.2
BN_EPS = 1e-5
LN_EPS = 1e-5
FAR = 1e30
G_FLOOR = -104.0

ST_DEN, ST_MAX, ST_DST, ST_W = DIM, DIM + H, DIM + 2 * H, DIM + 3 * H
SRC_W = H + DIM
TK_K, TK_V, TK_B, TK_NB, TK_G = DIM, 2 * DIM, 3 * DIM, 3 * DIM + H, 3 * DIM + 2 * H
TK_W = 3 * DIM + 3 * H


class Steps:

    def __init__(self, sem, names, lag=2):
        self.sem, self.names, self.lag, self.written = sem, names.split(), lag, 0
        assert len(set(self.names)) == len(self.names)

    @property
    def credit(self):
        return self.lag * len(self.names)

    def after(self, turn, name):
        k = len(self.names)
        return self.sem, (turn + self.lag) * k + self.names.index(name) + 1

    def done(self, name):
        assert name == self.names[self.written % len(self.names)], name
        self.written += 1
        return self.sem, 1


class Moves:

    def __init__(self, sems, each=1):
        self.sems, self.each = sems, each

    def after(self, pair, buf, back=0):
        return self.sems[buf], (pair + 1 - back) * 16 * self.each

    def done(self, buf):
        return self.sems[buf], 16


class Mem:

    def __init__(self, nc, ctx, tag):
        self.nc, self.ctx, self.tag = nc, ctx, tag

    def sb(self, name, shape, dt=F32):
        return self.ctx.enter_context(self.nc.sbuf_tensor(f"{self.tag}_{name}", shape, dt))

    def ps(self, name, shape=(P, 512), dt=F32):
        return self.ctx.enter_context(self.nc.psum_tensor(f"{self.tag}_{name}", list(shape), dt))

    def sem(self, name):
        return self.ctx.enter_context(self.nc.semaphore(f"{self.tag}_{name}"))

    def steps(self, name, names):
        return Steps(self.sem(name), names)

    def moves(self, name, each=1):
        return Moves([self.sem(f"{name}{b}") for b in range(2)], each)


def give_credit(eng, *counts):
    for c in counts:
        eng.sem_inc(c.sem, c.credit)


def turns(eng, n):
    yield 0
    with eng.Fori(1, n) as i:
        yield i


def held(eng, passed):
    eng.sem_inc(passed, 1)


def heads(ap, n=H):
    return ap.rearrange("p (h c) -> p h c", h=n)


def over_c(ap, c=C):
    return ap.unsqueeze(2).to_broadcast([ap.shape[0], ap.shape[1], c])


def over_h(ap, n):
    return ap.unsqueeze(1).to_broadcast([ap.shape[0], n, ap.shape[1]])


def constants(nc, m):
    k = {
        "ident": m.sb("ident", [P, P]),
        "identb": m.sb("identb", [P, P], BF16),
        "at_or_after": m.sb("at_or_after", [P, P]),
        "before": m.sb("before", [P, P]),
        "after": m.sb("after", [P, P]),
        "hide": m.sb("hide", [P, P], BF16),
        "ones": m.sb("ones", [P, P]),
        "minus_half": m.sb("minus_half", [P, 1]),
        "zeros": m.sb("zeros", [P, ST_W]),
        "pairs": m.sb("pairs", [P, P]),
        "merge": m.sb("merge", [P, 5, P]),
        "dump": m.sb("dump", [P, 1]),
        "dumpslot": m.sb("dumpslot", [P, 1]),
        "chunk_no": m.sb("chunk_no", [P, NCH + 4]),
    }
    made = m.sem("constants_made")
    with nc.Block() as block:

        @block.gpsimd
        def _(pool):
            step = [0]

            def then(ins):
                step[0] += 1
                ins.then_inc(made, 1)
                pool.wait_ge(made, step[0])

            for name in ("ident", "at_or_after", "before", "after", "ones"):
                nc.gpsimd.memset(k[name][:], 1.0)
            nc.gpsimd.memset(k["minus_half"][:], -0.5)
            nc.gpsimd.memset(k["hide"][:], 0.0)
            nc.gpsimd.memset(k["merge"][:], 0.0)
            nc.gpsimd.memset(k["pairs"][:], 0.0)
            then(nc.gpsimd.memset(k["zeros"][:], 0.0))
            row = [[1, P]]
            nc.gpsimd.affine_select(out=k["ident"][:], in_=k["ident"][:], pattern=row, compare_op=ALU.is_equal, fill=0.0, base=0, channel_multiplier=-1)
            nc.gpsimd.affine_select(out=k["at_or_after"][:], in_=k["at_or_after"][:], pattern=row, compare_op=ALU.is_ge, fill=0.0, base=0, channel_multiplier=-1)
            nc.gpsimd.affine_select(out=k["after"][:], in_=k["after"][:], pattern=row, compare_op=ALU.is_gt, fill=0.0, base=0, channel_multiplier=-1)
            nc.gpsimd.affine_select(out=k["hide"][:], in_=k["hide"][:], pattern=row, compare_op=ALU.is_ge, fill=-30000.0, base=0, channel_multiplier=-1)
            nc.gpsimd.iota(k["dump"][:], [[0, 1]], base=N, channel_multiplier=1, allow_small_or_imprecise_dtypes=True)
            nc.gpsimd.iota(k["dumpslot"][:], [[0, 1]], base=SLOTS, channel_multiplier=1, allow_small_or_imprecise_dtypes=True)
            nc.gpsimd.iota(k["chunk_no"][:], [[1, NCH + 4]], base=0, channel_multiplier=0, allow_small_or_imprecise_dtypes=True)
            then(nc.gpsimd.affine_select(out=k["before"][:], in_=k["before"][:], pattern=[[-1, P]], compare_op=ALU.is_gt, fill=0.0, base=0, channel_multiplier=1))
            then(nc.gpsimd.tensor_copy(k["identb"][:], k["ident"][:]))
            for lv in range(5):
                b = 1 << lv
                cols = k["merge"][:, lv, :].rearrange("p (m r) -> p m r", r=2 * b)[:, :, b:2 * b]
                pairs = P // (2 * b)
                then(nc.gpsimd.memset(cols, 1.0))
                then(nc.gpsimd.affine_select(out=cols, in_=cols, pattern=[[-2 * b, pairs], [0, b]], compare_op=ALU.is_ge, fill=0.0, base=0, channel_multiplier=1))
                then(nc.gpsimd.affine_select(out=cols, in_=cols, pattern=[[2 * b, pairs], [0, b]], compare_op=ALU.is_ge, fill=0.0, base=b - 1, channel_multiplier=-1))
                then(nc.gpsimd.tensor_tensor(k["merge"][:, lv, :], k["merge"][:, lv, :], k["ident"][:], ALU.add))
            evencols = k["pairs"][:].rearrange("p (m r) -> p m r", r=2)[:, :, 0:1]
            then(nc.gpsimd.memset(evencols, 1.0))
            then(nc.gpsimd.affine_select(out=evencols, in_=evencols, pattern=[[-2, P // 2], [0, 1]], compare_op=ALU.is_equal, fill=0.0, base=-1, channel_multiplier=1))
            then(nc.gpsimd.tensor_tensor(k["pairs"][:], k["pairs"][:], k["ident"][:], ALU.add))
    return k


def project_nodes(nc, k, a, d):
    with ExitStack() as ctx:
        m = Mem(nc, ctx, "nodes")
        w = m.sb("w", [P, 2, KC, DIM])
        att = m.sb("att", [P, 2, DIM])
        bskip = m.sb("bskip", [P, DIM])
        x = m.sb("x", [TP, 2, DIM])
        xn = m.sb("xn", [TP, 2, DIM])
        xT = m.sb("xT", [P, 2, KC, TP])
        row = m.sb("row", [TP, 2, H + ST_W])
        skip = m.sb("skip", [TP, 2, DIM])
        prod = m.sb("prod", [TP, 2, DIM])
        stats = m.sb("stats", [TP, 2, 6])
        mv = m.sb("mv", [TP, 2, 2])
        veps = m.sb("veps", [TP, 2, 1])
        rstd = m.sb("rstd", [TP, 2, 1])
        asum = m.sb("asum", [TP, 2, H])
        p_t = [m.ps(f"p_t{b}") for b in range(2)]
        p_h = [m.ps(f"p_h{b}") for b in range(2)]
        p_s = [m.ps(f"p_s{b}") for b in range(2)]
        weights = m.sem("weights")
        x_in = m.moves("x_in")
        out = m.moves("out", 3)
        unused = m.sem("unused")
        LN = m.steps("norm", "stats aggr xn")
        V = m.steps("vector", "skip psrc pdst asrc adst den sum max")
        G = m.steps("gpsimd", "veps rstd")
        S = m.steps("scalar", "xT h")
        T = m.steps("tensor", "xT h skip")
        passed_dve = m.sem("passed_dve")
        passed_pool = m.sem("passed_pool")
        with nc.Block() as block:

            @block.sync
            def _(sp):
                sp.dma_start(w[:, 0], a["L0_gnn_W_gat"].rearrange("(c p) n -> p c n", p=P)).then_inc(weights, 16)
                sp.dma_start(w[:, 1], a["L0_gnn_W_skip"].rearrange("(c p) n -> p c n", p=P)).then_inc(weights, 16)
                sp.dma_start(att[:, 0], a["L0_gnn_att_src"].rearrange("h c -> (h c)").partition_broadcast(P)).then_inc(weights, 16)
                sp.dma_start(att[:, 1], a["L0_gnn_att_dst"].rearrange("h c -> (h c)").partition_broadcast(P)).then_inc(weights, 16)
                sp.dma_start(bskip[:], a["L0_gnn_b_skip"].partition_broadcast(P)).then_inc(weights, 16)
                with sp.Fori(0, NT // 2) as i:
                    for b in range(2):
                        t = i * 2 + b
                        sp.wait_ge(*LN.after(t - 2, "xn"))
                        sp.dma_start(x[:, b], a["x"][bass.ds(t * TP, TP), :]).then_inc(*x_in.done(b))
                sp.dma_start(d["state"][N:N + P, :], k["zeros"][:]).then_inc(unused, 16)
                sp.wait_ge(unused, 16)

            def norm(t, i, b, dve):
                dve.wait_ge(*x_in.after(i, b))
                nc.vector.bn_stats(stats[:, b], x[:, b]).then_inc(*LN.done("stats"))
                dve.wait_ge(*LN.after(t, "stats"))
                held(dve, passed_dve)
                nc.vector.bn_aggr(mv[:, b], stats[:, b]).then_inc(*LN.done("aggr"))
                dve.wait_ge(*G.after(t, "rstd"))
                dve.wait_ge(*T.after(t - 2, "xT"))
                nc.vector.tensor_scalar(xn[:, b], x[:, b], mv[:, b, 0:1], rstd[:, b], ALU.subtract, ALU.mult).then_inc(*LN.done("xn"))

            def scores(t, i, b, dve):
                dve.wait_ge(*T.after(t, "skip"))
                dve.wait_ge(*out.after(i, b, 1))
                nc.vector.tensor_tensor(skip[:, b], p_s[b][0:TP, :], bskip[0:TP, :], ALU.add).then_inc(*V.done("skip"))
                dve.wait_ge(*S.after(t, "h"))
                nc.vector.tensor_tensor(prod[:, 0], row[:, b, H:H + DIM], att[0:TP, 0], ALU.mult).then_inc(*V.done("psrc"))
                nc.vector.tensor_tensor(prod[:, 1], row[:, b, H:H + DIM], att[0:TP, 1], ALU.mult).then_inc(*V.done("pdst"))
                dve.wait_ge(*V.after(t, "psrc"))
                nc.vector.tensor_reduce(row[:, b, 0:H], heads(prod[:, 0]), AX.X, ALU.add).then_inc(*V.done("asrc"))
                dve.wait_ge(*V.after(t, "pdst"))
                nc.vector.tensor_reduce(row[:, b, H + ST_DST:H + ST_W], heads(prod[:, 1]), AX.X, ALU.add).then_inc(*V.done("adst"))
                nc.vector.memset(row[:, b, H + ST_DEN:H + ST_MAX], 1.0).then_inc(*V.done("den"))
                dve.wait_ge(*V.after(t, "adst"))
                nc.vector.tensor_tensor(asum[:, b], row[:, b, 0:H], row[:, b, H + ST_DST:H + ST_W], ALU.add).then_inc(*V.done("sum"))
                dve.wait_ge(*V.after(t, "sum"))
                nc.vector.scalar_tensor_tensor(row[:, b, H + ST_MAX:H + ST_DST], asum[:, b], NEG_SLOPE, asum[:, b], ALU.mult, ALU.max).then_inc(*V.done("max"))

            @block.vector
            def _(dve):
                give_credit(dve, V, LN)
                dve.wait_ge(weights, 80)
                norm(0, 0, 0, dve)
                for i in turns(dve, NT // 2 - 1):
                    norm(i * 2 + 1, i, 1, dve)
                    scores(i * 2, i, 0, dve)
                    norm(i * 2 + 2, i + 1, 0, dve)
                    scores(i * 2 + 1, i, 1, dve)
                norm(NT - 1, NT // 2 - 1, 1, dve)
                scores(NT - 2, NT // 2 - 1, 0, dve)
                scores(NT - 1, NT // 2 - 1, 1, dve)

            @block.tensor
            def _(pe):
                give_credit(pe, T)
                pe.wait_ge(weights, 80)
                with pe.Fori(0, NT // 2) as i:
                    for b in range(2):
                        t = i * 2 + b
                        pe.wait_ge(*LN.after(t, "xn"))
                        pe.wait_ge(*S.after(t - 2, "xT"))
                        for c in range(KC):
                            last = nc.tensor.transpose(p_t[b][:, c * TP:(c + 1) * TP], xn[:, b, c * P:(c + 1) * P], k["ident"][0:TP, 0:TP])
                        last.then_inc(*T.done("xT"))
                        pe.wait_ge(*S.after(t, "xT"))
                        pe.wait_ge(*S.after(t - 2, "h"))
                        for c in range(KC):
                            last = nc.tensor.matmul(p_h[b][0:TP, :], xT[:, b, c], w[:, 0, c], start=c == 0, stop=c == KC - 1)
                        last.then_inc(*T.done("h"))
                        pe.wait_ge(*V.after(t - 2, "skip"))
                        for c in range(KC):
                            last = nc.tensor.matmul(p_s[b][0:TP, :], xT[:, b, c], w[:, 1, c], start=c == 0, stop=c == KC - 1)
                        last.then_inc(*T.done("skip"))

            @block.scalar
            def _(act):
                give_credit(act, S)
                for i in turns(act, NT // 2):
                    for b in range(2):
                        t = i * 2 + b
                        act.wait_ge(*T.after(t, "xT"))
                        act.wait_ge(*T.after(t - 2, "skip"))
                        nc.scalar.copy(xT[:, b].rearrange("p c t -> p (c t)"), p_t[b][:, 0:KC * TP]).then_inc(*S.done("xT"))
                        act.wait_ge(*T.after(t, "h"))
                        act.wait_ge(*out.after(i, b, 1))
                        act.wait_ge(*V.after(t - 2, "pdst"))
                        nc.scalar.copy(row[:, b, H:H + DIM], p_h[b][0:TP, :]).then_inc(*S.done("h"))

            def root(t, b, pool):
                pool.wait_ge(*LN.after(t, "aggr"))
                held(pool, passed_pool)
                nc.gpsimd.tensor_scalar(veps[:, b], mv[:, b, 1:2], LN_EPS, None, ALU.add).then_inc(*G.done("veps"))
                pool.wait_ge(*G.after(t, "veps"))
                pool.wait_ge(*LN.after(t - 2, "xn"))
                nc.gpsimd.tensor_tensor(rstd[:, b], veps[:, b], k["minus_half"][0:TP, 0:1], ALU.pow).then_inc(*G.done("rstd"))

            def store(t, b, pool):
                pool.wait_ge(*V.after(t, "max"))
                rows = bass.ds(t * TP, TP)
                pool.dma_start(d["source"][rows, :], row[:, b, 0:SRC_W]).then_inc(*out.done(b))
                pool.dma_start(d["state"][rows, :], row[:, b, H:H + ST_W]).then_inc(*out.done(b))
                pool.dma_start(d["skip"][rows, :], skip[:, b]).then_inc(*out.done(b))

            @block.gpsimd
            def _(pool):
                give_credit(pool, G)
                root(0, 0, pool)
                with pool.Fori(0, NT // 2 - 1) as i:
                    root(i * 2 + 1, 1, pool)
                    store(i * 2, 0, pool)
                    root(i * 2 + 2, 0, pool)
                    store(i * 2 + 1, 1, pool)
                root(NT - 1, 1, pool)
                store(NT - 2, 0, pool)
                store(NT - 1, 1, pool)
                for b in range(2):
                    pool.wait_ge(*out.after(NT // 2 - 1, b))


def send_messages(nc, k, a, d):
    with ExitStack() as ctx:
        m = Mem(nc, ctx, "edges")
        src = m.sb("src", [TP, 2, 1], I32)
        dst = m.sb("dst", [TP, 2, 1], I32)
        dstrow = m.sb("dstrow", [TP, 2, TP], I32)
        dstf = m.sb("dstf", [TP, 2, 1])
        same = m.sb("same", [TP, 2, TP])
        far = m.sb("far", [TP, 2, TP], BF16)
        earlier = m.sb("earlier", [TP, TP])
        dup = m.sb("dup", [TP, 1])
        first = m.sb("first", [TP, 1])
        off = m.sb("off", [TP, 1])
        target = m.sb("target", [TP, 2, 1], I32)
        hs = m.sb("hs", [TP, 2, SRC_W])
        st = m.sb("st", [TP, ST_W])
        new = m.sb("new", [TP, ST_W])
        e0 = m.sb("e0", [TP, H])
        e = m.sb("e", [TP, H])
        tmax = m.sb("tmax", [TP, H])
        diff = m.sb("diff", [TP, 2, H])
        scale = m.sb("scale", [TP, H])
        pay = m.sb("pay", [TP, DIM + H])
        p_e = m.ps("p_e", [P, 2, 512])
        p_m = m.ps("p_m", [P, 2, 512])
        idx_in = m.moves("idx_in", 3)
        hs_in = m.moves("hs_in")
        st_in = m.moves("st_in")
        st_out = m.moves("st_out")
        V = m.steps("vector", "dstf same far earlier dup first off target e0 e tmax0 tmax1 max dnew dold pay0 pay1 adst acc den acc20 acc21 den2")
        S = m.steps("scalar", "ex scale")
        T = m.steps("tensor", "far e0 e1 sum0 sum1")
        passed_pool = m.sem("passed_pool")
        passed_sp = m.sem("passed_sp")
        with nc.Block() as block:

            @block.sync
            def _(sp):
                for i in turns(sp, NT // 2):
                    for b in range(2):
                        t = i * 2 + b
                        sp.wait_ge(*V.after(t - 2, "target"))
                        held(sp, passed_sp)
                        sp.wait_ge(*hs_in.after(i, b, 1))
                        sp.wait_ge(*st_in.after(i, b, 1))
                        sp.dma_start(src[:, b], a["src"][bass.ds(t * TP, TP)].unsqueeze(1)).then_inc(*idx_in.done(b))
                        sp.dma_start(dst[:, b], a["dst"][bass.ds(t * TP, TP)].unsqueeze(1)).then_inc(*idx_in.done(b))
                        sp.dma_start(dstrow[:, b], a["dst"][bass.ds(t * TP, TP)].partition_broadcast(TP)).then_inc(*idx_in.done(b))

            @block.gpsimd
            def _(pool):
                for i in turns(pool, NT // 2):
                    for b in range(2):
                        t = i * 2 + b
                        pool.wait_ge(*idx_in.after(i, b))
                        pool.wait_ge(*V.after(t - 2, "pay1"))
                        held(pool, passed_pool)
                        nc.gpsimd.indirect_dma_start(out=hs[:, b], out_offset=None, in_=d["source"][:, :], in_offset=bass.IndirectOffsetOnAxis(ap=src[:, b], axis=0)).then_inc(*hs_in.done(b))
                        pool.wait_ge(*(st_out.after(i, 0) if b else st_out.after(i, 1, 1)))
                        pool.wait_ge(*V.after(t - 1, "den"))
                        held(pool, passed_pool)
                        nc.gpsimd.indirect_dma_start(out=st[:], out_offset=None, in_=d["state"][:, :], in_offset=bass.IndirectOffsetOnAxis(ap=dst[:, b], axis=0)).then_inc(*st_in.done(b))
                        pool.wait_ge(*V.after(t, "den2"))
                        held(pool, passed_pool)
                        nc.gpsimd.indirect_dma_start(out=d["state"][:, :], out_offset=bass.IndirectOffsetOnAxis(ap=target[:, b], axis=0), in_=new[:], in_offset=None).then_inc(*st_out.done(b))
                for b in range(2):
                    pool.wait_ge(*st_out.after(NT // 2 - 1, b))

            @block.vector
            def _(dve):
                give_credit(dve, V)
                for i in turns(dve, NT // 2):
                    for b in range(2):
                        t = i * 2 + b
                        dve.wait_ge(*idx_in.after(i, b))
                        nc.vector.tensor_copy(dstf[:, b], dst[:, b]).then_inc(*V.done("dstf"))
                        dve.wait_ge(*V.after(t, "dstf"))
                        dve.wait_ge(*T.after(t - 2, "sum1"))
                        nc.vector.tensor_scalar(same[:, b], dstrow[:, b], dstf[:, b], None, ALU.is_equal).then_inc(*V.done("same"))
                        dve.wait_ge(*V.after(t, "same"))
                        dve.wait_ge(*T.after(t - 2, "far"))
                        nc.vector.tensor_scalar(far[:, b], same[:, b], FAR, -FAR, ALU.mult, ALU.add).then_inc(*V.done("far"))
                        nc.vector.tensor_tensor(earlier[:], same[:, b], k["before"][0:TP, 0:TP], ALU.mult).then_inc(*V.done("earlier"))
                        dve.wait_ge(*V.after(t, "earlier"))
                        nc.vector.reduce_sum(dup[:], earlier[:], AX.X).then_inc(*V.done("dup"))
                        dve.wait_ge(*V.after(t, "dup"))
                        nc.vector.tensor_scalar(first[:], dup[:], 0.0, None, ALU.is_equal).then_inc(*V.done("first"))
                        nc.vector.tensor_tensor(off[:], dstf[:, b], k["dump"][0:TP], ALU.subtract).then_inc(*V.done("off"))
                        dve.wait_ge(*V.after(t, "off"))
                        dve.wait_ge(*st_out.after(i, b, 1))
                        nc.vector.scalar_tensor_tensor(target[:, b], off[:], first[:], k["dump"][0:TP], ALU.mult, ALU.add).then_inc(*V.done("target"))
                        dve.wait_ge(*hs_in.after(i, b))
                        dve.wait_ge(*st_in.after(i, b))
                        nc.vector.tensor_tensor(e0[:], hs[:, b, 0:H], st[:, ST_DST:ST_W], ALU.add).then_inc(*V.done("e0"))
                        dve.wait_ge(*V.after(t, "e0"))
                        nc.vector.scalar_tensor_tensor(e[:], e0[:], NEG_SLOPE, e0[:], ALU.mult, ALU.max).then_inc(*V.done("e"))
                        for g in range(2):
                            dve.wait_ge(*T.after(t, f"e{g}"))
                            nc.vector.tensor_reduce(tmax[:, 4 * g:4 * g + 4], p_e[0:TP, g, 0:4 * TP].rearrange("p (h j) -> p h j", h=4), AX.X, ALU.max).then_inc(*V.done(f"tmax{g}"))
                        dve.wait_ge(*V.after(t, "tmax1"))
                        dve.wait_ge(*(st_out.after(i, 0) if b else st_out.after(i, 1, 1)))
                        nc.vector.tensor_tensor(new[:, ST_MAX:ST_DST], st[:, ST_MAX:ST_DST], tmax[:], ALU.max).then_inc(*V.done("max"))
                        dve.wait_ge(*V.after(t, "max"))
                        dve.wait_ge(*S.after(t - 1, "scale"))
                        nc.vector.tensor_tensor(diff[:, 0], e[:], new[:, ST_MAX:ST_DST], ALU.subtract).then_inc(*V.done("dnew"))
                        nc.vector.tensor_tensor(diff[:, 1], st[:, ST_MAX:ST_DST], new[:, ST_MAX:ST_DST], ALU.subtract).then_inc(*V.done("dold"))
                        dve.wait_ge(*S.after(t, "ex"))
                        for g in range(2):
                            cols = slice(4 * C * g, 4 * C * g + 4 * C)
                            nc.vector.tensor_tensor(heads(pay[:, cols], 4), heads(hs[:, b, H + 4 * C * g:H + 4 * C * g + 4 * C], 4), over_c(pay[:, DIM + 4 * g:DIM + 4 * g + 4]), ALU.mult).then_inc(*V.done(f"pay{g}"))
                        nc.vector.tensor_copy(new[:, ST_DST:ST_W], st[:, ST_DST:ST_W]).then_inc(*V.done("adst"))
                        dve.wait_ge(*S.after(t, "scale"))
                        nc.vector.tensor_tensor(heads(new[:, 0:DIM]), heads(st[:, 0:DIM]), over_c(scale[:]), ALU.mult).then_inc(*V.done("acc"))
                        nc.vector.tensor_tensor(new[:, ST_DEN:ST_MAX], st[:, ST_DEN:ST_MAX], scale[:], ALU.mult).then_inc(*V.done("den"))
                        dve.wait_ge(*V.after(t, "den"))
                        for g in range(2):
                            cols = slice(4 * C * g, 4 * C * g + 4 * C)
                            dve.wait_ge(*T.after(t, f"sum{g}"))
                            nc.vector.tensor_tensor(new[:, cols], new[:, cols], p_m[0:TP, g, 0:4 * C], ALU.add).then_inc(*V.done(f"acc2{g}"))
                        nc.vector.tensor_tensor(new[:, ST_DEN:ST_MAX], new[:, ST_DEN:ST_MAX], p_m[0:TP, 1, 4 * C:4 * C + H], ALU.add).then_inc(*V.done("den2"))

            @block.scalar
            def _(act):
                give_credit(act, S)
                with act.Fori(0, NT // 2) as i:
                    for b in range(2):
                        t = i * 2 + b
                        act.wait_ge(*V.after(t, "dold"))
                        act.wait_ge(*T.after(t - 1, "sum1"))
                        nc.scalar.activation(pay[:, DIM:DIM + H], diff[:, 0], ACT.Exp).then_inc(*S.done("ex"))
                        act.wait_ge(*V.after(t - 1, "den"))
                        nc.scalar.activation(scale[:], diff[:, 1], ACT.Exp).then_inc(*S.done("scale"))

            @block.tensor
            def _(pe):
                give_credit(pe, T)
                with pe.Fori(0, NT // 2) as i:
                    for b in range(2):
                        t = i * 2 + b
                        pe.wait_ge(*V.after(t, "far"))
                        pe.wait_ge(*V.after(t - 1, "tmax1"))
                        for g in range(2):
                            last = nc.tensor.matmul(p_e[0:TP, g, 0:4 * TP].rearrange("p (h j) -> p h j", h=4), k["identb"][0:TP, 0:TP], over_h(far[:, b], 4), start=True, stop=False)
                        last.then_inc(*T.done("far"))
                        pe.wait_ge(*V.after(t, "e"))
                        for g in range(2):
                            for h in range(4):
                                last = nc.tensor.matmul(p_e[0:TP, g, h * TP:(h + 1) * TP], e[:, 4 * g + h:4 * g + h + 1].to_broadcast([TP, TP]),
                                                        k["ident"][0:TP, 0:TP], start=False, stop=h == 3)
                            last.then_inc(*T.done(f"e{g}"))
                        pe.wait_ge(*V.after(t - 1, "den2"))
                        for g in range(2):
                            pe.wait_ge(*V.after(t, f"pay{g}"))
                            last = nc.tensor.matmul(p_m[0:TP, g, 0:4 * C], same[:, b], pay[:, 4 * C * g:4 * C * g + 4 * C], start=True, stop=True)
                            if g == 1:
                                last = nc.tensor.matmul(p_m[0:TP, g, 4 * C:4 * C + H], same[:, b], pay[:, DIM:DIM + H], start=True, stop=True)
                            last.then_inc(*T.done(f"sum{g}"))


def batch_norm(nc, k, a, d, keep):
    with ExitStack() as ctx:
        m = Mem(nc, ctx, "bn")
        bias = m.sb("bias", [P, DIM])
        gamma = m.sb("gamma", [P, DIM])
        beta = m.sb("beta", [P, DIM])
        st = m.sb("st", [TP, 2, ST_MAX])
        rden = m.sb("rden", [TP, 2, H])
        o = m.sb("o", [TP, 2, DIM])
        sq = m.sb("sq", [TP, 2, DIM])
        ob = m.sb("ob", [TP, 2, DIM])
        mean = m.sb("mean", [P, DIM])
        meansq = m.sb("meansq", [P, DIM])
        var = m.sb("var", [P, DIM])
        p_s = m.ps("p_s")
        p_q = m.ps("p_q")
        weights = m.sem("weights")
        end = m.sem("end")
        root = m.sem("root")
        st_in = m.moves("st_in")
        out = m.moves("out")
        V = m.steps("vector", "rden o ob")
        S = m.steps("scalar", "sq")
        T = m.steps("tensor", "sum sumsq")
        with nc.Block() as block:

            @block.sync
            def _(sp):
                sp.dma_start(bias[:], a["L0_gnn_gat_bias"].partition_broadcast(P)).then_inc(weights, 16)
                sp.dma_start(gamma[:], a["L0_gnn_bn_gamma"].partition_broadcast(P)).then_inc(weights, 16)
                sp.dma_start(beta[:], a["L0_gnn_bn_beta"].partition_broadcast(P)).then_inc(weights, 16)
                with sp.Fori(0, NT // 2) as i:
                    for b in range(2):
                        t = i * 2 + b
                        sp.wait_ge(*V.after(t - 2, "o"))
                        sp.dma_start(st[:, b], d["state"][bass.ds(t * TP, TP), 0:ST_MAX]).then_inc(*st_in.done(b))

            @block.vector
            def _(dve):
                give_credit(dve, V)
                dve.wait_ge(weights, 48)
                for i in turns(dve, NT // 2):
                    for b in range(2):
                        t = i * 2 + b
                        dve.wait_ge(*st_in.after(i, b))
                        nc.vector.reciprocal(rden[:, b], st[:, b, ST_DEN:ST_MAX]).then_inc(*V.done("rden"))
                        dve.wait_ge(*V.after(t, "rden"))
                        dve.wait_ge(*T.after(t - 2, "sum"))
                        dve.wait_ge(*S.after(t - 2, "sq"))
                        nc.vector.tensor_tensor(heads(o[:, b]), heads(st[:, b, 0:DIM]), over_c(rden[:, b]), ALU.mult).then_inc(*V.done("o"))
                        dve.wait_ge(*V.after(t, "o"))
                        dve.wait_ge(*out.after(i, b, 1))
                        nc.vector.tensor_tensor(ob[:, b], o[:, b], bias[0:TP], ALU.add).then_inc(*V.done("ob"))
                dve.wait_ge(end, 1)
                step = [1]

                def then(ins):
                    step[0] += 1
                    ins.then_inc(end, 1)
                    dve.wait_ge(end, step[0])

                then(nc.vector.tensor_scalar(mean[:], p_s[:], 1.0 / N, None, ALU.mult))
                then(nc.vector.tensor_tensor(meansq[:], mean[:], mean[:], ALU.mult))
                then(nc.vector.scalar_tensor_tensor(var[:], p_q[:], 1.0 / N, meansq[:], ALU.mult, ALU.subtract))
                then(nc.vector.tensor_scalar(var[:], var[:], 0.0, BN_EPS, ALU.max, ALU.add))
                dve.wait_ge(root, 1)
                then(nc.vector.reciprocal(var[:], var[:]))
                then(nc.vector.tensor_tensor(keep["bn_scale"][:], var[:], gamma[:], ALU.mult))
                then(nc.vector.tensor_tensor(mean[:], mean[:], bias[:], ALU.add))
                then(nc.vector.tensor_tensor(mean[:], mean[:], keep["bn_scale"][:], ALU.mult))
                then(nc.vector.tensor_tensor(keep["bn_shift"][:], beta[:], mean[:], ALU.subtract))

            @block.scalar
            def _(act):
                give_credit(act, S)
                with act.Fori(0, NT // 2) as i:
                    for b in range(2):
                        t = i * 2 + b
                        act.wait_ge(*V.after(t, "o"))
                        act.wait_ge(*T.after(t - 2, "sumsq"))
                        nc.scalar.activation(sq[:, b], o[:, b], ACT.Square).then_inc(*S.done("sq"))
                act.wait_ge(end, 5)
                nc.scalar.activation(var[:], var[:], ACT.Sqrt).then_inc(root, 1)

            @block.tensor
            def _(pe):
                give_credit(pe, T)
                nc.tensor.matmul(p_s[:], k["zeros"][:, 0:P], k["zeros"][:, 0:DIM], start=True, stop=False)
                nc.tensor.matmul(p_q[:], k["zeros"][:, 0:P], k["zeros"][:, 0:DIM], start=True, stop=False)
                with pe.Fori(0, NT // 2) as i:
                    for b in range(2):
                        t = i * 2 + b
                        pe.wait_ge(*V.after(t, "o"))
                        nc.tensor.matmul(p_s[:], k["ones"][0:TP, :], o[:, b], start=False, stop=False).then_inc(*T.done("sum"))
                        pe.wait_ge(*S.after(t, "sq"))
                        nc.tensor.matmul(p_q[:], k["ones"][0:TP, :], sq[:, b], start=False, stop=False).then_inc(*T.done("sumsq"))
                nc.tensor.matmul(p_s[:], k["zeros"][:, 0:P], k["zeros"][:, 0:DIM], start=False, stop=True)
                nc.tensor.matmul(p_q[:], k["zeros"][:, 0:P], k["zeros"][:, 0:DIM], start=False, stop=True).then_inc(end, 1)

            @block.gpsimd
            def _(pool):
                with pool.Fori(0, NT // 2) as i:
                    for b in range(2):
                        t = i * 2 + b
                        pool.wait_ge(*V.after(t, "ob"))
                        pool.dma_start(d["gat"][bass.ds(t * TP, TP), :], ob[:, b]).then_inc(*out.done(b))
                for b in range(2):
                    pool.wait_ge(*out.after(NT // 2 - 1, b))


def project_tokens(nc, k, a, d, keep):
    ZW = NE + 2 * H
    with ExitStack() as ctx:
        m = Mem(nc, ctx, "tokens")
        w = m.sb("w", [P, 4, KC, DIM])
        wz = m.sb("wz", [P, KC, ZW])
        decay = m.sb("decay", [P, H])
        dtb = m.sb("dtb", [P, H])
        tie = m.sb("tie", [P, NE, NE])
        gat = m.sb("gat", [TP, 2, DIM])
        xin = m.sb("xin", [TP, 2, DIM])
        skip = m.sb("skip", [TP, 2, DIM])
        res = m.sb("res", [TP, DIM])
        y = m.sb("y", [TP, DIM])
        gl = m.sb("gl", [TP, DIM])
        x2 = m.sb("x2", [TP, 2, DIM])
        stats = m.sb("stats", [TP, 6])
        mv = m.sb("mv", [TP, 2])
        veps = m.sb("veps", [TP, 1])
        rstd = m.sb("rstd", [TP, 1])
        xn = m.sb("xn", [TP, 2, DIM])
        xT = m.sb("xT", [P, 2, KC, TP])
        row = m.sb("row", [TP, 2, TK_W])
        gate = m.sb("gate", [TP, 2, DIM])
        sq = m.sb("sq", [TP, 2 * DIM])
        ss = m.sb("ss", [TP, 2 * H])
        rn = m.sb("rn", [TP, 2 * H])
        z = m.sb("z", [TP, ZW])
        ez = m.sb("ez", [TP, ZW])
        top = m.sb("top", [TP, 1])
        za = m.sb("za", [TP, H])
        zn = m.sb("zn", [TP, H])
        s1 = m.sb("s1", [TP, H])
        s2 = m.sb("s2", [TP, H])
        s3 = m.sb("s3", [TP, H])
        poly = m.sb("poly", [TP, 9, H])
        b1 = m.sb("b1", [TP, H])
        psum_ = m.sb("psum", [TP, 1])
        pr = m.sb("pr", [TP, NE])
        gt = m.sb("gt", [TP, NE, NE])
        eq = m.sb("eq", [TP, NE, NE])
        rank = m.sb("rank", [TP, NE])
        two = m.sb("two", [TP, NE])
        wsum = m.sb("wsum", [TP, 1])
        p_t = m.ps("p_t")
        p_z = [m.ps(f"p_z{b}") for b in range(2)]
        p_w = [[m.ps(f"p_w{j}{b}") for b in range(2)] if j < 1 else [m.ps(f"p_w{j}")] * 2 for j in range(4)]
        weights = m.sem("weights")
        ready = m.sem("ready")
        loads = m.moves("loads", 3)
        out = m.moves("out", 2)
        x2_out = m.moves("x2_out")
        L = m.steps("ahead", "scaled y x2 stats aggr xn")
        V = m.steps("vector", "top zmax zb za zn nza b1 beta nbeta s1 s2 s3 "
                              "poly0 poly1 poly2 poly3 poly4 poly5 poly6 poly7 poly8 log pos sp g gfloor "
                              "psum prs pr gt eqr eq both rank two w1 wsum wrec w mask ss")
        VU = m.steps("vector_units", "rn_q rn_k")
        GL = m.steps("gpsimd_ahead", "res veps rstd")
        G = m.steps("gpsimd", "sq sseps rn")
        SL = m.steps("scalar_ahead", "gelu")
        ST = m.steps("scalar_turned", "xT")
        S = m.steps("scalar", "exp q k v gate")
        T = m.steps("tensor", "xT z q k v gate")
        passed_dve = m.sem("passed_dve")
        passed_pool = m.sem("passed_pool")
        passed_sp = m.sem("passed_sp")
        with nc.Block() as block:

            @block.sync
            def _(sp):
                for j, name in enumerate(("Wq", "Wk", "Wv", "Wg")):
                    sp.dma_start(w[:, j], a["L0_ffn_" + name].rearrange("(c p) n -> p c n", p=P)).then_inc(weights, 16)
                sp.dma_start(wz[:, :, 0:NE], a["L0_ffn_Wgate"].rearrange("(c p) n -> p c n", p=P)).then_inc(weights, 16)
                sp.dma_start(wz[:, :, NE:NE + H], a["L0_ffn_Wb"].rearrange("(c p) n -> p c n", p=P)).then_inc(weights, 16)
                sp.dma_start(wz[:, :, NE + H:ZW], a["L0_ffn_Wa"].rearrange("(c p) n -> p c n", p=P)).then_inc(weights, 16)
                sp.dma_start(decay[:], a["L0_ffn_A_log"].partition_broadcast(P)).then_inc(weights, 16)
                sp.dma_start(dtb[:], a["L0_ffn_dt_bias"].partition_broadcast(P)).then_inc(weights, 16)

                def load(t, b):
                    rows = bass.ds(t * TP, TP)
                    sp.wait_ge(*L.after(t - 2, "scaled"))
                    held(sp, passed_sp)
                    sp.wait_ge(*GL.after(t - 2, "res"))
                    sp.dma_start(gat[:, b], d["gat"][rows, :]).then_inc(*loads.done(b))
                    sp.dma_start(xin[:, b], a["x"][rows, :]).then_inc(*loads.done(b))
                    sp.dma_start(skip[:, b], d["skip"][rows, :]).then_inc(*loads.done(b))

                def store(t, b):
                    rows = bass.ds(t * TP, TP)
                    sp.wait_ge(*L.after(t, "x2"))
                    sp.dma_start(d["x2"][rows, :], x2[:, b]).then_inc(*x2_out.done(b))
                    sp.wait_ge(*VU.after(t, "rn_k"))
                    held(sp, passed_sp)
                    sp.wait_ge(*S.after(t, "gate"))
                    sp.dma_start(d["token"][rows, :], row[:, b]).then_inc(*out.done(b))
                    sp.dma_start(d["gate"][rows, :], gate[:, b]).then_inc(*out.done(b))

                for t in range(4):
                    load(t, t % 2)
                with sp.Fori(0, NT // 2 - 2) as i:
                    for b in range(2):
                        load(i * 2 + 4 + b, b)
                        store(i * 2 + b, b)
                for t in range(NT - 4, NT):
                    store(t, t % 2)
                for b in range(2):
                    sp.wait_ge(*out.after(NT // 2 - 1, b))
                    sp.wait_ge(*x2_out.after(NT // 2 - 1, b))

            def node_end(t, i, b, dve):
                dve.wait_ge(*loads.after(i, b))
                nc.vector.tensor_tensor(y[:], gat[:, b], keep["bn_scale"][0:TP], ALU.mult).then_inc(*L.done("scaled"))
                dve.wait_ge(*L.after(t, "scaled"))
                nc.vector.tensor_tensor(y[:], y[:], keep["bn_shift"][0:TP], ALU.add).then_inc(*L.done("y"))

            def norm(t, i, b, dve):
                dve.wait_ge(*SL.after(t, "gelu"))
                dve.wait_ge(*GL.after(t, "res"))
                dve.wait_ge(*x2_out.after(i, b, 1))
                nc.vector.tensor_tensor(x2[:, b], gl[:], res[:], ALU.add).then_inc(*L.done("x2"))
                dve.wait_ge(*L.after(t, "x2"))
                nc.vector.bn_stats(stats[:], x2[:, b]).then_inc(*L.done("stats"))
                dve.wait_ge(*L.after(t, "stats"))
                held(dve, passed_dve)
                nc.vector.bn_aggr(mv[:], stats[:]).then_inc(*L.done("aggr"))
                dve.wait_ge(*GL.after(t, "rstd"))
                dve.wait_ge(*T.after(t - 2, "xT"))
                nc.vector.tensor_scalar(xn[:, b], x2[:, b], mv[:, 0:1], rstd[:], ALU.subtract, ALU.mult).then_inc(*L.done("xn"))

            def exponents(t, b, dve):
                dve.wait_ge(*T.after(t, "z"))
                dve.wait_ge(*S.after(t - 1, "exp"))
                nc.vector.reduce_max(top[:], p_z[b][0:TP, 0:NE], AX.X).then_inc(*V.done("top"))
                dve.wait_ge(*V.after(t, "top"))
                nc.vector.tensor_scalar(z[:, 0:NE], p_z[b][0:TP, 0:NE], top[:], None, ALU.subtract).then_inc(*V.done("zmax"))
                nc.vector.tensor_scalar(z[:, NE:NE + H], p_z[b][0:TP, NE:NE + H], -1.0, None, ALU.mult).then_inc(*V.done("zb"))
                nc.vector.tensor_tensor(za[:], p_z[b][0:TP, NE + H:ZW], dtb[0:TP], ALU.add).then_inc(*V.done("za"))
                dve.wait_ge(*V.after(t, "za"))
                nc.vector.tensor_scalar(zn[:], za[:], -1.0, None, ALU.mult).then_inc(*V.done("zn"))
                dve.wait_ge(*V.after(t, "zn"))
                nc.vector.tensor_tensor(z[:, NE + H:ZW], za[:], zn[:], ALU.min).then_inc(*V.done("nza"))

            def gates_and_router(t, i, b, dve):
                dve.wait_ge(*S.after(t, "exp"))
                nc.vector.tensor_scalar(b1[:], ez[:, NE:NE + H], 1.0, None, ALU.add).then_inc(*V.done("b1"))
                dve.wait_ge(*V.after(t, "b1"))
                dve.wait_ge(*out.after(i, b, 1))
                nc.vector.reciprocal(row[:, b, TK_B:TK_NB], b1[:]).then_inc(*V.done("beta"))
                dve.wait_ge(*V.after(t, "beta"))
                nc.vector.tensor_scalar(row[:, b, TK_NB:TK_G], row[:, b, TK_B:TK_NB], -1.0, None, ALU.mult).then_inc(*V.done("nbeta"))
                nc.vector.tensor_scalar(s1[:], ez[:, NE + H:ZW], 2.0, None, ALU.add).then_inc(*V.done("s1"))
                dve.wait_ge(*V.after(t, "s1"))
                nc.vector.reciprocal(s2[:], s1[:]).then_inc(*V.done("s2"))
                dve.wait_ge(*V.after(t, "s2"))
                nc.vector.tensor_tensor(s1[:], s2[:], ez[:, NE + H:ZW], ALU.mult).then_inc(*V.done("s3"))
                dve.wait_ge(*V.after(t, "s3"))
                nc.vector.tensor_tensor(s3[:], s1[:], s1[:], ALU.mult).then_inc(*V.done("poly0"))
                dve.wait_ge(*V.after(t, "poly0"))
                nc.vector.tensor_scalar(poly[:, 0], s3[:], 2.0 / 17, None, ALU.mult).then_inc(*V.done("poly1"))
                for j in range(7):
                    dve.wait_ge(*V.after(t, f"poly{j + 1}"))
                    nc.vector.scalar_tensor_tensor(poly[:, j + 1], poly[:, j], 2.0 / (15 - 2 * j), s3[:], ALU.add, ALU.mult).then_inc(*V.done(f"poly{j + 2}"))
                dve.wait_ge(*V.after(t, "poly8"))
                nc.vector.scalar_tensor_tensor(poly[:, 8], poly[:, 7], 2.0, s1[:], ALU.add, ALU.mult).then_inc(*V.done("log"))
                nc.vector.tensor_scalar(zn[:], za[:], 0.0, None, ALU.max).then_inc(*V.done("pos"))
                dve.wait_ge(*V.after(t, "pos"))
                nc.vector.tensor_tensor(zn[:], zn[:], poly[:, 8], ALU.add).then_inc(*V.done("sp"))
                dve.wait_ge(*V.after(t, "sp"))
                nc.vector.scalar_tensor_tensor(za[:], zn[:], -1.0, decay[0:TP], ALU.mult, ALU.mult).then_inc(*V.done("g"))
                dve.wait_ge(*V.after(t, "g"))
                nc.vector.tensor_scalar(row[:, b, TK_G:TK_W], za[:], G_FLOOR, None, ALU.max).then_inc(*V.done("gfloor"))
                nc.vector.reduce_sum(psum_[:], ez[:, 0:NE], AX.X).then_inc(*V.done("psum"))
                dve.wait_ge(*V.after(t, "psum"))
                nc.vector.reciprocal(wsum[:], psum_[:]).then_inc(*V.done("prs"))
                dve.wait_ge(*V.after(t, "prs"))
                nc.vector.tensor_scalar(pr[:], ez[:, 0:NE], wsum[:], None, ALU.mult).then_inc(*V.done("pr"))
                dve.wait_ge(*V.after(t, "pr"))
                mine, other = pr[:].unsqueeze(2).to_broadcast([TP, NE, NE]), pr[:].unsqueeze(1).to_broadcast([TP, NE, NE])
                nc.vector.tensor_tensor(gt[:], other, mine, ALU.is_gt).then_inc(*V.done("gt"))
                nc.vector.tensor_tensor(eq[:], other, mine, ALU.is_equal).then_inc(*V.done("eqr"))
                dve.wait_ge(*V.after(t, "eqr"))
                nc.vector.tensor_tensor(eq[:], eq[:], tie[0:TP], ALU.mult).then_inc(*V.done("eq"))
                dve.wait_ge(*V.after(t, "eq"))
                nc.vector.tensor_tensor(gt[:], gt[:], eq[:], ALU.add).then_inc(*V.done("both"))
                dve.wait_ge(*V.after(t, "both"))
                nc.vector.tensor_reduce(rank[:], gt[:], AX.X, ALU.add).then_inc(*V.done("rank"))
                dve.wait_ge(*V.after(t, "rank"))
                nc.vector.tensor_scalar(two[:], rank[:], 1.5, None, ALU.is_lt).then_inc(*V.done("two"))
                dve.wait_ge(*V.after(t, "two"))
                nc.vector.tensor_tensor(two[:], two[:], pr[:], ALU.mult).then_inc(*V.done("w1"))
                dve.wait_ge(*V.after(t, "w1"))
                nc.vector.reduce_sum(psum_[:], two[:], AX.X).then_inc(*V.done("wsum"))
                dve.wait_ge(*V.after(t, "wsum"))
                nc.vector.reciprocal(wsum[:], psum_[:]).then_inc(*V.done("wrec"))
                dve.wait_ge(*V.after(t, "wrec"))
                nc.vector.tensor_scalar(two[:], two[:], wsum[:], None, ALU.mult).then_inc(*V.done("w"))
                dve.wait_ge(*V.after(t, "w"))
                nc.vector.tensor_copy(keep["weight"][0:TP, :, bass.ds(t, 1)], two[:].unsqueeze(2)).then_inc(*V.done("mask"))

            def square_sums(t, dve):
                dve.wait_ge(*G.after(t, "sq"))
                dve.wait_ge(*G.after(t - 1, "sseps"))
                nc.vector.tensor_reduce(ss[:], heads(sq[:], 2 * H), AX.X, ALU.add).then_inc(*V.done("ss"))

            def unit_rows(t, b, dve):
                dve.wait_ge(*G.after(t, "rn"))
                nc.vector.scalar_tensor_tensor(heads(row[:, b, 0:DIM]), heads(row[:, b, 0:DIM]), float(C) ** -0.5, over_c(rn[:, 0:H]), ALU.mult, ALU.mult).then_inc(*VU.done("rn_q"))
                nc.vector.tensor_tensor(heads(row[:, b, TK_K:TK_V]), heads(row[:, b, TK_K:TK_V]), over_c(rn[:, H:2 * H]), ALU.mult).then_inc(*VU.done("rn_k"))

            @block.vector
            def _(dve):
                give_credit(dve, V, VU, L)
                dve.wait_ge(weights, 16 * 9)
                dve.wait_ge(ready, 2)
                def turn(t, i, b, i_next):
                    node_end(t + 2, i_next, b, dve)
                    gates_and_router(t, i, b, dve)
                    norm(t + 2, i_next, b, dve)
                    square_sums(t, dve)
                    exponents(t + 1, 1 - b, dve)
                    unit_rows(t, b, dve)

                for b in range(2):
                    node_end(b, 0, b, dve)
                    norm(b, 0, b, dve)
                exponents(0, 0, dve)
                for i in turns(dve, NT // 2 - 1):
                    turn(i * 2, i, 0, i + 1)
                    turn(i * 2 + 1, i, 1, i + 1)
                for b in range(2):
                    gates_and_router(NT - 2 + b, NT // 2 - 1, b, dve)
                    square_sums(NT - 2 + b, dve)
                    if b == 0:
                        exponents(NT - 1, 1, dve)
                    unit_rows(NT - 2 + b, b, dve)

            def residual(t, i, b, pool):
                pool.wait_ge(*loads.after(i, b))
                pool.wait_ge(*L.after(t - 1, "x2"))
                nc.gpsimd.tensor_tensor(res[:], xin[:, b], skip[:, b], ALU.add).then_inc(*GL.done("res"))

            def deviation(t, pool):
                pool.wait_ge(*L.after(t, "aggr"))
                held(pool, passed_pool)
                nc.gpsimd.tensor_scalar(veps[:], mv[:, 1:2], LN_EPS, None, ALU.add).then_inc(*GL.done("veps"))
                pool.wait_ge(*GL.after(t, "veps"))
                pool.wait_ge(*L.after(t - 1, "xn"))
                nc.gpsimd.tensor_tensor(rstd[:], veps[:], k["minus_half"][0:TP], ALU.pow).then_inc(*GL.done("rstd"))

            def squares(t, b, pool):
                pool.wait_ge(*S.after(t, "k"))
                pool.wait_ge(*V.after(t - 1, "ss"))
                nc.gpsimd.tensor_tensor(sq[:], row[:, b, 0:TK_V], row[:, b, 0:TK_V], ALU.mult).then_inc(*G.done("sq"))

            def lengths(t, pool):
                pool.wait_ge(*V.after(t, "ss"))
                held(pool, passed_pool)
                nc.gpsimd.tensor_scalar(ss[:], ss[:], 1e-6, None, ALU.add).then_inc(*G.done("sseps"))
                pool.wait_ge(*G.after(t, "sseps"))
                pool.wait_ge(*VU.after(t - 1, "rn_k"))
                nc.gpsimd.tensor_tensor(rn[:], ss[:], k["minus_half"][0:TP].to_broadcast([TP, 2 * H]), ALU.pow).then_inc(*G.done("rn"))

            @block.gpsimd
            def _(pool):
                give_credit(pool, G, GL)
                nc.gpsimd.memset(tie[:], 1.0).then_inc(ready, 1)
                pool.wait_ge(ready, 2)
                nc.gpsimd.affine_select(out=tie[:], in_=tie[:], pattern=[[1, NE], [-1, NE]], compare_op=ALU.is_gt, fill=0.0, base=0, channel_multiplier=0).then_inc(ready, 1)
                for b in range(2):
                    residual(b, 0, b, pool)
                    deviation(b, pool)
                with pool.Fori(0, NT // 2 - 1) as i:
                    for b in range(2):
                        t = i * 2 + b
                        squares(t, b, pool)
                        residual(t + 2, i + 1, b, pool)
                        deviation(t + 2, pool)
                        lengths(t, pool)
                for b in range(2):
                    squares(NT - 2 + b, b, pool)
                    lengths(NT - 2 + b, pool)

            def gelu(t, act):
                act.wait_ge(*L.after(t, "y"))
                act.wait_ge(*L.after(t - 1, "x2"))
                nc.scalar.activation(gl[:], y[:], ACT.Gelu).then_inc(*SL.done("gelu"))

            def turned(t, b, act):
                act.wait_ge(*T.after(t, "xT"))
                act.wait_ge(*T.after(t - 2, "gate"))
                nc.scalar.copy(xT[:, b].rearrange("p c t -> p (c t)"), p_t[:, 0:KC * TP]).then_inc(*ST.done("xT"))

            def behind(t, i, b, act):
                act.wait_ge(*V.after(t, "nza"))
                act.wait_ge(*V.after(t - 1, "pr"))
                nc.scalar.activation(ez[:], z[:], ACT.Exp).then_inc(*S.done("exp"))
                act.wait_ge(*out.after(i, b, 1))
                for j, name in enumerate(("q", "k", "v", "gate")):
                    act.wait_ge(*T.after(t, name))
                    to = gate[:, b] if j == 3 else row[:, b, j * DIM:(j + 1) * DIM]
                    nc.scalar.activation(to, p_w[j][b][0:TP, :], ACT.Silu).then_inc(*S.done(name))

            @block.scalar
            def _(act):
                give_credit(act, S, SL, ST)
                act.wait_ge(weights, 16 * 9)
                nc.scalar.activation(decay[:], decay[:], ACT.Exp).then_inc(ready, 1)
                gelu(0, act)
                gelu(1, act)
                turned(0, 0, act)
                for i in turns(act, NT // 2 - 1):
                    for b in range(2):
                        t = i * 2 + b
                        turned(t + 1, 1 - b, act)
                        behind(t, i, b, act)
                        gelu(t + 2, act)
                turned(NT - 1, 1, act)
                behind(NT - 2, NT // 2 - 1, 0, act)
                behind(NT - 1, NT // 2 - 1, 1, act)

            def transposes(t, b, pe):
                pe.wait_ge(*L.after(t, "xn"))
                pe.wait_ge(*ST.after(t - 1, "xT"))
                for c in range(KC):
                    last = nc.tensor.transpose(p_t[:, c * TP:(c + 1) * TP], xn[:, b, c * P:(c + 1) * P], k["ident"][0:TP, 0:TP])
                last.then_inc(*T.done("xT"))

            @block.tensor
            def _(pe):
                give_credit(pe, T)
                pe.wait_ge(weights, 16 * 9)
                with pe.Fori(0, NT // 2) as i:
                    for b in range(2):
                        t = i * 2 + b
                        transposes(t, b, pe)
                        pe.wait_ge(*ST.after(t, "xT"))
                        pe.wait_ge(*V.after(t - 2, "za"))
                        for c in range(KC):
                            last = nc.tensor.matmul(p_z[b][0:TP, 0:ZW], xT[:, b, c], wz[:, c], start=c == 0, stop=c == KC - 1)
                        last.then_inc(*T.done("z"))
                        for j, name in enumerate(("q", "k", "v", "gate")):
                            pe.wait_ge(*S.after(t - 2 if j < 1 else t - 1, name))
                            for c in range(KC):
                                last = nc.tensor.matmul(p_w[j][b][0:TP, :], xT[:, b, c], w[:, j, c], start=c == 0, stop=c == KC - 1)
                            last.then_inc(*T.done(name))


def route(nc, k, a, d, keep):
    M = NE * NT
    with ExitStack() as ctx:
        m = Mem(nc, ctx, "route")
        mask = m.sb("mask", [P, NE, NT])
        prefix = m.sb("prefix", [P, NE, NT])
        total = m.sb("total", [P, NE, NT])
        upto = m.sb("upto", [P, NE, NT])
        pos = m.sb("pos", [P, NE, NT])
        hid = m.sb("hid", [P, NE, NT])
        tmp = m.sb("tmp", [P, NE, NT])
        sel = m.sb("sel", [P, NE, NT])
        one = m.sb("one", [P, NT])
        starts = m.sb("starts", [P, NE + 1])
        count = m.sb("count", [P, NCH])
        chunks = m.sb("chunks", [P, NE])
        slot = m.sb("slot", [P, 2, NT])
        both = m.sb("both", [P, NT])
        dumped = m.sb("dumped", [P, NT])
        isstart = m.sb("isstart", [P, NCH + 4])
        sc = m.sb("sc", [P, 2, NT], I32)
        token = m.sb("token", [P, NT], I32)
        zero = m.sb("zero", [P, NCH + 4], I32)
        col = m.sb("col", [TP, 2, 3, 1], I32)
        p_p = m.ps("p_p")
        p_t = m.ps("p_t")
        V = m.sem("vector")
        made = m.sem("made")
        counted = m.sem("counted")
        cleared = m.sem("cleared")
        G = m.steps("gpsimd", "copy0 copy1 copy2")
        moved = m.moves("moved", 2)
        ROUTED = 70
        n_steps = [0]
        passed_pool = m.sem("passed_pool")
        with nc.Block() as block:

            @block.vector
            def _(dve):
                step = [0]

                def then(ins):
                    step[0] += 1
                    ins.then_inc(V, 1)
                    dve.wait_ge(V, step[0])

                wt = keep["weight"]
                then(nc.vector.memset(one[:], 1.0))
                then(nc.vector.tensor_scalar(mask[0:TP], wt[0:TP], 0.0, None, ALU.is_gt))
                dve.wait_ge(counted, 1)
                then(nc.vector.tensor_copy(prefix[0:TP].rearrange("p e t -> p (e t)"), p_p[0:TP, 0:M]))
                then(nc.vector.tensor_copy(total[:].rearrange("p e t -> p (e t)"), p_t[:, 0:M]))
                for e in range(NE):
                    then(nc.vector.tensor_tensor_scan(upto[:, e], one[:], total[:, e], 0.0, ALU.mult, ALU.add))
                then(nc.vector.memset(starts[:], 0.0))
                for e in range(NE):
                    then(nc.vector.tensor_scalar(count[:], k["chunk_no"][:, 0:NCH], float(CH), upto[:, e, NT - 1:NT], ALU.mult, ALU.is_lt))
                    then(nc.vector.reduce_sum(chunks[:, e:e + 1], count[:], AX.X))
                    then(nc.vector.tensor_tensor(starts[:, e + 1:e + 2], starts[:, e:e + 1], chunks[:, e:e + 1], ALU.add))
                then(nc.vector.tensor_tensor(pos[:], upto[:], total[:], ALU.subtract))
                then(nc.vector.tensor_tensor(pos[0:TP], pos[0:TP], prefix[0:TP], ALU.add))
                for e in range(NE):
                    then(nc.vector.tensor_scalar(count[:, 0:1], starts[:, e:e + 1], float(CH), None, ALU.mult))
                    then(nc.vector.tensor_scalar(pos[:, e], pos[:, e], count[:, 0:1], None, ALU.add))
                for s, (far, op) in enumerate(((1.0, ALU.min), (-1.0, ALU.max))):
                    then(nc.vector.tensor_scalar(hid[0:TP], mask[0:TP], -1e6 * far, 1e6 * far, ALU.mult, ALU.add))
                    then(nc.vector.tensor_tensor(tmp[0:TP], pos[0:TP], mask[0:TP], ALU.mult))
                    then(nc.vector.tensor_tensor(tmp[0:TP], tmp[0:TP], hid[0:TP], ALU.add))
                    then(nc.vector.tensor_reduce(slot[0:TP, s], tmp[0:TP].rearrange("p e t -> p t e"), AX.X, op))
                    then(nc.vector.tensor_tensor(sel[0:TP], tmp[0:TP], slot[0:TP, s].unsqueeze(1).to_broadcast([TP, NE, NT]), ALU.is_equal))
                    then(nc.vector.tensor_tensor(sel[0:TP], sel[0:TP], wt[0:TP], ALU.mult))
                    then(nc.vector.tensor_reduce(keep["slot_weight"][0:TP, s], sel[0:TP].rearrange("p e t -> p t e"), AX.X, ALU.add))
                then(nc.vector.tensor_tensor(both[0:TP], slot[0:TP, 1], slot[0:TP, 0], ALU.is_gt))
                then(nc.vector.tensor_tensor(keep["slot_weight"][0:TP, 1], keep["slot_weight"][0:TP, 1], both[0:TP], ALU.mult))
                then(nc.vector.tensor_copy(keep["slot"][0:TP], slot[0:TP]))
                then(nc.vector.tensor_copy(sc[0:TP, 0], slot[0:TP, 0]))
                then(nc.vector.tensor_scalar(dumped[0:TP], slot[0:TP, 1], k["dumpslot"][0:TP], None, ALU.subtract))
                then(nc.vector.tensor_tensor(dumped[0:TP], dumped[0:TP], both[0:TP], ALU.mult))
                then(nc.vector.tensor_scalar(sc[0:TP, 1], dumped[0:TP], k["dumpslot"][0:TP], None, ALU.add))
                then(nc.vector.memset(keep["goes_on"][:], 1.0))
                for e in range(NE):
                    then(nc.vector.tensor_scalar(isstart[:], k["chunk_no"][:], starts[:, e:e + 1], None, ALU.not_equal))
                    then(nc.vector.tensor_tensor(keep["goes_on"][:], keep["goes_on"][:], isstart[:], ALU.mult))
                n_steps[0] = step[0]

            @block.tensor
            def _(pe):
                pe.wait_ge(V, 2)
                nc.tensor.matmul(p_p[0:TP, 0:M], k["after"][0:TP, 0:TP], mask[0:TP].rearrange("p e t -> p (e t)"), start=True, stop=True)
                nc.tensor.matmul(p_t[:, 0:M], k["ones"][0:TP, :], mask[0:TP].rearrange("p e t -> p (e t)"), start=True, stop=True).then_inc(counted, 1)

            @block.gpsimd
            def _(pool):
                give_credit(pool, G)
                nc.gpsimd.iota(token[:], [[TP, NT]], base=0, channel_multiplier=1)
                nc.gpsimd.memset(zero[:], 0).then_inc(made, 1)
                pool.wait_ge(cleared, 16)
                pool.wait_ge(V, n_steps[0])
                for i in turns(pool, NT // 2):
                    for b in range(2):
                        t = i * 2 + b
                        pool.wait_ge(*moved.after(i, b, 1))
                        nc.gpsimd.tensor_copy(col[:, b, 0], sc[0:TP, 0, bass.ds(t, 1)]).then_inc(*G.done("copy0"))
                        nc.gpsimd.tensor_copy(col[:, b, 1], sc[0:TP, 1, bass.ds(t, 1)]).then_inc(*G.done("copy1"))
                        nc.gpsimd.tensor_copy(col[:, b, 2], token[0:TP, bass.ds(t, 1)]).then_inc(*G.done("copy2"))
                        pool.wait_ge(*G.after(t, "copy2"))
                        held(pool, passed_pool)
                        for s in range(2):
                            nc.gpsimd.indirect_dma_start(out=d["table"][:, :], out_offset=bass.IndirectOffsetOnAxis(ap=col[:, b, s], axis=0), in_=col[:, b, 2], in_offset=None).then_inc(*moved.done(b))
                for b in range(2):
                    pool.wait_ge(*moved.after(NT // 2 - 1, b))

            @block.sync
            def _(sp):
                sp.wait_ge(made, 1)
                sp.dma_start(d["table"].rearrange("(p c) o -> p (c o)", p=P), zero[:]).then_inc(cleared, 16)
                sp.wait_ge(cleared, 16)


def delta_rule(nc, k, a, d, keep):
    with ExitStack() as ctx:
        m = Mem(nc, ctx, "delta")
        idx = m.sb("idx", [P, 2, 1], I32)
        x = m.sb("x", [P, 2, TK_W])
        vb = m.sb("vb", [P, 2, DIM])
        gb = m.sb("gb", [P, H, P])
        nb = m.sb("nb", [P, H, P])
        kT = m.sb("kT", [P, 2, 4, P])
        qT = m.sb("qT", [P, 2, 4, P])
        kT0 = m.sb("kT0", [P, H, P])
        ex = m.sb("ex", [P, 2, 3 * H])
        exb = m.sb("exb", [P, 2, H])
        exk = m.sb("exk", [P, 2, 2 * H])
        gsel = m.sb("gsel", [P, 2, 4])
        dec = m.sb("dec", [P, 2, H, P])
        bm = m.sb("bm", [P, 2, H, P])
        pm = m.sb("pm", [P, 2, H, P])
        first = m.sb("first", [P, H, P])
        T = m.sb("T", [P, H, P])
        U = m.sb("U", [P, 2, H, P])
        join = m.sb("join", [P, H, P])
        join32 = m.sb("join32", [P, H, TR])
        join64 = m.sb("join64", [64, H, 64])
        kd = m.sb("kd", [P, 2, DIM])
        state = m.sb("state", [P, 4, P])
        s1 = m.sb("s1", [P, 4, C])
        r1 = m.sb("r1", [P, DIM])
        r = m.sb("r", [P, DIM])
        dl = m.sb("dl", [P, DIM])
        oq = m.sb("oq", [P, DIM])
        o = m.sb("o", [P, 2, DIM])
        z_ = [m.ps(f"z{n}") for n in range(2)]
        u_ = [m.ps(f"u{n}") for n in range(2)]
        e_ = [m.ps(f"e{n}") for n in range(2)]
        c_ = m.ps("c", [P, 2, 512])
        idx_in = m.moves("idx_in")
        x_in = m.moves("x_in")
        out = m.moves("out")
        levels = range(1, 5)
        TE = m.steps("pe_early", "k q sums diff0 diff1 kk0 kk1 qk0 qk1")
        SE = m.steps("act_early", "kT qT ex dec0 dec1")
        VE = m.steps("dve_early", "exk gselA gselB exb kd a0 a1 pm0 pm1")
        GE = m.steps("pool_early", "gb0 gb1 vb nb0 nb1 bm0 bm1 first")
        TL = m.steps("pe_late", " ".join(f"z{v}0 z{v}1 u{v}0 u{v}1" for v in levels) + " z5 u5 zlast ulast")
        SL = m.steps("act_late", " ".join(f"u{v}0 u{v}1" for v in levels) + " u5 ulast")
        VL = m.steps("dve_late", "u0 " + " ".join(f"j{v}0 j{v}1 t{v}0 t{v}1" for v in levels) + " j5 t5 jlast")
        TC = m.steps("pe_chain", "kq d s o")
        SC = m.steps("act_chain", "d")
        VC = m.steps("dve_chain", "r1 oq r s1A s1B sA sB o")
        GC = m.steps("pool_chain", "decay")
        init = m.sem("init")

        def place(h):
            return h % 2 * 4 + h // 2

        def half(tile, n):
            return tile[:, 4 * n:4 * n + 4].rearrange("p h c -> p (h c)")

        def quads(ap):
            return ap.rearrange("p (h c) -> p h c", h=4)

        pairs = [(slice(s, s + TR), slice(s + TR, s + 2 * TR)) for s in range(0, P, 2 * TR)]
        passed_pool = m.sem("passed_pool")
        passed_pe = m.sem("passed_pe")
        with nc.Block() as block:

            @block.sync
            def _(sp):
                def load(i, b):
                    sp.wait_ge(*x_in.after(i, b, 1))
                    sp.dma_start(idx[:, b], d["table"][bass.ds((i * 2 + b) * CH, CH), :]).then_inc(*idx_in.done(b))

                def store(c, b):
                    sp.wait_ge(*VC.after(c, "o"))
                    sp.dma_start(d["o"][bass.ds(c * CH, CH), :], o[:, b]).then_inc(*out.done(b))

                load(0, 0)
                load(0, 1)
                load(1, 0)
                with sp.Fori(0, NCH // 2) as i:
                    load(i + 1, 1)
                    store(i * 2, 0)
                    load(i + 2, 0)
                    store(i * 2 + 1, 1)
                sp.wait_ge(*idx_in.after(NCH // 2 + 1, 0))
                sp.wait_ge(*idx_in.after(NCH // 2, 1))
                for b in range(2):
                    sp.wait_ge(*out.after(NCH // 2 - 1, b))

            @block.gpsimd
            def _(pool):
                def gather(i, b):
                    p = i * 2 + b
                    pool.wait_ge(*idx_in.after(i, b))
                    pool.wait_ge(*TE.after(p - 2, "sums"))
                    pool.wait_ge(*VE.after(p - 2, "kd"))
                    pool.wait_ge(*GE.after(p - 2, "nb1"))
                    held(pool, passed_pool)
                    nc.gpsimd.indirect_dma_start(out=x[:, b], out_offset=None, in_=d["token"][:, :], in_offset=bass.IndirectOffsetOnAxis(ap=idx[:, b], axis=0)).then_inc(*x_in.done(b))

                def decay(c, b):
                    pool.wait_ge(*SL.after(c, "ulast"))
                    nc.gpsimd.tensor_tensor(U[:, b], U[:, b], dec[:, b], ALU.mult).then_inc(*GC.done("decay"))

                def sums(i, b):
                    p = i * 2 + b
                    pool.wait_ge(*x_in.after(i, b))
                    pool.wait_ge(*TE.after(p - 1, "diff1"))
                    for n in range(2):
                        g = x[:, b, TK_G:TK_W].rearrange("p (q r) -> p r q", r=2)[:, n]
                        nc.gpsimd.tensor_tensor(gb[:, 4 * n:4 * n + 4], over_h(k["at_or_after"][:], 4), over_c(g, P), ALU.mult).then_inc(*GE.done(f"gb{n}"))

                def early(i, b):
                    p = i * 2 + b
                    pool.wait_ge(*VC.after(p - 2, "r"))
                    nc.gpsimd.tensor_tensor(heads(vb[:, b]), heads(x[:, b, TK_V:TK_B]), over_c(x[:, b, TK_B:TK_NB]), ALU.mult).then_inc(*GE.done("vb"))
                    for n in range(2):
                        pool.wait_ge(*VE.after(p - 1, f"a{n}"))
                        beta = x[:, b, TK_NB:TK_G].rearrange("p (q r) -> p r q", r=2)[:, n]
                        nc.gpsimd.tensor_tensor(nb[:, 4 * n:4 * n + 4], over_h(k["before"][:], 4), over_c(beta, P), ALU.mult).then_inc(*GE.done(f"nb{n}"))
                    for n in range(2):
                        pool.wait_ge(*VE.after(p, f"a{n}"))
                        held(pool, passed_pool)
                        part = bm[:, b, 4 * n:4 * n + 4]
                        nc.gpsimd.affine_select(out=part, in_=part, pattern=[[0, 4], [1, P]], compare_op=ALU.not_equal, fill=1.0, base=0, channel_multiplier=-1).then_inc(*GE.done(f"bm{n}"))
                    pool.wait_ge(*GE.after(p, "bm1"))
                    pool.wait_ge(*TL.after(p - 1, "u11"))
                    nc.gpsimd.tensor_tensor(first[:], bm[:, b], over_h(k["pairs"][:], H), ALU.mult).then_inc(*GE.done("first"))

                give_credit(pool, GE, GC)
                nc.gpsimd.memset(kT0[:], 0.0)
                nc.gpsimd.memset(join32[:], 0.0)
                nc.gpsimd.memset(state[:], 0.0).then_inc(init, 1)
                gather(0, 0)
                gather(0, 1)
                sums(0, 0)
                early(0, 0)
                gather(1, 0)
                sums(0, 1)
                early(0, 1)
                with pool.Fori(0, NCH // 2) as i:
                    gather(i + 1, 1)
                    sums(i + 1, 0)
                    decay(i * 2, 0)
                    early(i + 1, 0)
                    gather(i + 2, 0)
                    sums(i + 1, 1)
                    decay(i * 2 + 1, 1)
                    early(i + 1, 1)
                pool.wait_ge(*x_in.after(NCH // 2 + 1, 0))

            @block.vector
            def _(dve):
                def decays(p, b):
                    dve.wait_ge(*SE.after(p, "ex"))
                    dve.wait_ge(*TC.after(p - 2, "s"))
                    nc.vector.tensor_scalar(exk[:, b], ex[:, b, H:3 * H], keep["goes_on"][:, bass.ds(p + 1, 1)], None, ALU.mult).then_inc(*VE.done("exk"))
                    dve.wait_ge(*VE.after(p, "exk"))
                    for r0, name in ((0, "gselA"), (1, "gselB")):
                        part = slice(C * r0, C * r0 + C)
                        nc.vector.tensor_copy(gsel[part, b], exk[part, b, H:2 * H].rearrange("p (h r) -> p h r", r=2)[:, :, r0]).then_inc(*VE.done(name))
                    nc.vector.tensor_tensor(exb[:, b], ex[:, b, 0:H], x[:, b, TK_NB:TK_G], ALU.mult).then_inc(*VE.done("exb"))
                    nc.vector.tensor_tensor(heads(kd[:, b]), heads(x[:, b, TK_K:TK_V]), over_c(exk[:, b, 0:H]), ALU.mult).then_inc(*VE.done("kd"))

                def key_grams(p, b, n):
                    if n == 0:
                        dve.wait_ge(*TL.after(p - 2, "zlast"))
                    dve.wait_ge(*TE.after(p, f"kk{n}"))
                    dve.wait_ge(*GE.after(p, f"nb{n}"))
                    nc.vector.tensor_tensor(half(bm[:, b], n), e_[n][:], half(nb, n), ALU.mult).then_inc(*VE.done(f"a{n}"))

                def query_grams(p, b, n):
                    if n == 0:
                        dve.wait_ge(*TC.after(p - 2, "o"))
                    dve.wait_ge(*TE.after(p, f"qk{n}"))
                    dve.wait_ge(*SE.after(p, f"dec{n}"))
                    nc.vector.tensor_tensor(half(pm[:, b], n), e_[n][:], half(dec[:, b], n), ALU.mult).then_inc(*VE.done(f"pm{n}"))

                def first_level(p, b):
                    dve.wait_ge(*GE.after(p, "first"))
                    dve.wait_ge(*TC.after(p - 2, "d"))
                    nc.vector.transpose(U[:, b].rearrange("p h c -> p (h c)"), first[:].rearrange("p h c -> p (h c)")).then_inc(*VL.done("u0"))

                def level_join(p, v):
                    for n in range(2):
                        dve.wait_ge(*TL.after(p, f"z{v}{n}"))
                        nc.vector.tensor_tensor(join[:, 4 * n:4 * n + 4], quads(z_[n][:]), over_h(k["merge"][:, v], 4), ALU.mult).then_inc(*VL.done(f"j{v}{n}"))

                def level_transpose(p, b, v):
                    for n in range(2):
                        dve.wait_ge(*SL.after(p, f"u{v}{n}"))
                        nc.vector.transpose(half(T, n), half(U[:, b], n)).then_inc(*VL.done(f"t{v}{n}"))

                def join_blocks(p):
                    dve.wait_ge(*TL.after(p, "z5"))
                    for even, odd in pairs:
                        last = nc.vector.tensor_copy(join32[even], z_[0][even, 0:H * TR].rearrange("p (h c) -> p h c", h=H))
                    last.then_inc(*VL.done("j5"))

                def transpose_joined(p, b):
                    dve.wait_ge(*SL.after(p, "u5"))
                    nc.vector.transpose(T[TR:2 * TR, :, 0:TR], U[0:TR, b, :, TR:2 * TR]).then_inc(*VL.done("t5"))

                def last_level(p):
                    dve.wait_ge(*TL.after(p, "zlast"))
                    nc.vector.tensor_copy(join64[:].rearrange("p h c -> p (h c)"), z_[0][0:64, :]).then_inc(*VL.done("jlast"))

                def rows(c, b):
                    dve.wait_ge(*TC.after(c, "kq"))
                    nc.vector.tensor_tensor(heads(r1[:]), heads(c_[:, 0]), over_c(exb[:, b]), ALU.mult).then_inc(*VC.done("r1"))
                    nc.vector.tensor_tensor(heads(oq[:]), heads(c_[:, 1]), over_c(ex[:, b, 0:H]), ALU.mult).then_inc(*VC.done("oq"))
                    dve.wait_ge(*VC.after(c, "r1"))
                    nc.vector.tensor_tensor(r[:], r1[:], vb[:, b], ALU.add).then_inc(*VC.done("r"))
                    for r0, name in ((0, "s1A"), (1, "s1B")):
                        part = slice(C * r0, C * r0 + C)
                        nc.vector.tensor_tensor(s1[part], state[part, :, part], over_c(gsel[part, b]), ALU.mult).then_inc(*VC.done(name))

                def advance(c, i, b):
                    dve.wait_ge(*TC.after(c, "s"))
                    for r0, name in ((0, "sA"), (1, "sB")):
                        part = slice(C * r0, C * r0 + C)
                        nc.vector.tensor_tensor(state[part, :, part], s1[part], quads(c_[part, 0])[:, :, part], ALU.add).then_inc(*VC.done(name))
                    dve.wait_ge(*TC.after(c, "o"))
                    dve.wait_ge(*out.after(i, b, 1))
                    nc.vector.tensor_tensor(o[:, b], oq[:], c_[:, 1], ALU.add).then_inc(*VC.done("o"))

                def turn(i, b, c):
                    last_level(c)
                    first_level(c + 1, 1 - b)
                    rows(c, b)
                    level_join(c + 1, 1)
                    level_transpose(c + 1, 1 - b, 1)
                    level_join(c + 1, 2)
                    level_transpose(c + 1, 1 - b, 2)
                    level_join(c + 1, 3)
                    advance(c, i, b)
                    decays(c + 2, b)
                    level_transpose(c + 1, 1 - b, 3)
                    key_grams(c + 2, b, 0)
                    level_join(c + 1, 4)
                    key_grams(c + 2, b, 1)
                    level_transpose(c + 1, 1 - b, 4)
                    join_blocks(c + 1)
                    query_grams(c + 2, b, 0)
                    query_grams(c + 2, b, 1)
                    transpose_joined(c + 1, 1 - b)

                give_credit(dve, VE, VL, VC)
                dve.wait_ge(init, 1)
                for p in range(2):
                    decays(p, p)
                    for n in range(2):
                        key_grams(p, p, n)
                    for n in range(2):
                        query_grams(p, p, n)
                    if p == 0:
                        first_level(0, 0)
                        for v in levels:
                            level_join(0, v)
                            level_transpose(0, 0, v)
                        join_blocks(0)
                        transpose_joined(0, 0)
                for i in turns(dve, NCH // 2):
                    turn(i, 0, i * 2)
                    turn(i, 1, i * 2 + 1)

            @block.scalar
            def _(act):
                def key_rows(p, b):
                    act.wait_ge(*TE.after(p, "k"))
                    act.wait_ge(*TE.after(p - 1, "qk1"))
                    act.wait_ge(*TC.after(p - 2, "kq"))
                    for n in range(2):
                        part = slice(C * n, C * n + C)
                        nc.scalar.copy(half(kT0[part], n), e_[0][part])
                    nc.scalar.copy(kT[:, b].rearrange("p h c -> p (h c)"), e_[0][:]).then_inc(*SE.done("kT"))

                def query_rows(p, b):
                    act.wait_ge(*TE.after(p, "q"))
                    act.wait_ge(*TC.after(p - 2, "kq"))
                    nc.scalar.copy(qT[:, b].rearrange("p h c -> p (h c)"), e_[1][:]).then_inc(*SE.done("qT"))
                    act.wait_ge(*TE.after(p, "sums"))
                    act.wait_ge(*VC.after(p - 2, "oq"))
                    nc.scalar.activation(ex[:, b], e_[0][:, 0:3 * H], ACT.Exp).then_inc(*SE.done("ex"))

                def decays(p, b, n):
                    act.wait_ge(*TE.after(p, f"diff{n}"))
                    act.wait_ge(*GC.after(p - 2, "decay"))
                    nc.scalar.activation(half(dec[:, b], n), e_[n][:], ACT.Exp).then_inc(*SE.done(f"dec{n}"))

                def level(p, b, v):
                    for n in range(2):
                        act.wait_ge(*TL.after(p, f"u{v}{n}"))
                        act.wait_ge(*VL.after(p, "u0" if v == 1 else f"t{v - 1}{n}"))
                        nc.scalar.copy(half(U[:, b], n), u_[n][:]).then_inc(*SL.done(f"u{v}{n}"))

                def join_blocks(p, b):
                    act.wait_ge(*TL.after(p, "u5"))
                    for even, odd in pairs:
                        last = nc.scalar.copy(U[even, b, :, odd], u_[0][even, 0:H * TR].rearrange("p (h c) -> p h c", h=H))
                    last.then_inc(*SL.done("u5"))

                def last_level(p, b):
                    act.wait_ge(*TL.after(p, "ulast"))
                    nc.scalar.copy(U[0:64, b, :, 64:P], u_[0][0:64].rearrange("p (h c) -> p h c", h=H)).then_inc(*SL.done("ulast"))

                def rows(c):
                    act.wait_ge(*TC.after(c, "d"))
                    nc.scalar.copy(dl[:], c_[:, 0]).then_inc(*SC.done("d"))

                def turn(b, c):
                    last_level(c, b)
                    key_rows(c + 2, b)
                    query_rows(c + 2, b)
                    level(c + 1, 1 - b, 1)
                    rows(c)
                    decays(c + 2, b, 0)
                    level(c + 1, 1 - b, 2)
                    decays(c + 2, b, 1)
                    level(c + 1, 1 - b, 3)
                    level(c + 1, 1 - b, 4)
                    join_blocks(c + 1, 1 - b)

                give_credit(act, SE, SL, SC)
                act.wait_ge(init, 1)
                for p in range(2):
                    key_rows(p, p)
                    query_rows(p, p)
                    for n in range(2):
                        decays(p, p, n)
                    if p == 0:
                        for v in levels:
                            level(0, 0, v)
                        join_blocks(0, 0)
                with act.Fori(0, NCH // 2) as i:
                    turn(0, i * 2)
                    turn(1, i * 2 + 1)

            @block.tensor
            def _(pe):
                ident = k["ident"][:]

                def keys(p, i, b):
                    pe.wait_ge(*x_in.after(i, b))
                    pe.wait_ge(*VE.after(p - 1, "pm0"))
                    for q in range(4):
                        last = nc.tensor.transpose(e_[0][:, q * P:(q + 1) * P], x[:, b, TK_K + q * P:TK_K + (q + 1) * P], ident)
                    last.then_inc(*TE.done("k"))

                def queries(p, b):
                    pe.wait_ge(*VE.after(p - 1, "pm1"))
                    for q in range(4):
                        last = nc.tensor.transpose(e_[1][:, q * P:(q + 1) * P], x[:, b, q * P:(q + 1) * P], ident)
                    last.then_inc(*TE.done("q"))

                def sums(p, b):
                    pe.wait_ge(*SE.after(p, "kT"))
                    g = x[:, b, TK_G:TK_W]
                    nc.tensor.matmul(e_[0][:, 0:H], k["at_or_after"][:], g, start=True, stop=True)
                    nc.tensor.matmul(e_[0][:, H:2 * H], k["before"][:], g, start=True, stop=True)
                    nc.tensor.matmul(e_[0][:, 2 * H:3 * H], k["ones"][:], g, start=True, stop=True).then_inc(*TE.done("sums"))

                def differences(p, n):
                    pe.wait_ge(*GE.after(p, f"gb{n}"))
                    pe.wait_ge(*SE.after(p, ("ex", "qT")[n]))
                    nc.tensor.matmul(e_[n][:], k["before"][:], half(gb, n), start=True, stop=False)
                    nc.tensor.matmul(quads(e_[n][:]), k["identb"][:], over_h(k["hide"][:], 4), start=False, stop=True).then_inc(*TE.done(f"diff{n}"))

                def grams(p, b, right, name, n):
                    for q in range(4):
                        last = nc.tensor.matmul(e_[n][:, q * P:q * P + P], kT0[:, 4 * n + q], right[:, b, q], start=True, stop=True)
                    last.then_inc(*TE.done(f"{name}{n}"))

                def key_grams(p, b, n):
                    pe.wait_ge(*SE.after(p, f"dec{n}"))
                    grams(p, b, kT, "kk", n)

                def query_grams(p, b, n):
                    pe.wait_ge(*VE.after(p, f"a{n}"))
                    grams(p, b, qT, "qk", n)

                def product(to, left, right, n):
                    for h in range(4):
                        last = nc.tensor.matmul(to[:, h * P:(h + 1) * P], left[:, 4 * n + h], right[:, 4 * n + h], start=True, stop=True)
                    return last

                def level_z(p, b, v):
                    for n in range(2):
                        pe.wait_ge(*(VL.after(p, "u0") if v == 1 else SL.after(p, f"u{v - 1}{n}")))
                        if v == 1:
                            pe.wait_ge(*GE.after(p, "bm1"))
                        product(z_[n], bm[:, b], U[:, b], n).then_inc(*TL.done(f"z{v}{n}"))

                def level_u(p, v):
                    for n in range(2):
                        pe.wait_ge(*VL.after(p, f"j{v}{n}"))
                        if v == 1:
                            pe.wait_ge(*SL.after(p - 1, "ulast"))
                        product(u_[n], first if v == 1 else T, join, n).then_inc(*TL.done(f"u{v}{n}"))

                def join_z(p, b):
                    pe.wait_ge(*SL.after(p, "u41"))
                    for h in range(H):
                        for even, odd in pairs:
                            last = nc.tensor.matmul(z_[0][even, h * TR:(h + 1) * TR], bm[:, b, h, even], U[:, b, h, odd], start=True, stop=True)
                    last.then_inc(*TL.done("z5"))

                def join_u(p):
                    pe.wait_ge(*VL.after(p, "j5"))
                    for h in range(H):
                        for even, odd in pairs:
                            last = nc.tensor.matmul(u_[0][even, h * TR:(h + 1) * TR], T[:, h, even], join32[:, h], start=True, stop=True)
                    last.then_inc(*TL.done("u5"))

                def last_z(p, b):
                    pe.wait_ge(*SL.after(p, "u5"))
                    held(pe, passed_pe)
                    for h in range(H):
                        last = nc.tensor.matmul(z_[0][0:64, h * 64:h * 64 + 64], bm[64:P, b, h, 0:64], U[64:P, b, h, 64:P], start=True, stop=True)
                    last.then_inc(*TL.done("zlast"))

                def last_u(p):
                    pe.wait_ge(*VL.after(p, "jlast"))
                    held(pe, passed_pe)
                    for h in range(H):
                        last = nc.tensor.matmul(u_[0][0:64, h * 64:h * 64 + 64], T[0:64, h, 0:64], join64[:, h], start=True, stop=True)
                    last.then_inc(*TL.done("ulast"))

                def apply_state(c, b):
                    pe.wait_ge(*VC.after(c - 1, "o"))
                    for n, left in enumerate((kT, qT)):
                        for q in range(4):
                            last = nc.tensor.matmul(c_[:, n, q * P:(q + 1) * P], left[:, b, q], state[:, q], start=True, stop=True)
                    last.then_inc(*TC.done("kq"))

                def solve(c, b):
                    pe.wait_ge(*VC.after(c, "r"))
                    pe.wait_ge(*GC.after(c, "decay"))
                    for h in range(H):
                        last = nc.tensor.matmul(c_[:, 0, h * C:(h + 1) * C], U[:, b, place(h)], r[:, h * C:(h + 1) * C], start=True, stop=True)
                    last.then_inc(*TC.done("d"))

                def update(c, b):
                    pe.wait_ge(*SC.after(c, "d"))
                    for q in range(4):
                        two = slice(q * P, (q + 1) * P)
                        last = nc.tensor.matmul(c_[:, 0, two], kd[:, b, two], dl[:, two], start=True, stop=True)
                    last.then_inc(*TC.done("s"))
                    for h in range(H):
                        last = nc.tensor.matmul(c_[:, 1, h * C:(h + 1) * C], pm[:, b, place(h)], dl[:, h * C:(h + 1) * C], start=True, stop=True)
                    last.then_inc(*TC.done("o"))

                def turn(i, b, c):
                    apply_state(c, b)
                    last_z(c, b)
                    keys(c + 2, i + 1, b)
                    last_u(c)
                    queries(c + 2, b)
                    level_z(c + 1, 1 - b, 1)
                    sums(c + 2, b)
                    level_u(c + 1, 1)
                    solve(c, b)
                    level_z(c + 1, 1 - b, 2)
                    differences(c + 2, 0)
                    level_u(c + 1, 2)
                    differences(c + 2, 1)
                    level_z(c + 1, 1 - b, 3)
                    update(c, b)
                    level_u(c + 1, 3)
                    key_grams(c + 2, b, 0)
                    level_z(c + 1, 1 - b, 4)
                    key_grams(c + 2, b, 1)
                    level_u(c + 1, 4)
                    query_grams(c + 2, b, 0)
                    join_z(c + 1, 1 - b)
                    query_grams(c + 2, b, 1)
                    join_u(c + 1)

                give_credit(pe, TE, TL, TC)
                pe.wait_ge(init, 1)
                for p in range(2):
                    keys(p, 0, p)
                    queries(p, p)
                    sums(p, p)
                    for n in range(2):
                        differences(p, n)
                    for n in range(2):
                        key_grams(p, p, n)
                    for n in range(2):
                        query_grams(p, p, n)
                    if p == 0:
                        for v in levels:
                            level_z(0, 0, v)
                            level_u(0, v)
                        join_z(0, 0)
                        join_u(0)
                with pe.Fori(0, NCH // 2) as i:
                    turn(i, 0, i * 2)
                    turn(i, 1, i * 2 + 1)


def combine(nc, k, a, d, keep):
    with ExitStack() as ctx:
        m = Mem(nc, ctx, "out")
        w = m.sb("w", [P, KC, DIM])
        onw = m.sb("onw", [P, C])
        col = m.sb("col", [TP, 2, 2, 1], I32)
        og = m.sb("og", [TP, 2, 2, DIM])
        gate = m.sb("gate", [TP, 2, DIM])
        x2 = m.sb("x2", [TP, 2, DIM])
        g2 = m.sb("g2", [TP, 2, DIM])
        c1 = m.sb("c1", [TP, 2, DIM])
        sq = m.sb("sq", [TP, 2, DIM])
        ss = m.sb("ss", [TP, 2, H])
        rn = m.sb("rn", [TP, 2, H])
        xT = m.sb("xT", [P, 2, KC, TP])
        y = m.sb("y", [TP, 2, DIM])
        p_t = [m.ps(f"p_t{b}") for b in range(2)]
        p_y = [m.ps(f"p_y{b}") for b in range(2)]
        weights = m.sem("weights")
        gate_in = m.moves("gate_in")
        x2_in = m.moves("x2_in")
        gathers = m.moves("gathers", 2)
        out = m.moves("out")
        L = m.steps("mixed", "first core")
        LS = m.steps("summed", "ss sseps")
        V = m.steps("vector", "norm gated")
        Y = m.steps("vector_behind", "y")
        GC = m.steps("columns", "col0 col1")
        G = m.steps("gpsimd", "g2 rn")
        SQ = m.steps("scalar_ahead", "sq")
        S = m.steps("scalar", "xT")
        T = m.steps("tensor", "xT y")
        passed_pool = m.sem("passed_pool")
        with nc.Block() as block:

            @block.sync
            def _(sp):
                sp.dma_start(w[:], a["L0_ffn_Wo"].rearrange("(c p) n -> p c n", p=P)).then_inc(weights, 16)
                sp.dma_start(onw[:], a["L0_ffn_o_norm_weight"].partition_broadcast(P)).then_inc(weights, 16)
                with sp.Fori(0, NT // 2) as i:
                    for b in range(2):
                        t = i * 2 + b
                        rows = bass.ds(t * TP, TP)
                        sp.wait_ge(*G.after(t - 2, "g2"))
                        sp.dma_start(gate[:, b], d["gate"][rows, :]).then_inc(*gate_in.done(b))
                        sp.wait_ge(*Y.after(t - 2, "y"))
                        sp.dma_start(x2[:, b], d["x2"][rows, :]).then_inc(*x2_in.done(b))

            @block.gpsimd
            def _(pool):
                def gather(t, i, b):
                    pool.wait_ge(*gathers.after(i, b, 1))
                    for s in range(2):
                        nc.gpsimd.tensor_copy(col[:, b, s], keep["slot"][0:TP, s, bass.ds(t, 1)]).then_inc(*GC.done(f"col{s}"))
                    pool.wait_ge(*GC.after(t, "col1"))
                    pool.wait_ge(*L.after(t - 2, "core"))
                    held(pool, passed_pool)
                    for s in range(2):
                        nc.gpsimd.indirect_dma_start(out=og[:, b, s], out_offset=None, in_=d["o"][:, :], in_offset=bass.IndirectOffsetOnAxis(ap=col[:, b, s], axis=0)).then_inc(*gathers.done(b))

                def work(t, i, b):
                    pool.wait_ge(*gate_in.after(i, b))
                    pool.wait_ge(*V.after(t - 2, "gated"))
                    nc.gpsimd.tensor_tensor(heads(g2[:, b]), heads(gate[:, b]), over_h(onw[0:TP], H), ALU.mult).then_inc(*G.done("g2"))
                    pool.wait_ge(*LS.after(t, "sseps"))
                    pool.wait_ge(*V.after(t - 2, "norm"))
                    nc.gpsimd.tensor_tensor(rn[:, b], ss[:, b], k["minus_half"][0:TP].to_broadcast([TP, H]), ALU.pow).then_inc(*G.done("rn"))

                give_credit(pool, G, GC)
                pool.wait_ge(weights, 32)
                gather(0, 0, 0)
                gather(1, 0, 1)
                with pool.Fori(0, NT // 2 - 1) as i:
                    for b in range(2):
                        gather(i * 2 + 2 + b, i + 1, b)
                        work(i * 2 + b, i, b)
                for b in range(2):
                    work(NT - 2 + b, NT // 2 - 1, b)

            @block.vector
            def _(dve):
                def mix(t, i, b):
                    dve.wait_ge(*gathers.after(i, b))
                    dve.wait_ge(*T.after(t - 2, "xT"))
                    nc.vector.tensor_scalar(c1[:, b], og[:, b, 0], keep["slot_weight"][0:TP, 0, bass.ds(t, 1)], None, ALU.mult).then_inc(*L.done("first"))
                    dve.wait_ge(*L.after(t, "first"))
                    nc.vector.scalar_tensor_tensor(c1[:, b], og[:, b, 1], keep["slot_weight"][0:TP, 1, bass.ds(t, 1)], c1[:, b], ALU.mult, ALU.add).then_inc(*L.done("core"))

                def sums(t, b):
                    dve.wait_ge(*SQ.after(t, "sq"))
                    dve.wait_ge(*G.after(t - 2, "rn"))
                    nc.vector.tensor_reduce(ss[:, b], heads(sq[:, b]), AX.X, ALU.add).then_inc(*LS.done("ss"))
                    dve.wait_ge(*LS.after(t, "ss"))
                    nc.vector.tensor_scalar(ss[:, b], ss[:, b], 1.0 / C, LN_EPS, ALU.mult, ALU.add).then_inc(*LS.done("sseps"))

                def gated(t, b):
                    dve.wait_ge(*G.after(t, "rn"))
                    nc.vector.tensor_tensor(heads(c1[:, b]), heads(c1[:, b]), over_c(rn[:, b]), ALU.mult).then_inc(*V.done("norm"))
                    dve.wait_ge(*V.after(t, "norm"))
                    nc.vector.tensor_tensor(c1[:, b], c1[:, b], g2[:, b], ALU.mult).then_inc(*V.done("gated"))

                def residual(t, i, b):
                    dve.wait_ge(*T.after(t, "y"))
                    dve.wait_ge(*x2_in.after(i, b))
                    dve.wait_ge(*out.after(i, b, 1))
                    nc.vector.tensor_tensor(y[:, b], p_y[b][0:TP, :], x2[:, b], ALU.add).then_inc(*Y.done("y"))

                def turn(t, i, b):
                    mix(t + 2, i + 1, b)
                    gated(t + 1, 1 - b)
                    sums(t + 2, b)
                    residual(t, i, b)

                give_credit(dve, V, Y, L, LS)
                for b in range(2):
                    mix(b, 0, b)
                    sums(b, b)
                gated(0, 0)
                for i in turns(dve, NT // 2 - 1):
                    turn(i * 2, i, 0)
                    turn(i * 2 + 1, i, 1)
                gated(NT - 1, 1)
                for b in range(2):
                    residual(NT - 2 + b, NT // 2 - 1, b)

            @block.tensor
            def _(pe):
                give_credit(pe, T)
                pe.wait_ge(weights, 32)
                with pe.Fori(0, NT // 2) as i:
                    for b in range(2):
                        t = i * 2 + b
                        pe.wait_ge(*V.after(t, "gated"))
                        pe.wait_ge(*S.after(t - 2, "xT"))
                        for c in range(KC):
                            last = nc.tensor.transpose(p_t[b][:, c * TP:(c + 1) * TP], c1[:, b, c * P:(c + 1) * P], k["ident"][0:TP, 0:TP])
                        last.then_inc(*T.done("xT"))
                        pe.wait_ge(*S.after(t, "xT"))
                        pe.wait_ge(*Y.after(t - 2, "y"))
                        for c in range(KC):
                            last = nc.tensor.matmul(p_y[b][0:TP, :], xT[:, b, c], w[:, c], start=c == 0, stop=c == KC - 1)
                        last.then_inc(*T.done("y"))

            @block.scalar
            def _(act):
                def squares(t, b):
                    act.wait_ge(*L.after(t, "core"))
                    act.wait_ge(*LS.after(t - 2, "ss"))
                    nc.scalar.activation(sq[:, b], c1[:, b], ACT.Square).then_inc(*SQ.done("sq"))

                def finish(t, b):
                    act.wait_ge(*T.after(t, "xT"))
                    act.wait_ge(*T.after(t - 2, "y"))
                    nc.scalar.copy(xT[:, b].rearrange("p c t -> p (c t)"), p_t[b][:, 0:KC * TP]).then_inc(*S.done("xT"))

                def store(t, b):
                    act.wait_ge(*Y.after(t, "y"))
                    act.dma_start(a["out"][bass.ds(t * TP, TP), :], y[:, b]).then_inc(*out.done(b))

                give_credit(act, S, SQ)
                squares(0, 0)
                squares(1, 1)
                finish(0, 0)
                with act.Fori(0, NT // 2 - 1) as i:
                    for b in range(2):
                        t = i * 2 + b
                        squares(t + 2, b)
                        finish(t + 1, 1 - b)
                        store(t, b)
                finish(NT - 1, 1)
                for b in range(2):
                    store(NT - 2 + b, b)
                for b in range(2):
                    act.wait_ge(*out.after(NT // 2 - 1, b))


def build(nc, a):
    def table(name, shape, dt=F32):
        return nc.dram_tensor(name, shape, dt, kind="Internal").ap()

    d = {
        "source": table("source", (N, SRC_W)), "state": table("state", (N + P, ST_W)),
        "skip": table("skip", (N, DIM)), "gat": table("gat", (N, DIM)), "x2": table("x2", (N, DIM)),
        "token": table("token", (N, TK_W)), "gate": table("gate", (N, DIM)),
        "table": table("table", (SLOTS + 4 * CH, 1), I32), "o": table("o", (SLOTS, DIM)),
    }
    with ExitStack() as ctx:
        m = Mem(nc, ctx, "all")
        k = constants(nc, m)
        keep = {
            "bn_scale": m.sb("bn_scale", [P, DIM]), "bn_shift": m.sb("bn_shift", [P, DIM]),
            "weight": m.sb("weight", [P, NE, NT]),
            "slot": m.sb("slot", [P, 2, NT], I32), "slot_weight": m.sb("slot_weight", [P, 2, NT]),
            "goes_on": m.sb("goes_on", [P, NCH + 4]),
        }
        project_nodes(nc, k, a, d)
        send_messages(nc, k, a, d)
        batch_norm(nc, k, a, d, keep)
        project_tokens(nc, k, a, d, keep)
        route(nc, k, a, d, keep)
        delta_rule(nc, k, a, d, keep)
        combine(nc, k, a, d, keep)


INS = {
    "x": (N, DIM), "src": (N,), "dst": (N,),
    "L0_gnn_W_gat": (DIM, DIM), "L0_gnn_att_src": (H, C), "L0_gnn_att_dst": (H, C), "L0_gnn_gat_bias": (DIM,),
    "L0_gnn_bn_gamma": (DIM,), "L0_gnn_bn_beta": (DIM,), "L0_gnn_W_skip": (DIM, DIM), "L0_gnn_b_skip": (DIM,),
    "L0_ffn_Wq": (DIM, DIM), "L0_ffn_Wgate": (DIM, NE), "L0_ffn_Wk": (DIM, DIM), "L0_ffn_Wv": (DIM, DIM),
    "L0_ffn_Wb": (DIM, H), "L0_ffn_Wa": (DIM, H), "L0_ffn_A_log": (H,), "L0_ffn_dt_bias": (H,),
    "L0_ffn_Wg": (DIM, DIM), "L0_ffn_o_norm_weight": (C,), "L0_ffn_Wo": (DIM, DIM),
}


def kernel(**inputs):
    import numpy as np
    import concourse.bacc as bacc
    from concourse.bass_utils import run_bass_kernel_spmd

    nc = bacc.Bacc("TRN2", target_bir_lowering=False, num_devices=1)
    a, arrays = {}, {}
    for name, shape in INS.items():
        arrays[name] = np.ascontiguousarray(inputs[name])
        a[name] = nc.dram_tensor(name, shape, I32 if name in ("src", "dst") else F32, kind="ExternalInput").ap()
    a["out"] = nc.dram_tensor("out", (N, DIM), F32, kind="ExternalOutput").ap()
    build(nc, a)
    r = run_bass_kernel_spmd(nc, [arrays], core_ids=[0])
    return r.results[0]["out"]
```
